# Optimizing a Trainium2 kernel written in Bass

```python
import numpy as np
import jax
import jax.numpy as jnp

def _softmax(x, axis=-1):
    return jax.nn.softmax(x, axis=axis)

def _gelu(x):
    return jax.nn.gelu(x, approximate=True)

def _silu(x):
    return jax.nn.silu(x)

def _sigmoid(x):
    return jax.nn.sigmoid(x)

def _layernorm(x, axis=-1, eps=1e-05):
    m = jnp.mean(x, axis=axis, keepdims=True)
    v = jnp.var(x, axis=axis, keepdims=True)
    return (x - m) / jnp.sqrt(v + eps)

def _scatter_add(tgt, idx, src, axis=0):
    return tgt.at[idx].add(src)

def _segment_sum(src, seg, n):
    return jax.ops.segment_sum(src, seg, n)
kernel_name = 'mk_gnn_preln_d4_gnn_r32_0ab987'

def setup_inputs(seed: int=0):
    np.random.seed(seed)
    _w = jnp.asarray

    def _rec_inputs():
        import jax
        import jax.numpy as jnp
        _gk = jax.random.key(seed)
        x = -0.000202 + 1 * jax.random.normal(jax.random.fold_in(_gk, 1), (50000, 128), jnp.float32)
        src = jax.random.randint(jax.random.fold_in(_gk, 2), (25000,), 0, 50000, jnp.int32)
        dst = jax.random.randint(jax.random.fold_in(_gk, 3), (25000,), 0, 50000, jnp.int32)
        _o = jnp.argsort(dst, stable=True)
        src = src[_o]
        dst = dst[_o]
        edge_attr_16 = -0.00010739 + 0.99994 * jax.random.normal(jax.random.fold_in(_gk, 12), (25000, 16), jnp.float32)
        edge_weight1 = 0.000614103 + 0.999867 * jax.random.normal(jax.random.fold_in(_gk, 15), (25000, 1), jnp.float32)
        return (x, src, dst, edge_attr_16, edge_weight1)
    x, src, dst, edge_attr_16, edge_weight1 = _rec_inputs()

    def _L0_gnn_setup():
        import jax, jax.numpy as jnp
        import numpy as np
        N_NODES = 50000
        N_EDGES = 25000
        IN_F = 128
        OUT_F = 128
        SLOPE = 0.2
        key = jax.random.key(seed)
        k1, k2, k3, k4 = jax.random.split(key, 4)
        input = jax.random.normal(k1, (N_NODES, IN_F), dtype=jnp.float32)
        W = jax.random.normal(k2, (OUT_F, IN_F), dtype=jnp.float32) * (1.414 / np.sqrt(IN_F))
        a = jax.random.normal(k3, (2 * OUT_F, 1), dtype=jnp.float32) * (1.414 / np.sqrt(OUT_F))
        edge_index = jax.random.randint(k4, (N_EDGES, 2), 0, N_NODES, dtype=jnp.int64 if jax.config.jax_enable_x64 else jnp.int32)
        return {'input': input, 'W': W, 'a': a, 'edge_index': edge_index}
    _L0_gnn_all = _L0_gnn_setup()
    _L0_gnn_in = {k: v for k, v in _L0_gnn_all.items() if k in ('W', 'a')}
    del _L0_gnn_all

    def _L1_gnn_setup():
        import jax, jax.numpy as jnp
        import numpy as np
        BN_EPS = 0.001
        D = 128
        EDGE_DIM = 16
        N_NODES = 50000
        N_EDGES = 25000

        def _bn(x, gamma, beta, mean, var):
            return (x - mean) * jax.lax.rsqrt(var + BN_EPS) * gamma + beta
        key = jax.random.key(seed)
        ks = jax.random.split(key, 12)
        inp = {'node_feat': jax.random.normal(ks[0], (N_NODES, D), jnp.float32), 'edge_feat': jax.random.normal(ks[1], (N_EDGES, EDGE_DIM), jnp.float32), 'src': jax.random.randint(ks[2], (N_EDGES,), 0, N_NODES, jnp.int32), 'dst': jax.random.randint(ks[3], (N_EDGES,), 0, N_NODES, jnp.int32), 'We1': jax.random.normal(ks[4], (EDGE_DIM, 2 * D), jnp.float32) * 0.05, 'be1': jnp.zeros((2 * D,), jnp.float32), 'We2': jax.random.normal(ks[5], (2 * D, D), jnp.float32) * 0.05, 'be2': jnp.zeros((D,), jnp.float32), 'eps': jax.random.normal(ks[6], (1,), jnp.float32) * 0.05, 'Wm1': jax.random.normal(ks[7], (D, 2 * D), jnp.float32) * 0.05, 'bm1': jnp.zeros((2 * D,), jnp.float32), 'g1': jnp.ones((2 * D,), jnp.float32), 'b1': jnp.zeros((2 * D,), jnp.float32), 'm1': jnp.zeros((2 * D,), jnp.float32), 'v1': jnp.ones((2 * D,), jnp.float32), 'Wm2': jax.random.normal(ks[8], (2 * D, D), jnp.float32) * 0.05, 'bm2': jnp.zeros((D,), jnp.float32), 'g2': jnp.ones((D,), jnp.float32), 'b2': jnp.zeros((D,), jnp.float32), 'm2': jnp.zeros((D,), jnp.float32), 'v2': jnp.ones((D,), jnp.float32)}
        return inp
    _L1_gnn_all = _L1_gnn_setup()
    _L1_gnn_in = {k: v for k, v in _L1_gnn_all.items() if k in ('We1', 'be1', 'We2', 'be2', 'eps', 'Wm1', 'bm1', 'g1', 'b1', 'm1', 'v1', 'Wm2', 'bm2', 'g2', 'b2', 'm2', 'v2')}
    del _L1_gnn_all

    def _L2_gnn_setup():
        import jax, jax.numpy as jnp
        import numpy as np
        N_NODES = 50000
        N_EDGES = 25000
        IN_NF = 128
        OUT_NF = 128
        HID_NF = 256
        EDGE_D = 1
        key = jax.random.key(seed)
        ks = jax.random.split(key, 12)
        s = 0.02
        inp = {'h': jax.random.normal(ks[0], (N_NODES, IN_NF), dtype=jnp.float32), 'edge_index': jax.random.randint(ks[1], (2, N_EDGES), 0, N_NODES, dtype=jnp.int64), 'edge_attr': jax.random.normal(ks[2], (N_EDGES, EDGE_D), dtype=jnp.float32), 'eW1': jax.random.normal(ks[3], (2 * IN_NF + EDGE_D, HID_NF), dtype=jnp.float32) * s, 'eb1': jnp.zeros((HID_NF,), dtype=jnp.float32), 'eW2': jax.random.normal(ks[4], (HID_NF, HID_NF), dtype=jnp.float32) * s, 'eb2': jnp.zeros((HID_NF,), dtype=jnp.float32), 'nW1': jax.random.normal(ks[5], (HID_NF + IN_NF, HID_NF), dtype=jnp.float32) * s, 'nb1': jnp.zeros((HID_NF,), dtype=jnp.float32), 'nW2': jax.random.normal(ks[6], (HID_NF, OUT_NF), dtype=jnp.float32) * s, 'nb2': jnp.zeros((OUT_NF,), dtype=jnp.float32)}
        return inp
    _L2_gnn_all = _L2_gnn_setup()
    _L2_gnn_in = {k: v for k, v in _L2_gnn_all.items() if k in ('eW1', 'eb1', 'eW2', 'eb2', 'nW1', 'nb1', 'nW2', 'nb2')}
    del _L2_gnn_all

    def _L3_gnn_setup():
        import jax, jax.numpy as jnp
        import numpy as np
        N_NODES = 50000
        N_EDGES = 25000
        D_IN = 128
        D_H = 128
        D_SIG = 16
        D_OUT = 128

        def _linear_params(key, fan_in, fan_out):
            kw, kb = jax.random.split(key)
            bound = 1.0 / np.sqrt(fan_in)
            w = jax.random.uniform(kw, (fan_in, fan_out), jnp.float32, -bound, bound)
            b = jax.random.uniform(kb, (fan_out,), jnp.float32, -bound, bound)
            return (w, b)
        key = jax.random.key(seed)
        ks = jax.random.split(key, 7)
        x = jax.random.normal(ks[0], (N_NODES, D_IN), jnp.float32)
        edge_index = jax.random.randint(ks[1], (2, N_EDGES), 0, N_NODES, jnp.int64 if jax.config.jax_enable_x64 else jnp.int32)
        enc_w, enc_b = _linear_params(ks[2], D_IN, D_H)
        sig_w, sig_b = _linear_params(ks[3], D_H, D_SIG)
        msg_w, msg_b = _linear_params(ks[4], D_H, D_H)
        agg_w, agg_b = _linear_params(ks[5], 2 * D_H, D_H)
        dec_w, dec_b = _linear_params(ks[6], D_H, D_OUT)
        return {'x': x, 'edge_index': edge_index, 'enc_w': enc_w, 'enc_b': enc_b, 'sig_w': sig_w, 'sig_b': sig_b, 'msg_w': msg_w, 'msg_b': msg_b, 'agg_w': agg_w, 'agg_b': agg_b, 'dec_w': dec_w, 'dec_b': dec_b}
    _L3_gnn_all = _L3_gnn_setup()
    _L3_gnn_in = {k: v for k, v in _L3_gnn_all.items() if k in ('enc_w', 'enc_b', 'sig_w', 'sig_b', 'msg_w', 'msg_b', 'agg_w', 'agg_b', 'dec_w', 'dec_b')}
    del _L3_gnn_all
    return {'x': x, 'src': src, 'dst': dst, 'edge_attr_16': edge_attr_16, 'edge_weight1': edge_weight1, 'L0_gnn_W': _L0_gnn_in['W'], 'L0_gnn_a': _L0_gnn_in['a'], 'L1_gnn_We1': _L1_gnn_in['We1'], 'L1_gnn_be1': _L1_gnn_in['be1'], 'L1_gnn_We2': _L1_gnn_in['We2'], 'L1_gnn_be2': _L1_gnn_in['be2'], 'L1_gnn_eps': _L1_gnn_in['eps'], 'L1_gnn_Wm1': _L1_gnn_in['Wm1'], 'L1_gnn_bm1': _L1_gnn_in['bm1'], 'L1_gnn_g1': _L1_gnn_in['g1'], 'L1_gnn_b1': _L1_gnn_in['b1'], 'L1_gnn_m1': _L1_gnn_in['m1'], 'L1_gnn_v1': _L1_gnn_in['v1'], 'L1_gnn_Wm2': _L1_gnn_in['Wm2'], 'L1_gnn_bm2': _L1_gnn_in['bm2'], 'L1_gnn_g2': _L1_gnn_in['g2'], 'L1_gnn_b2': _L1_gnn_in['b2'], 'L1_gnn_m2': _L1_gnn_in['m2'], 'L1_gnn_v2': _L1_gnn_in['v2'], 'L2_gnn_eW1': _L2_gnn_in['eW1'], 'L2_gnn_eb1': _L2_gnn_in['eb1'], 'L2_gnn_eW2': _L2_gnn_in['eW2'], 'L2_gnn_eb2': _L2_gnn_in['eb2'], 'L2_gnn_nW1': _L2_gnn_in['nW1'], 'L2_gnn_nb1': _L2_gnn_in['nb1'], 'L2_gnn_nW2': _L2_gnn_in['nW2'], 'L2_gnn_nb2': _L2_gnn_in['nb2'], 'L3_gnn_enc_w': _L3_gnn_in['enc_w'], 'L3_gnn_enc_b': _L3_gnn_in['enc_b'], 'L3_gnn_sig_w': _L3_gnn_in['sig_w'], 'L3_gnn_sig_b': _L3_gnn_in['sig_b'], 'L3_gnn_msg_w': _L3_gnn_in['msg_w'], 'L3_gnn_msg_b': _L3_gnn_in['msg_b'], 'L3_gnn_agg_w': _L3_gnn_in['agg_w'], 'L3_gnn_agg_b': _L3_gnn_in['agg_b'], 'L3_gnn_dec_w': _L3_gnn_in['dec_w'], 'L3_gnn_dec_b': _L3_gnn_in['dec_b']}

def reference(x, src, dst, edge_attr_16, edge_weight1, L0_gnn_W, L0_gnn_a, L1_gnn_We1, L1_gnn_be1, L1_gnn_We2, L1_gnn_be2, L1_gnn_eps, L1_gnn_Wm1, L1_gnn_bm1, L1_gnn_g1, L1_gnn_b1, L1_gnn_m1, L1_gnn_v1, L1_gnn_Wm2, L1_gnn_bm2, L1_gnn_g2, L1_gnn_b2, L1_gnn_m2, L1_gnn_v2, L2_gnn_eW1, L2_gnn_eb1, L2_gnn_eW2, L2_gnn_eb2, L2_gnn_nW1, L2_gnn_nb1, L2_gnn_nW2, L2_gnn_nb2, L3_gnn_enc_w, L3_gnn_enc_b, L3_gnn_sig_w, L3_gnn_sig_b, L3_gnn_msg_w, L3_gnn_msg_b, L3_gnn_agg_w, L3_gnn_agg_b, L3_gnn_dec_w, L3_gnn_dec_b):
    import jax
    import jax.numpy as jnp

    def _L0_gnn_ref(input, W, a, edge_index):
        import jax, jax.numpy as jnp
        import numpy as np
        N_NODES = 50000
        N_EDGES = 25000
        IN_F = 128
        OUT_F = 128
        SLOPE = 0.2
        h = input @ W.T
        num_nodes = h.shape[0]
        src = edge_index[:, 0]
        dst = edge_index[:, 1]
        out_f = h.shape[1]
        a1 = a[:out_f, 0]
        a2 = a[out_f:, 0]
        score = (h @ a1)[src] + (h @ a2)[dst]
        alpha = jnp.exp(-jax.nn.leaky_relu(score, SLOPE))
        alpha = jnp.clip(alpha, -5.0, 5.0)
        rowsum = jax.ops.segment_sum(alpha, src, num_segments=num_nodes)
        rowsum = jnp.where(rowsum > 0, rowsum, jnp.float32(1e-08))
        msgs = alpha[:, None] * h[dst]
        h_prime = jax.ops.segment_sum(msgs, src, num_segments=num_nodes)
        h_prime = h_prime / rowsum[:, None]
        return jax.nn.elu(h_prime)

    def _L1_gnn_ref(node_feat, edge_feat, src, dst, We1, be1, We2, be2, eps, Wm1, bm1, g1, b1, m1, v1, Wm2, bm2, g2, b2, m2, v2):
        import jax, jax.numpy as jnp
        import numpy as np
        BN_EPS = 0.001
        D = 128
        EDGE_DIM = 16
        N_NODES = 50000
        N_EDGES = 25000

        def _bn(x, gamma, beta, mean, var):
            return (x - mean) * jax.lax.rsqrt(var + BN_EPS) * gamma + beta
        e = (edge_feat @ We1 + be1) @ We2 + be2
        msg = jax.nn.relu(e + node_feat[src])
        pooled = jax.ops.segment_sum(msg, dst, num_segments=node_feat.shape[0])
        h = (1.0 + eps) * node_feat + pooled
        h = jax.nn.relu(_bn(h @ Wm1 + bm1, g1, b1, m1, v1)) @ Wm2 + bm2
        return _bn(h, g2, b2, m2, v2)

    def _L2_gnn_ref(h, edge_index, edge_attr, eW1, eb1, eW2, eb2, nW1, nb1, nW2, nb2):
        import jax, jax.numpy as jnp
        import numpy as np
        N_NODES = 50000
        N_EDGES = 25000
        IN_NF = 128
        OUT_NF = 128
        HID_NF = 256
        EDGE_D = 1
        row, col = (edge_index[0], edge_index[1])
        e_in = jnp.concatenate([h[row], h[col], edge_attr], axis=1)
        m = jax.nn.silu(e_in @ eW1 + eb1)
        m = jax.nn.silu(m @ eW2 + eb2)
        agg = jax.ops.segment_sum(m, row, num_segments=h.shape[0])
        n_in = jnp.concatenate([h, agg], axis=1)
        out = jax.nn.silu(n_in @ nW1 + nb1) @ nW2 + nb2
        return out

    def _L3_gnn_ref(x, edge_index, enc_w, enc_b, sig_w, sig_b, msg_w, msg_b, agg_w, agg_b, dec_w, dec_b):
        import jax, jax.numpy as jnp
        import numpy as np
        N_NODES = 50000
        N_EDGES = 25000
        D_IN = 128
        D_H = 128
        D_SIG = 16
        D_OUT = 128

        def _linear_params(key, fan_in, fan_out):
            kw, kb = jax.random.split(key)
            bound = 1.0 / np.sqrt(fan_in)
            w = jax.random.uniform(kw, (fan_in, fan_out), jnp.float32, -bound, bound)
            b = jax.random.uniform(kb, (fan_out,), jnp.float32, -bound, bound)
            return (w, b)
        n = x.shape[0]
        h = x @ enc_w + enc_b
        sig = h @ sig_w + sig_b
        sig = sig / jnp.maximum(jnp.linalg.norm(sig, axis=-1, keepdims=True), 1e-12)
        msg = jax.nn.relu(h @ msg_w + msg_b)
        src, dst = (edge_index[0], edge_index[1])
        scores = jnp.sum(sig[src] * sig[dst], axis=-1)
        smax = jax.ops.segment_max(scores, src, num_segments=n)
        smax = jnp.where(jnp.isfinite(smax), smax, 0.0)
        e = jnp.exp(scores - smax[src])
        denom = jax.ops.segment_sum(e, src, num_segments=n)
        w = e / denom[src]
        comm = jax.ops.segment_sum(w[:, None] * msg[dst], src, num_segments=n)
        combined = jax.nn.relu(jnp.concatenate([h, comm], axis=-1) @ agg_w + agg_b)
        return combined @ dec_w + dec_b
    edge_index = jnp.stack([src, dst])
    edge_index_t = jnp.stack([src, dst], axis=1)
    h = jnp.maximum(_layernorm(x, axis=-1), 0.0)
    x = x + _L0_gnn_ref(h, L0_gnn_W, L0_gnn_a, edge_index_t)
    h = jnp.maximum(_layernorm(x, axis=-1), 0.0)
    x = x + _L1_gnn_ref(h, edge_attr_16, src, dst, L1_gnn_We1, L1_gnn_be1, L1_gnn_We2, L1_gnn_be2, L1_gnn_eps, L1_gnn_Wm1, L1_gnn_bm1, L1_gnn_g1, L1_gnn_b1, L1_gnn_m1, L1_gnn_v1, L1_gnn_Wm2, L1_gnn_bm2, L1_gnn_g2, L1_gnn_b2, L1_gnn_m2, L1_gnn_v2)
    h = jnp.maximum(_layernorm(x, axis=-1), 0.0)
    x = x + _L2_gnn_ref(h, edge_index, edge_weight1, L2_gnn_eW1, L2_gnn_eb1, L2_gnn_eW2, L2_gnn_eb2, L2_gnn_nW1, L2_gnn_nb1, L2_gnn_nW2, L2_gnn_nb2)
    h = jnp.maximum(_layernorm(x, axis=-1), 0.0)
    x = x + _L3_gnn_ref(h, edge_index, L3_gnn_enc_w, L3_gnn_enc_b, L3_gnn_sig_w, L3_gnn_sig_b, L3_gnn_msg_w, L3_gnn_msg_b, L3_gnn_agg_w, L3_gnn_agg_b, L3_gnn_dec_w, L3_gnn_dec_b)
    return x

_drawn_inputs = setup_inputs


def setup_inputs(seed=0):
    import zlib

    import numpy as np

    out = dict(_drawn_inputs(seed))
    spreads = {'L1_gnn_be1': (0.0, 0.563),
     'L1_gnn_be2': (0.0, 0.398),
     'L1_gnn_bm1': (0.0, 0.1),
     'L1_gnn_g1': (1.0, 0.2),
     'L1_gnn_b1': (0.0, 0.1),
     'L1_gnn_m1': (0.0, 0.1),
     'L1_gnn_v1': (1.0, 0.538),
     'L1_gnn_bm2': (0.0, 0.1),
     'L1_gnn_g2': (1.0, 0.2),
     'L1_gnn_b2': (0.0, 0.1),
     'L1_gnn_m2': (0.0, 0.1),
     'L1_gnn_v2': (1.0, 0.2),
     'L2_gnn_eb1': (0.0, 0.8),
     'L2_gnn_eb2': (0.0, 2.0),
     'L2_gnn_nb1': (0.0, 0.703),
     'L2_gnn_nb2': (0.0, 0.1)}
    factors = {'edge_weight1': 8.0,
     'L2_gnn_eW1': 8.0,
     'L2_gnn_eW2': 8.0,
     'L3_gnn_enc_b': 7.272,
     'L3_gnn_sig_w': 64.0,
     'L3_gnn_sig_b': 64.0,
     'L3_gnn_msg_w': 5.283,
     'L3_gnn_msg_b': 8.0,
     'L3_gnn_agg_b': 4.561}
    for name, (base, spread) in spreads.items():
        noise = np.random.default_rng([zlib.crc32(name.encode()), seed]).standard_normal(out[name].shape)
        drawn = base * np.exp(spread * noise) if base else spread * noise
        out[name] = jnp.asarray(drawn.astype(out[name].dtype))
    for name, factor in factors.items():
        out[name] = (out[name] * factor).astype(out[name].dtype)
    return out
```

```python
from contextlib import ExitStack

import concourse.bass as bass
from concourse import mybir

F32 = mybir.dt.float32
I32 = mybir.dt.int32
ALU = mybir.AluOpType
ACT = mybir.ActivationFunctionType
AXX = mybir.AxisListType.X

P = 128
D = 128
N = 50000
E = 25000
J = 4
GROUP = P * J
NODE_GROUPS = -(-N // GROUP)
NPAD = NODE_GROUPS * GROUP
SPARE = NPAD
ROWS = NPAD + P
LAST_P = (N - (NODE_GROUPS - 1) * GROUP) // J
EP = 125
ET = E // EP
EDGE_GROUPS = ET // J
COLS = ET + 2 * J
LN_EPS = 1e-5
MAGIC = 1597463007.0
NEWTON = 3
ZERO = 6288


class Parts:
    pass


def column(ap):
    return ap.rearrange("(k o) -> k o", o=1)


def columns(ap):
    return ap.rearrange("(c k) -> k c", k=P)


def spread(ap):
    return ap.rearrange("(o n) -> o n", o=1).partition_broadcast(P)


class Chain:

    def __init__(self, sem, steps):
        self.sem, self.steps, self.k = sem, steps, 0

    def begin(self):
        self.k = 0

    def done(self, ins):
        self.k += 1
        assert self.k <= self.steps
        ins.then_inc(self.sem, 1)

    def wait(self, eng, g):
        eng.wait_ge(self.sem, g * self.steps + self.k)

    def end(self):
        assert self.k == self.steps, (self.k, self.steps)


def in_turn(eng, groups, front, back):
    front(0, 0)
    with eng.Fori(0, groups // 2 - 1) as i:
        front(i, 1)
        back(i, 0)
        front(i + 1, 0)
        back(i, 1)
    last = groups // 2 - 1
    front(last, 1)
    back(last, 0)
    back(last, 1)


def rsqrt(dve, g, chain, v, y, t):
    chain.done(dve.tensor_scalar(y.bitcast(I32), v.bitcast(I32), 1, None, ALU.logical_shift_right))
    chain.wait(dve, g)
    chain.done(dve.tensor_scalar(y.bitcast(I32), y.bitcast(I32), -1.0, MAGIC, ALU.mult, ALU.add))
    chain.wait(dve, g)
    for _ in range(NEWTON):
        chain.done(dve.scalar_tensor_tensor(out=t, in0=y, scalar=-0.5, in1=v, op0=ALU.mult, op1=ALU.mult))
        chain.wait(dve, g)
        chain.done(dve.tensor_tensor(t, t, y, ALU.mult))
        chain.wait(dve, g)
        chain.done(dve.scalar_tensor_tensor(out=y, in0=t, scalar=1.5, in1=y, op0=ALU.add, op1=ALU.mult))
        chain.wait(dve, g)


RSQRT_STEPS = 2 + 3 * NEWTON


def moments(dve, g, chain, tiles, stats, mv, spot):
    for k, x in enumerate(tiles):
        ins = dve.bn_stats(stats[:, k, :], x)
    chain.done(ins)
    chain.wait(dve, g)
    dve.memset(spot, 0.0)
    for k in range(len(tiles)):
        ins = dve.bn_aggr(mv[:, k, :], stats[:, k, :])
    chain.done(ins)
    chain.wait(dve, g)


NORM_STEPS = 2 + 1 + RSQRT_STEPS + 1 + 1


def normalise(dve, g, chain, tiles, w):
    n = len(tiles)
    moments(dve, g, chain, tiles, w.stats, w.mv, w.spot)
    chain.done(dve.tensor_scalar(w.var[:, 0:n], w.mv[:, 0:n, 1], LN_EPS, None, ALU.add))
    chain.wait(dve, g)
    rsqrt(dve, g, chain, w.var[:, 0:n], w.rstd[:, 0:n], w.tmp[:, 0:n])
    chain.done(dve.scalar_tensor_tensor(out=w.shift[:, 0:n], in0=w.mv[:, 0:n, 0], scalar=-1.0,
                                        in1=w.rstd[:, 0:n], op0=ALU.mult, op1=ALU.mult))
    chain.wait(dve, g)
    for k, x in enumerate(tiles):
        ins = dve.tensor_scalar(x, x, w.rstd[:, k:k + 1], w.shift[:, k:k + 1], ALU.mult, ALU.add)
    chain.done(ins)
    chain.wait(dve, g)


def norm_space(sb, n):
    q = Parts()
    q.stats = sb("stats", [P, n, 6])
    q.mv = sb("mv", [P, n, 2])
    q.var = sb("var", [P, n])
    q.rstd = sb("rstd", [P, n])
    q.tmp = sb("tmp", [P, n])
    q.shift = sb("shift", [P, n])
    q.spot = sb("spot", [P, 1])[0:1, 0:1]
    return q


def build(nc, a, out):
    with ExitStack() as whole:
        def keep(name, shape, dt=F32):
            return whole.enter_context(nc.sbuf_tensor(name, shape, dt))

        def table(name, rows, width):
            return nc.dram_tensor(name, (rows, width), F32, kind="Internal").ap()

        g = Parts()
        g.T = [table(f"sums{k}", ROWS, w) for k, w in enumerate((D + 1, D, 2 * D, D + 1))]
        g.X = [a["x"], None, table("x2", NPAD, D), table("x3", NPAD, D)]
        g.ident = keep("ident", [P, P])
        g.before = keep("before", [P, P])
        g.src = keep("src_key", [P, COLS])
        g.dst = keep("dst_key", [P, COLS])
        g.src_row = keep("src_row", [P, COLS])
        g.spare = keep("spare", [P, 1])
        g.ew = keep("ew", [P, COLS])
        g.ef = keep("ef", [P, COLS * 16])
        g.zeros = keep("zeros", [P, ZERO])
        g.Wv = keep("Wv", [P, D + 1])
        g.v1 = keep("v1", [P, D])
        g.WE = keep("WE", [17, D])
        g.Wm1 = keep("Wm1", [P, 2 * D])
        g.s1 = keep("s1", [P, 2])
        g.c1 = keep("c1", [P, 2])
        g.Wm2 = keep("Wm2", [P, 2, D])
        g.c2 = keep("c2", [P, J, D])
        g.eps1 = keep("eps1", [P, 1])
        g.eW1s = keep("eW1s", [P, 2 * D])
        g.eW1d = keep("eW1d", [P, 2 * D])
        g.eW1w = keep("eW1w", [P, 2])
        g.eb1 = keep("eb1", [P, 2])
        g.eb2 = keep("eb2", [P, 2])
        g.eW2 = keep("eW2", [P, 2, 2 * D])
        g.nW1a = keep("nW1a", [P, 2 * D])
        g.nW1b = keep("nW1b", [P, 2, 2 * D])
        g.nb1 = keep("nb1", [P, 2])
        g.nW2 = keep("nW2", [P, 2, D])
        g.nb2 = keep("nb2", [P, J, D])
        g.Wsig = keep("Wsig", [P, 16])
        g.bsig = keep("bsig", [P, 8, 16])
        g.Wmsg = keep("Wmsg", [P, D])
        g.bmsg = keep("bmsg", [P, 1])
        g.Wtop = keep("Wtop", [P, D])
        g.btop = keep("btop", [P, 1])
        g.Wbot = keep("Wbot", [P, D])
        g.dec = keep("dec", [P, D])
        g.decb = keep("decb", [P, J, D])
        g.zeroed = [whole.enter_context(nc.semaphore(f"zeroed{k}")) for k in range(4)]
        prepare(nc, a, g)
        edges0(nc, g)
        edges1(nc, g)
        nodes(nc, g, 1, None)
        edges2(nc, g)
        nodes(nc, g, 2, None)
        edges3(nc, g)
        nodes(nc, g, 3, out)


def zero_chunks(t):
    v = t.rearrange("(p r) d -> p (r d)", p=P)
    n = v.shape[1]
    return [(v[:, k:min(k + ZERO, n)], min(ZERO, n - k)) for k in range(0, n, ZERO)]


def prepare(nc, a, g):
    with ExitStack() as ctx:
        sb, sem, ps = makers(nc, ctx, "prepare")
        raw = [sb("raw_src", [P, COLS], I32), sb("raw_dst", [P, COLS], I32)]
        part = sb("part", [P, 1], I32)
        has_edge = sb("has_edge", [P, 1])
        idle_row = sb("idle_row", [P, 1])
        one_row = sb("one_row", [1, 17])
        ones = sb("ones", [P, P])
        half = sb("half", [P, 2 + P])
        W = sb("W", [P, P])
        a12 = sb("a12", [P, 2])
        a1s = sb("a1s", [P, P])
        We1 = sb("We1", [16, 2 * D])
        We1T = sb("We1T", [P, 2, 17])
        We2 = sb("We2", [P, 2, D])
        be1 = sb("be1", [P, 2])
        be2 = sb("be2", [1, D])
        bn1 = sb("bn1", [P, 5, 2])
        bn2 = sb("bn2", [P, 5, D])
        var = sb("var", [P, 2 + D])
        scale = sb("scale", [P, 2 + D])
        c2 = sb("c2row", [P, D])
        enc = sb("enc", [P, D])
        encT = sb("encT", [P, D])
        encb = sb("encb", [P, 1])
        encbs = sb("encbs", [P, P])
        sigw = sb("sigw", [P, 16])
        sigb = sb("sigb", [P, 16])
        msgw = sb("msgw", [P, D])
        msgb = sb("msgb", [P, 1])
        aggt = sb("aggt", [P, D])
        aggb = sb("aggb", [P, 1])
        pT, p1, p2 = (ps(n, 1)[:, 0, :] for n in ("p_turned", "p_first", "p_second"))

        cleared, loaded, consts, turned, copied = (sem(n) for n in (
            "cleared", "weights_loaded", "consts_ready", "turned", "turned_copied"))
        product, vec, root = sem("products_ready"), sem("vec_step"), sem("roots_ready")
        graph = sem("graph_loaded")

        loads = [
            (W[:, :], a["L0_gnn_W"]), (a12[:, :], columns(a["L0_gnn_a"].rearrange("n o -> (n o)"))),
            (We1[:, :], a["L1_gnn_We1"]), (We2[:, :, :], a["L1_gnn_We2"].rearrange("(c k) n -> k c n", k=P)),
            (be1[:, :], columns(a["L1_gnn_be1"])), (be2[:, :], a["L1_gnn_be2"].rearrange("(o n) -> o n", o=1)),
            (g.eps1[:, :], spread(a["L1_gnn_eps"])), (g.Wm1[:, :], a["L1_gnn_Wm1"]),
            (g.Wm2[:, :, :], a["L1_gnn_Wm2"].rearrange("(c k) n -> k c n", k=P)),
            (g.eW1s[:, :], a["L2_gnn_eW1"][0:P, :]), (g.eW1d[:, :], a["L2_gnn_eW1"][P:2 * P, :]),
            (g.eW1w[:, :], columns(a["L2_gnn_eW1"][2 * P:2 * P + 1, :].rearrange("o n -> (o n)"))),
            (g.eb1[:, :], columns(a["L2_gnn_eb1"])), (g.eb2[:, :], columns(a["L2_gnn_eb2"])),
            (g.eW2[:, :, :], a["L2_gnn_eW2"].rearrange("(c k) n -> k c n", k=P)),
            (g.nW1a[:, :], a["L2_gnn_nW1"][0:P, :]),
            (g.nW1b[:, :, :], a["L2_gnn_nW1"][P:3 * P, :].rearrange("(c k) n -> k c n", k=P)),
            (g.nb1[:, :], columns(a["L2_gnn_nb1"])),
            (g.nW2[:, :, :], a["L2_gnn_nW2"].rearrange("(c k) n -> k c n", k=P)),
            (enc[:, :], a["L3_gnn_enc_w"]), (encb[:, :], column(a["L3_gnn_enc_b"])),
            (sigw[:, :], a["L3_gnn_sig_w"]), (sigb[:, :], spread(a["L3_gnn_sig_b"])),
            (msgw[:, :], a["L3_gnn_msg_w"]), (msgb[:, :], column(a["L3_gnn_msg_b"])),
            (aggt[:, :], a["L3_gnn_agg_w"][0:P, :]), (g.Wbot[:, :], a["L3_gnn_agg_w"][P:2 * P, :]),
            (aggb[:, :], column(a["L3_gnn_agg_b"])), (g.dec[:, :], a["L3_gnn_dec_w"]),
        ]
        loads += [(bn1[:, k, :], columns(a["L1_gnn_" + n])) for k, n in enumerate(("g1", "b1", "m1", "v1", "bm1"))]
        loads += [(bn2[:, k, :], spread(a["L1_gnn_" + n])) for k, n in enumerate(("g2", "b2", "m2", "v2", "bm2"))]
        for j in range(J):
            loads += [(g.nb2[:, j, :], spread(a["L2_gnn_nb2"])), (g.decb[:, j, :], spread(a["L3_gnn_dec_b"]))]
        graph_loads = [
            (raw[0][0:EP, 0:ET], a["src"].rearrange("(p t) -> p t", t=ET)),
            (raw[1][0:EP, 0:ET], a["dst"].rearrange("(p t) -> p t", t=ET)),
            (g.ew[0:EP, 0:ET], a["edge_weight1"].rearrange("(p t) o -> p (t o)", t=ET)),
            (g.ef[0:EP, 0:ET * 16], a["edge_attr_16"].rearrange("(p t) d -> p (t d)", t=ET)),
        ]

        with nc.Block() as block:
            @block.sync
            def _(sp):
                sp.wait_ge(cleared, 4)
                for to, of in graph_loads:
                    sp.dma_start(to, of).then_inc(graph, 16)
                sp.wait_ge(consts, 6)
                for to, n in zero_chunks(g.T[0]):
                    sp.dma_start(to, g.zeros[:, 0:n]).then_inc(g.zeroed[0], 16)

            @block.scalar
            def _(act):
                with nc.allow_non_contiguous_dma(reason="short vectors, one element per partition"):
                    for to, of in loads:
                        act.dma_start(to, of).then_inc(loaded, 16)

            @block.gpsimd
            def _(pool):
                pool.memset(raw[0][:, :], 0).then_inc(cleared, 1)
                pool.memset(raw[1][:, :], 0).then_inc(cleared, 1)
                pool.memset(g.ew[:, :], 0.0).then_inc(cleared, 1)
                pool.memset(g.ef[:, :], 0.0).then_inc(cleared, 1)
                pool.memset(g.ident[:, :], 0.0).then_inc(consts, 1)
                pool.memset(g.before[:, :], 1.0).then_inc(consts, 1)
                pool.memset(half[:, :], -0.5)
                pool.iota(part[:, :], [[0, 1]], base=0, channel_multiplier=1)
                pool.wait_ge(consts, 2)
                pool.affine_select(out=g.ident[:, :], in_=g.ident[:, :], compare_op=ALU.not_equal, fill=1.0,
                                   base=0, pattern=[[-1, P]], channel_multiplier=1)
                pool.affine_select(out=g.before[:, :], in_=g.before[:, :], compare_op=ALU.is_gt, fill=0.0,
                                   base=0, pattern=[[-1, P]], channel_multiplier=1).then_inc(consts, 1)
                pool.memset(one_row[:, :], 0.0).then_inc(consts, 1)
                pool.wait_ge(consts, 4)
                pool.memset(one_row[:, 16:17], 1.0).then_inc(consts, 1)
                pool.memset(g.zeros[:, :], 0.0).then_inc(consts, 1)
                pool.wait_ge(vec, 1)
                pool.tensor_tensor(scale[:, :], var[:, :], half[:, :], ALU.pow).then_inc(root, 1)

            @block.tensor
            def _(pe):
                pe.wait_ge(consts, 6)
                pe.wait_ge(loaded, 16 * len(loads))
                pe.transpose(pT[:, 0:128], W[:, :], g.ident[:, :])
                pe.transpose(pT[:, 128:256], enc[:, :], g.ident[:, :])
                for c in range(2):
                    ins = pe.transpose(pT[:, 256 + 16 * c:272 + 16 * c], We1[:, c * P:(c + 1) * P],
                                       g.ident[0:16, 0:16])
                ins.then_inc(turned, 1)
                pe.wait_ge(copied, 1)
                pe.matmul(p1[:, 0:128], a1s[:, :], W[:, :], start=True, stop=True)
                pe.matmul(p1[:, 128:129], W[:, :], a12[:, 1:2], start=True, stop=True)
                pe.matmul(p1[0:17, 129:257], We1T[:, 0, :], We2[:, 0, :], start=True, stop=False)
                pe.matmul(p1[0:17, 129:257], We1T[:, 1, :], We2[:, 1, :], start=False, stop=False)
                pe.matmul(p1[0:17, 129:257], one_row[:, :], be2[:, :], start=False, stop=True)
                pe.matmul(p2[:, 0:128], encT[:, :], msgw[:, :], start=True, stop=True)
                pe.matmul(p2[:, 128:256], encT[:, :], aggt[:, :], start=True, stop=True)
                pe.matmul(p2[:, 256:272], encT[:, :], sigw[:, :], start=True, stop=True)
                pe.matmul(p2[:, 272:288], encbs[:, :], sigw[:, :], start=True, stop=True)
                pe.matmul(p2[:, 288:289], msgw[:, :], encb[:, :], start=True, stop=True)
                pe.matmul(p2[:, 289:290], aggt[:, :], encb[:, :], start=True, stop=True).then_inc(product, 1)

            @block.vector
            def _(dve):
                link = Chain(vec, 99)
                dve.wait_ge(loaded, 16 * len(loads))
                dve.tensor_scalar(var[:, 0:2], bn1[:, 3, :], 1e-3, None, ALU.add)
                link.done(dve.tensor_scalar(var[:, 2:2 + D], bn2[:, 3, :], 1e-3, None, ALU.add))
                dve.tensor_scalar(g.eps1[:, :], g.eps1[:, :], 1.0, None, ALU.add)
                link.done(dve.memset(ones[:, :], 1.0))
                link.wait(dve, 0)
                dve.tensor_scalar(a1s[:, :], ones[:, :], a12[:, 0:1], None, ALU.mult)
                dve.tensor_scalar(encbs[:, :], ones[:, :], encb[:, 0:1], None, ALU.mult)
                dve.wait_ge(turned, 1)
                dve.tensor_copy(g.Wv[:, 0:D], pT[:, 0:128])
                dve.tensor_copy(encT[:, :], pT[:, 128:256])
                for c in range(2):
                    dve.tensor_copy(We1T[:, c, 0:16], pT[:, 256 + 16 * c:272 + 16 * c])
                    ins = dve.tensor_copy(We1T[:, c, 16:17], be1[:, c:c + 1])
                ins.then_inc(copied, 1)
                dve.wait_ge(graph, 16 * len(graph_loads))
                dve.wait_ge(consts, 6)
                link.done(dve.tensor_copy(g.spare[:, :], part[:, :]))
                link.wait(dve, 0)
                dve.tensor_scalar(has_edge[:, :], g.spare[:, :], float(EP), None, ALU.is_lt)
                dve.tensor_scalar(idle_row[:, :], g.spare[:, :], float(EP), None, ALU.is_ge)
                link.done(dve.tensor_scalar(g.spare[:, :], g.spare[:, :], float(SPARE), None, ALU.add))
                link.wait(dve, 0)
                link.done(dve.tensor_tensor(idle_row[:, :], idle_row[:, :], g.spare[:, :], ALU.mult))
                link.wait(dve, 0)
                for key, ids in ((g.src, raw[0]), (g.dst, raw[1])):
                    dve.tensor_scalar(key[:, :], ids[:, :], has_edge[:, 0:1], idle_row[:, 0:1], ALU.mult, ALU.add)
                dve.wait_ge(root, 1)
                for col, bn, s, c in ((0, bn1, g.s1, g.c1), (2, bn2, bn2[:, 3, :], c2)):
                    w = 2 if col == 0 else D
                    s = s[:, 0:w]
                    link.done(dve.tensor_tensor(s, scale[:, col:col + w], bn[:, 0, :], ALU.mult))
                    link.done(dve.tensor_tensor(bn[:, 4, :], bn[:, 4, :], bn[:, 2, :], ALU.subtract))
                    link.wait(dve, 0)
                    link.done(dve.tensor_tensor(bn[:, 4, :], bn[:, 4, :], s, ALU.mult))
                    link.wait(dve, 0)
                    link.done(dve.tensor_tensor(c[:, 0:w], bn[:, 4, :], bn[:, 1, :], ALU.add))
                    link.wait(dve, 0)
                for c in range(2):
                    dve.tensor_tensor(g.Wm2[:, c, :], g.Wm2[:, c, :], bn2[:, 3, :], ALU.mult)
                for j in range(J):
                    dve.tensor_copy(g.c2[:, j, :], c2[:, :])
                dve.wait_ge(product, 1)
                dve.tensor_copy(g.v1[:, :], p1[:, 0:128])
                dve.tensor_copy(g.Wv[:, D:D + 1], p1[:, 128:129])
                dve.tensor_copy(g.WE[:, :], p1[0:17, 129:257])
                dve.tensor_copy(g.Wmsg[:, :], p2[:, 0:128])
                dve.tensor_copy(g.Wtop[:, :], p2[:, 128:256])
                dve.tensor_copy(g.Wsig[:, :], p2[:, 256:272])
                for k in range(8):
                    dve.tensor_tensor(g.bsig[:, k, :], p2[:, 272:288], sigb[:, :], ALU.add)
                dve.tensor_tensor(g.bmsg[:, :], p2[:, 288:289], msgb[:, :], ALU.add)
                dve.tensor_tensor(g.btop[:, :], p2[:, 289:290], aggb[:, :], ALU.add)


def makers(nc, ctx, phase):
    def sb(name, shape, dt=F32):
        return ctx.enter_context(nc.sbuf_tensor(f"{phase}_{name}", shape, dt))

    sems = []

    def sem(name):
        sems.append(nc.alloc_semaphore(f"{phase}_{name}"))
        return sems[-1]

    def clear():
        nc.clear_and_free_semaphores(sems)
        nc.all_engine_barrier()

    ctx.callback(clear)

    def ps(name, banks):
        return ctx.enter_context(nc.psum_tensor(f"{phase}_{name}", [P, banks, 512], F32))

    return sb, sem, ps


def edge_space(nc, ctx, phase, gathers, width):
    sb, sem, ps = makers(nc, ctx, phase)
    q = Parts()
    q.phase = phase
    q.sb = sb
    q.sem = sem
    q.ps = ps
    q.gathers = gathers
    q.rows = [sb(f"rows{k}", [P, 2, J, t.shape[1]]) for k, (t, _) in enumerate(gathers)]
    q.index = [sb(f"index{k}", [P, 2, J], I32) for k, _ in enumerate(gathers)]
    q.key = sb("key", [P, J])
    q.to = sb("scatter_to", [P, 2, J], I32)
    q.total = sb("total", [P, 2, J, width])
    q.equal = sb("equal", [P, J, P])
    q.staged = sem("indices_staged")
    q.gathered = [sem("gathered_even"), sem("gathered_odd")]
    q.scattered = [sem("scattered_even"), sem("scattered_odd")]
    q.key_ready = sem("key_ready")
    q.keys_across = sem("keys_across")
    q.total_ready = sem("total_ready")
    q.settled = sem("settled")
    q.to_ready = sem("scatter_rows_ready")
    q.steps = sem("vec_steps")
    return q


def pool_edges(pool, s, table, used):
    def gather(b, j):
        for (of, _), rows, index in zip(s.gathers, s.rows, s.index):
            pool.indirect_dma_start(rows[:, b, j, :], None, of[:, :],
                                    bass.IndirectOffsetOnAxis(ap=index[:, b, j:j + 1], axis=0)
                                    ).then_inc(s.gathered[b], 16)

    def settle():
        pool.sem_inc(s.settled, 1)

    def scatter(i, b, j):
        if j:
            pool.wait_ge(s.scattered[b], 16 * J * i + 16 * j)
        else:
            pool.wait_ge(s.scattered[1 - b], 16 * J * (i + b))
            pool.wait_ge(s.to_ready, 2 * i + b + 1)
            pool.wait_ge(s.total_ready, 2 * i + b + 1)
        settle()
        pool.indirect_dma_start(table[:, :], bass.IndirectOffsetOnAxis(ap=s.to[:, b, j:j + 1], axis=0),
                                s.total[:, b, j, :], None, compute_op=ALU.add).then_inc(s.scattered[b], 16)

    for b in range(2):
        pool.wait_ge(s.staged, b + 1)
        for j in range(J):
            gather(b, j)
    with pool.Fori(0, EDGE_GROUPS // 2 - 1) as i:
        for b in range(2):
            pool.wait_ge(s.staged, 2 * i + b + 3)
            for rows_read in used:
                pool.wait_ge(rows_read, 2 * i + b + 1)
            settle()
            for j in range(J):
                gather(b, j)
                scatter(i, b, j)
    last = EDGE_GROUPS // 2 - 1
    for b in range(2):
        for j in range(J):
            scatter(last, b, j)
    pool.wait_ge(s.scattered[1], 16 * J * (last + 1))


def stage(dve, s, i, b, ahead):
    for (_, keys), index in zip(s.gathers, s.index):
        ins = dve.tensor_scalar(index[:, b, :], keys[:, bass.ds((2 * i + b + ahead) * J, J)], float(N - 1), None,
                                ALU.min)
    ins.then_inc(s.staged, 1)


def stage_key(dve, s, keys, i, b):
    dve.tensor_scalar(s.key[:, :], keys[:, bass.ds((2 * i + b) * J, J)], 0.0, None,
                      ALU.add).then_inc(s.key_ready, 1)


def arrived(eng, s, i, b):
    eng.wait_ge(s.gathered[b], 16 * J * len(s.gathers) * (i + 1))


def key_rows(pe, s, g_, grp, across):
    pe.wait_ge(s.key_ready, grp + 1)
    for j in range(J):
        ins = pe.transpose(across[:, 0, j * P:(j + 1) * P], s.key[:, j:j + 1].to_broadcast([P, P]), g_.ident[:, :])
    ins.then_inc(s.keys_across, 1)


ROW_STEPS = 5


def scatter_rows(dve, s, g_, i, b, chain, across, w, keep=None):
    grp = 2 * i + b
    dve.wait_ge(s.keys_across, grp + 1)
    for j in range(J):
        ins = dve.scalar_tensor_tensor(out=w.junk[:, j, :], in0=across[:, 0, j * P:(j + 1) * P],
                                       scalar=s.key[:, j:j + 1], in1=g_.before[:, :], op0=ALU.is_equal,
                                       op1=ALU.mult, accum_out=w.rank[:, j:j + 1])
    chain.done(ins)
    chain.wait(dve, grp)
    chain.done(dve.tensor_scalar(w.first[:, :], w.rank[:, :], 0.5, None, ALU.is_lt))
    chain.wait(dve, grp)
    chain.done(dve.scalar_tensor_tensor(out=w.row[:, :], in0=s.key[:, :], scalar=g_.spare[:, 0:1],
                                        in1=w.first[:, :], op0=ALU.subtract, op1=ALU.mult))
    chain.wait(dve, grp)
    chain.done(dve.tensor_scalar(w.row[:, :], w.row[:, :], g_.spare[:, 0:1], None, ALU.add))
    chain.wait(dve, grp)
    dve.wait_ge(s.scattered[b], 16 * J * i)
    dve.tensor_copy(s.to[:, b, :], w.row[:, :]).then_inc(s.to_ready, 1)
    if keep is not None:
        ins = dve.tensor_scalar(keep[:, bass.ds(grp * J, J)], w.row[:, :], 0.0, None, ALU.add)
    else:
        ins = dve.tensor_scalar(w.first[:, :], w.row[:, :], 0.0, None, ALU.add)
    chain.done(ins)


def row_space(sb):
    q = Parts()
    q.junk = sb("junk", [P, J, P])
    q.rank = sb("rank", [P, J])
    q.first = sb("first", [P, J])
    q.row = sb("row", [P, J])
    return q


def known_rows(dve, s, g_, i, b):
    dve.wait_ge(s.scattered[b], 16 * J * i)
    dve.tensor_scalar(s.to[:, b, :], g_.src_row[:, bass.ds((2 * i + b) * J, J)], 0.0, None,
                      ALU.add).then_inc(s.to_ready, 1)


def width129(t, j):
    return t[:, j // 2, (j % 2) * (D + 1):(j % 2 + 1) * (D + 1)]


def halves(t, lo, hi):
    return t[:, :, 0:2 * (D + 1)].rearrange("p h (q c) -> p h q c", q=2)[:, :, :, lo:hi]


def zero_ahead(sp, g, k):
    for to, n in zero_chunks(g.T[k]):
        sp.dma_start(to, g.zeros[:, 0:n]).then_inc(g.zeroed[k], 16)


def all_zeroed(eng, g, k):
    eng.wait_ge(g.zeroed[k], 16 * len(zero_chunks(g.T[k])))


def edges0(nc, g):
    with ExitStack() as ctx:
        s = edge_space(nc, ctx, "edges0", [(g.X[0], g.src), (g.X[0], g.dst)], D + 1)
        sb, sem = s.sb, s.sem
        w = norm_space(sb, 2 * J)
        r = row_space(sb)
        hT = sb("hT", [P, GROUP])
        score = sb("score", [P, J])
        z = sb("z", [P, J])
        alpha = sb("alpha", [P, J])
        msg = sb("msg", [P, J, D + 1])
        scored_junk = sb("scored_junk", [P, J, P])
        turned, across, prod, tot = s.ps("p_turned", 1), s.ps("p_across", 1), s.ps("p_prod", 2), s.ps("p_tot", 2)
        ones_set, h_norm, h_turned, h_copied, projected, z_ready, exp_ready, msg_ready, sel_ready, summed, scored = (
            sem(n) for n in ("ones_set", "h_normed", "h_turned", "h_copied", "projected", "z_ready", "exp_ready",
                             "messages_ready", "selection_ready", "summed", "source_scored"))
        K = NORM_STEPS + ROW_STEPS + 2

        with nc.Block() as block:
            @block.sync
            def _(sp):
                for k in range(1, 4):
                    zero_ahead(sp, g, k)

            @block.gpsimd
            def _(pool):
                all_zeroed(pool, g, 0)
                pool_edges(pool, s, g.T[0], used=(scored, h_turned))

            @block.vector
            def _(dve):
                chain = Chain(s.steps, K)
                dve.memset(msg[:, :, D:D + 1], 1.0).then_inc(ones_set, 1)
                stage(dve, s, 0, 0, 0)
                stage(dve, s, 0, 1, 0)

                def group(i, b):
                    grp = 2 * i + b
                    chain.begin()
                    dve.wait_ge(sel_ready, grp)
                    arrived(dve, s, i, b)
                    stage(dve, s, i, b, 2)
                    stage_key(dve, s, g.src, i, b)
                    src, dst = ([t[:, b, j, :] for j in range(J)] for t in s.rows)
                    normalise(dve, grp, chain, dst + src, w)
                    for j in range(J):
                        ins = dve.scalar_tensor_tensor(out=scored_junk[:, j, :], in0=src[j], scalar=0.0, in1=g.v1[:, :],
                                                       op0=ALU.max, op1=ALU.mult, accum_out=score[:, j:j + 1])
                    ins.then_inc(scored, 1)
                    scatter_rows(dve, s, g, i, b, chain, across, r, keep=g.src_row)
                    dve.wait_ge(projected, grp + 1)
                    chain.done(dve.tensor_tensor(z[:, :].rearrange("p (h q) -> p h q", h=2),
                                                 halves(prod, D, D + 1).rearrange("p h q o -> p h (q o)"),
                                                 score[:, :].rearrange("p (h q) -> p h q", h=2), ALU.add))
                    chain.wait(dve, grp)
                    dve.scalar_tensor_tensor(out=z[:, :], in0=z[:, :], scalar=0.2, in1=z[:, :], op0=ALU.mult,
                                             op1=ALU.max).then_inc(z_ready, 1)
                    dve.wait_ge(exp_ready, grp + 1)
                    chain.done(dve.tensor_scalar(alpha[:, :], alpha[:, :], 5.0, -5.0, ALU.min, ALU.max))
                    chain.wait(dve, grp)
                    for j in range(J):
                        ins = dve.tensor_scalar(s.equal[:, j, :], across[:, 0, j * P:(j + 1) * P], s.key[:, j:j + 1],
                                                alpha[:, j:j + 1], ALU.is_equal, ALU.mult)
                    ins.then_inc(sel_ready, 1)
                    chain.end()

                for_groups(dve, EDGE_GROUPS, group)

            @block.tensor
            def _(pe):
                def group(i, b):
                    grp = 2 * i + b
                    key_rows(pe, s, g, grp, across)
                    pe.wait_ge(s.steps, grp * K + NORM_STEPS)
                    for j in range(J):
                        ins = pe.transpose(turned[:, 0, j * P:(j + 1) * P], s.rows[1][:, b, j, :], g.ident[:, :])
                    ins.then_inc(h_turned, 1)
                    pe.wait_ge(h_copied, grp + 1)
                    for j in range(J):
                        ins = pe.matmul(width129(prod, j), hT[:, j * P:(j + 1) * P], g.Wv[:, :], start=True, stop=True)
                    ins.then_inc(projected, 1)
                    pe.wait_ge(msg_ready, grp + 1)
                    pe.wait_ge(sel_ready, grp + 1)
                    for j in range(J):
                        ins = pe.matmul(width129(tot, j), s.equal[:, j, :], msg[:, j, :], start=True, stop=True)
                    ins.then_inc(summed, 1)

                for_groups(pe, EDGE_GROUPS, group)

            @block.scalar
            def _(act):
                act.preload_act_table_set("exp_and_others")
                act.wait_ge(ones_set, 1)

                def group(i, b):
                    grp = 2 * i + b
                    act.wait_ge(h_turned, grp + 1)
                    act.activation(hT[:, :], turned[:, 0, :], ACT.Relu).then_inc(h_copied, 1)
                    act.wait_ge(z_ready, grp + 1)
                    act.activation(alpha[:, :], z[:, :], ACT.Exp, scale=-1.0).then_inc(exp_ready, 1)
                    act.activation(msg[:, :, 0:D].rearrange("p (h q) c -> p h q c", h=2), halves(prod, 0, D),
                                   ACT.Copy).then_inc(msg_ready, 1)
                    act.wait_ge(summed, grp + 1)
                    act.wait_ge(s.scattered[b], 16 * J * i)
                    act.activation(s.total[:, b, :, :].rearrange("p (h q) c -> p h q c", h=2), halves(tot, 0, D + 1),
                                   ACT.Copy).then_inc(s.total_ready, 1)

                for_groups(act, EDGE_GROUPS, group)


def for_groups(eng, groups, group):
    with eng.Fori(0, groups // 2) as i:
        group(i, 0)
        group(i, 1)


ELU_STEPS = 3 + 2


def elu_back(dve, grp, chain, x, sums, w, exp_arg, exp_ready, arg_ready):
    weight = sums[:, :, D]
    chain.done(dve.tensor_scalar(w.guard[:, :], weight, 0.0, 1e-8, ALU.is_le, ALU.mult))
    chain.wait(dve, grp)
    chain.done(dve.tensor_tensor(w.guard[:, :], w.guard[:, :], weight, ALU.add))
    chain.wait(dve, grp)
    chain.done(dve.reciprocal(w.inv[:, :], w.guard[:, :]))
    chain.wait(dve, grp)
    for j in range(J):
        ins = dve.tensor_scalar(exp_arg[:, j, :], sums[:, j, 0:D], w.inv[:, j:j + 1], 0.0, ALU.mult, ALU.min)
    ins.then_inc(arg_ready, 1)
    for j in range(J):
        ins = dve.tensor_scalar(w.pos[:, j, :], sums[:, j, 0:D], w.inv[:, j:j + 1], 0.0, ALU.mult, ALU.max)
    chain.done(ins)
    chain.wait(dve, grp)
    chain.done(dve.scalar_tensor_tensor(out=x, in0=w.pos[:, :, :], scalar=-1.0, in1=x, op0=ALU.add, op1=ALU.add))
    chain.wait(dve, grp)
    dve.wait_ge(exp_ready, grp + 1)


def elu_space(sb):
    q = Parts()
    q.guard = sb("guard", [P, J])
    q.inv = sb("inv", [P, J])
    q.pos = sb("pos", [P, J, D])
    return q


def edges1(nc, g):
    with ExitStack() as ctx:
        s = edge_space(nc, ctx, "edges1", [(g.X[0], g.src), (g.T[0], g.src)], D)
        sb, sem = s.sb, s.sem
        w = norm_space(sb, J)
        r = row_space(sb)
        el = elu_space(sb)
        exp_arg = sb("exp_arg", [P, J, D])
        feat = sb("feat", [P, J * 16])
        featT = sb("featT", [17, GROUP])
        msg = sb("msg", [P, J, D])
        across, turned, mapped, tot = (s.ps(n, 1) for n in ("p_across", "p_turned", "p_mapped", "p_tot"))
        ones_set, feat_ready, f_turned, f_copied, f_mapped, arg_ready, exp_ready, added, msg_ready, sel_ready, \
            summed = (sem(n) for n in ("ones_set", "features_staged", "features_turned", "features_copied",
                                       "features_mapped", "exp_arg_ready", "exp_ready", "message_added",
                                       "messages_ready", "selection_ready", "summed"))
        K = ELU_STEPS + 1 + NORM_STEPS + ROW_STEPS

        with nc.Block() as block:
            @block.gpsimd
            def _(pool):
                all_zeroed(pool, g, 1)
                pool_edges(pool, s, g.T[1], used=(added,))

            @block.vector
            def _(dve):
                chain = Chain(s.steps, K)
                dve.memset(featT[:, :], 1.0).then_inc(ones_set, 1)
                stage(dve, s, 0, 0, 0)
                stage(dve, s, 0, 1, 0)

                def group(i, b):
                    grp = 2 * i + b
                    chain.begin()
                    dve.wait_ge(sel_ready, grp)
                    dve.tensor_scalar(feat[:, :], g.ef[:, bass.ds(grp * (J * 16), J * 16)], 0.0, None,
                                      ALU.add).then_inc(feat_ready, 1)
                    stage_key(dve, s, g.dst, i, b)
                    arrived(dve, s, i, b)
                    stage(dve, s, i, b, 2)
                    x, sums = s.rows[0][:, b, :, :], s.rows[1][:, b, :, :]
                    elu_back(dve, grp, chain, x, sums, el, exp_arg, exp_ready, arg_ready)
                    chain.done(dve.tensor_tensor(x, x, exp_arg[:, :, :], ALU.add))
                    chain.wait(dve, grp)
                    normalise(dve, grp, chain, [x[:, j, :] for j in range(J)], w)
                    dve.wait_ge(f_mapped, grp + 1)
                    dve.scalar_tensor_tensor(out=msg[:, :, :], in0=x, scalar=0.0,
                                             in1=mapped[:, 0, :].rearrange("p (j c) -> p j c", j=J),
                                             op0=ALU.max, op1=ALU.add).then_inc(added, 1)
                    scatter_rows(dve, s, g, i, b, chain, across, r)
                    for j in range(J):
                        ins = dve.tensor_scalar(s.equal[:, j, :], across[:, 0, j * P:(j + 1) * P], s.key[:, j:j + 1],
                                                None, ALU.is_equal)
                    ins.then_inc(sel_ready, 1)
                    chain.end()

                for_groups(dve, EDGE_GROUPS, group)

            @block.tensor
            def _(pe):
                def group(i, b):
                    grp = 2 * i + b
                    pe.wait_ge(feat_ready, grp + 1)
                    for j in range(J):
                        ins = pe.transpose(turned[0:16, 0, j * P:(j + 1) * P], feat[:, j * 16:(j + 1) * 16],
                                           g.ident[:, :])
                    ins.then_inc(f_turned, 1)
                    key_rows(pe, s, g, grp, across)
                    pe.wait_ge(f_copied, grp + 1)
                    for j in range(J):
                        ins = pe.matmul(mapped[:, 0, j * P:(j + 1) * P], featT[:, j * P:(j + 1) * P], g.WE[:, :],
                                        start=True, stop=True)
                    ins.then_inc(f_mapped, 1)
                    pe.wait_ge(msg_ready, grp + 1)
                    pe.wait_ge(sel_ready, grp + 1)
                    for j in range(J):
                        ins = pe.matmul(tot[:, 0, j * P:(j + 1) * P], s.equal[:, j, :], msg[:, j, :],
                                        start=True, stop=True)
                    ins.then_inc(summed, 1)

                for_groups(pe, EDGE_GROUPS, group)

            @block.scalar
            def _(act):
                act.preload_act_table_set("exp_and_others")
                act.wait_ge(ones_set, 1)

                def group(i, b):
                    grp = 2 * i + b
                    act.wait_ge(f_turned, grp + 1)
                    act.activation(featT[0:16, :], turned[0:16, 0, :], ACT.Copy).then_inc(f_copied, 1)
                    act.wait_ge(arg_ready, grp + 1)
                    act.activation(exp_arg[:, :, :], exp_arg[:, :, :], ACT.Exp).then_inc(exp_ready, 1)
                    act.wait_ge(added, grp + 1)
                    act.activation(msg[:, :, :], msg[:, :, :], ACT.Relu).then_inc(msg_ready, 1)
                    act.wait_ge(summed, grp + 1)
                    act.wait_ge(s.scattered[b], 16 * J * i)
                    act.activation(s.total[:, b, :, :], tot[:, 0, :].rearrange("p (j c) -> p j c", j=J),
                                   ACT.Copy).then_inc(s.total_ready, 1)

                for_groups(act, EDGE_GROUPS, group)


def edges2(nc, g):
    with ExitStack() as ctx:
        s = edge_space(nc, ctx, "edges2", [(g.X[2], g.src), (g.X[2], g.dst)], 2 * D)
        sb, sem = s.sb, s.sem
        w = norm_space(sb, 2 * J)
        hT = [sb("hT_src", [P, GROUP]), sb("hT_dst", [P, GROUP])]
        ewc = sb("ew_column", [P, J])
        ewr = sb("ew_rows", [P, GROUP])
        m1 = sb("m1", [P, 2, GROUP])
        m2 = sb("m2", [P, 2, GROUP])
        msg = sb("msg", [P, J, 2 * D])
        across, wide = s.ps("p_across", 1), s.ps("p_ew", 1)
        turned, mid, tail = s.ps("p_turned", 2), s.ps("p_mid", 2), s.ps("p_tail", 2)
        names = ("h_turned", "h_copied", "ew_across", "ew_copied", "first_map", "first_added", "first_silu",
                 "second_map", "second_silu", "third_map", "messages_ready", "selection_ready", "summed")
        (h_turned, h_copied, ew_across, ew_copied, map1, added1, silu1, map2, silu2, map3, msg_ready, sel_ready,
         summed) = (sem(n) for n in names)
        K = NORM_STEPS

        with nc.Block() as block:
            @block.gpsimd
            def _(pool):
                all_zeroed(pool, g, 2)
                pool_edges(pool, s, g.T[2], used=(h_turned,))

            @block.vector
            def _(dve):
                chain = Chain(s.steps, K)
                stage(dve, s, 0, 0, 0)
                stage(dve, s, 0, 1, 0)

                def group(i, b):
                    grp = 2 * i + b
                    chain.begin()
                    dve.wait_ge(sel_ready, grp)
                    arrived(dve, s, i, b)
                    stage(dve, s, i, b, 2)
                    dve.tensor_scalar(ewc[:, :], g.ew[:, bass.ds(grp * J, J)], 0.0, None, ALU.add)
                    stage_key(dve, s, g.src, i, b)
                    src, dst = ([t[:, b, j, :] for j in range(J)] for t in s.rows)
                    normalise(dve, grp, chain, src + dst, w)
                    dve.wait_ge(s.keys_across, grp + 1)
                    for j in range(J):
                        ins = dve.tensor_scalar(s.equal[:, j, :], across[:, 0, j * P:(j + 1) * P], s.key[:, j:j + 1],
                                                None, ALU.is_equal)
                    ins.then_inc(sel_ready, 1)
                    known_rows(dve, s, g, i, b)
                    dve.wait_ge(ew_copied, grp + 1)
                    for f in range(2):
                        dve.wait_ge(map1, 2 * grp + f + 1)
                        dve.scalar_tensor_tensor(out=m1[:, f, :], in0=ewr[:, :], scalar=g.eW1w[:, f:f + 1],
                                                 in1=mid[:, f, :], op0=ALU.mult, op1=ALU.add).then_inc(added1, 1)
                    dve.wait_ge(map3, grp + 1)
                    dve.tensor_copy(msg[:, :, :].rearrange("p (h q) c -> p h (q c)", h=2), tail[:, :, :]
                                    ).then_inc(msg_ready, 1)
                    chain.end()

                for_groups(dve, EDGE_GROUPS, group)

            @block.tensor
            def _(pe):
                def group(i, b):
                    grp = 2 * i + b
                    key_rows(pe, s, g, grp, across)
                    for j in range(J):
                        ins = pe.transpose(wide[:, 0, j * P:(j + 1) * P], ewc[:, j:j + 1].to_broadcast([P, P]),
                                           g.ident[:, :])
                    ins.then_inc(ew_across, 1)
                    pe.wait_ge(s.steps, grp * K + NORM_STEPS)
                    for k in range(2):
                        for j in range(J):
                            ins = pe.transpose(turned[:, k, j * P:(j + 1) * P], s.rows[k][:, b, j, :], g.ident[:, :])
                    ins.then_inc(h_turned, 1)
                    pe.wait_ge(h_copied, grp + 1)
                    for f in range(2):
                        pe.matmul(mid[:, f, :], g.eW1s[:, f * P:(f + 1) * P], hT[0][:, :], start=True, stop=False)
                        pe.matmul(mid[:, f, :], g.eW1d[:, f * P:(f + 1) * P], hT[1][:, :], start=False,
                                  stop=True).then_inc(map1, 1)
                    for f in range(2):
                        pe.wait_ge(silu1, 2 * grp + 2)
                        for k in range(2):
                            ins = pe.matmul(mid[:, f, :], g.eW2[:, k, f * P:(f + 1) * P], m1[:, k, :],
                                            start=(k == 0), stop=(k == 1))
                        ins.then_inc(map2, 1)
                    pe.wait_ge(silu2, 2 * grp + 2)
                    pe.wait_ge(s.total_ready, grp)
                    for j in range(J):
                        for k in range(2):
                            ins = pe.matmul(tail[:, j // 2, (j % 2) * 256:(j % 2 + 1) * 256],
                                            m2[:, k, j * P:(j + 1) * P], g.nW1b[:, k, :],
                                            start=(k == 0), stop=(k == 1))
                    ins.then_inc(map3, 1)
                    pe.wait_ge(msg_ready, grp + 1)
                    pe.wait_ge(sel_ready, grp + 1)
                    for j in range(J):
                        ins = pe.matmul(tail[:, j // 2, (j % 2) * 256:(j % 2 + 1) * 256], s.equal[:, j, :],
                                        msg[:, j, :], start=True, stop=True)
                    ins.then_inc(summed, 1)

                for_groups(pe, EDGE_GROUPS, group)

            @block.scalar
            def _(act):
                act.preload_act_table_set("silu_and_others")

                def group(i, b):
                    grp = 2 * i + b
                    act.wait_ge(ew_across, grp + 1)
                    act.activation(ewr[:, :], wide[:, 0, :], ACT.Copy).then_inc(ew_copied, 1)
                    act.wait_ge(h_turned, grp + 1)
                    act.activation(hT[0][:, :], turned[:, 0, :], ACT.Relu)
                    act.activation(hT[1][:, :], turned[:, 1, :], ACT.Relu).then_inc(h_copied, 1)
                    for f in range(2):
                        act.wait_ge(added1, 2 * grp + f + 1)
                        act.activation(m1[:, f, :], m1[:, f, :], ACT.Silu, bias=g.eb1[:, f:f + 1]).then_inc(silu1, 1)
                    for f in range(2):
                        act.wait_ge(map2, 2 * grp + f + 1)
                        act.activation(m2[:, f, :], mid[:, f, :], ACT.Silu, bias=g.eb2[:, f:f + 1]).then_inc(silu2, 1)
                    act.wait_ge(summed, grp + 1)
                    act.wait_ge(s.scattered[b], 16 * J * i)
                    act.activation(s.total[:, b, :, :].rearrange("p (h q) c -> p h (q c)", h=2), tail[:, :, :],
                                   ACT.Copy).then_inc(s.total_ready, 1)

                for_groups(act, EDGE_GROUPS, group)


def edges3(nc, g):
    with ExitStack() as ctx:
        s = edge_space(nc, ctx, "edges3", [(g.X[3], g.src), (g.X[3], g.dst)], D + 1)
        sb, sem = s.sb, s.sem
        w = norm_space(sb, 2 * J)
        hT = [sb("hT_src", [P, GROUP]), sb("hT_dst", [P, GROUP])]
        sig = sb("sig", [P, 2 * J, 16])
        square = sb("square", [P, 2 * J, 16])
        cross = sb("cross", [P, J, 16])
        norm2 = sb("norm2", [P, 2 * J])
        inv = sb("inv_norm", [P, 2 * J])
        tmp = sb("tmp_norm", [P, 2 * J])
        dot = sb("dot", [P, J])
        e = sb("e", [P, J])
        mT = sb("msgT", [P, GROUP])
        msg = sb("msg", [P, J, D + 1])
        across, sigs, mid = s.ps("p_across", 1), s.ps("p_sig", 1), s.ps("p_mid", 1)
        turned, tail = s.ps("p_turned", 2), s.ps("p_tail", 2)
        names = ("ones_set", "h_turned", "h_copied", "sig_ready", "msg_map", "msg_relu", "agg_map", "messages_ready",
                 "dot_ready", "exp_ready", "selection_ready", "summed")
        (ones_set, h_turned, h_copied, sig_ready, map1, relu1, map2, msg_ready, dot_ready, exp_ready, sel_ready,
         summed) = (sem(n) for n in names)
        K = NORM_STEPS + 4 + RSQRT_STEPS + 1

        with nc.Block() as block:
            @block.gpsimd
            def _(pool):
                all_zeroed(pool, g, 3)
                pool_edges(pool, s, g.T[3], used=(h_turned,))

            @block.vector
            def _(dve):
                chain = Chain(s.steps, K)
                dve.memset(msg[:, :, D:D + 1], 1.0).then_inc(ones_set, 1)
                stage(dve, s, 0, 0, 0)
                stage(dve, s, 0, 1, 0)

                def group(i, b):
                    grp = 2 * i + b
                    chain.begin()
                    dve.wait_ge(sel_ready, grp)
                    arrived(dve, s, i, b)
                    stage(dve, s, i, b, 2)
                    stage_key(dve, s, g.src, i, b)
                    src, dst = ([t[:, b, j, :] for j in range(J)] for t in s.rows)
                    normalise(dve, grp, chain, src + dst, w)
                    known_rows(dve, s, g, i, b)
                    dve.wait_ge(sig_ready, grp + 1)
                    chain.done(dve.tensor_tensor(sig[:, :, :], sigs[:, 0, 0:128].rearrange("p (k c) -> p k c", c=16),
                                                 g.bsig[:, :, :], ALU.add))
                    chain.wait(dve, grp)
                    dve.tensor_tensor(square[:, :, :], sig[:, :, :], sig[:, :, :], ALU.mult)
                    chain.done(dve.tensor_tensor(cross[:, :, :], sig[:, 0:J, :], sig[:, J:2 * J, :], ALU.mult))
                    chain.wait(dve, grp)
                    dve.tensor_reduce(norm2[:, :], square[:, :, :], AXX, ALU.add)
                    chain.done(dve.tensor_reduce(dot[:, :], cross[:, :, :], AXX, ALU.add))
                    chain.wait(dve, grp)
                    chain.done(dve.tensor_scalar(norm2[:, :], norm2[:, :], 1e-24, None, ALU.max))
                    chain.wait(dve, grp)
                    rsqrt(dve, grp, chain, norm2[:, :], inv[:, :], tmp[:, :])
                    chain.done(dve.tensor_tensor(dot[:, :], dot[:, :], inv[:, 0:J], ALU.mult))
                    chain.wait(dve, grp)
                    dve.tensor_tensor(dot[:, :], dot[:, :], inv[:, J:2 * J], ALU.mult).then_inc(dot_ready, 1)
                    dve.wait_ge(s.keys_across, grp + 1)
                    dve.wait_ge(exp_ready, grp + 1)
                    for j in range(J):
                        ins = dve.tensor_scalar(s.equal[:, j, :], across[:, 0, j * P:(j + 1) * P], s.key[:, j:j + 1],
                                                e[:, j:j + 1], ALU.is_equal, ALU.mult)
                    ins.then_inc(sel_ready, 1)
                    chain.end()

                for_groups(dve, EDGE_GROUPS, group)

            @block.tensor
            def _(pe):
                def group(i, b):
                    grp = 2 * i + b
                    key_rows(pe, s, g, grp, across)
                    pe.wait_ge(s.steps, grp * K + NORM_STEPS)
                    for k in range(2):
                        for j in range(J):
                            ins = pe.transpose(turned[:, k, j * P:(j + 1) * P], s.rows[k][:, b, j, :], g.ident[:, :])
                    ins.then_inc(h_turned, 1)
                    pe.wait_ge(h_copied, grp + 1)
                    for k in range(2):
                        for j in range(J):
                            at = (k * J + j) * 16
                            ins = pe.matmul(sigs[:, 0, at:at + 16], hT[k][:, j * P:(j + 1) * P], g.Wsig[:, :],
                                            start=True, stop=True)
                    ins.then_inc(sig_ready, 1)
                    pe.matmul(mid[:, 0, :], g.Wmsg[:, :], hT[1][:, :], start=True, stop=True).then_inc(map1, 1)
                    pe.wait_ge(relu1, grp + 1)
                    for j in range(J):
                        at = (j % 2) * (D + 1)
                        ins = pe.matmul(tail[:, j // 2, at:at + D], mT[:, j * P:(j + 1) * P], g.Wbot[:, :],
                                        start=True, stop=True)
                    ins.then_inc(map2, 1)
                    pe.wait_ge(msg_ready, grp + 1)
                    pe.wait_ge(sel_ready, grp + 1)
                    for j in range(J):
                        ins = pe.matmul(width129(tail, j), s.equal[:, j, :], msg[:, j, :], start=True, stop=True)
                    ins.then_inc(summed, 1)

                for_groups(pe, EDGE_GROUPS, group)

            @block.scalar
            def _(act):
                act.preload_act_table_set("exp_and_others")
                act.wait_ge(ones_set, 1)

                def group(i, b):
                    grp = 2 * i + b
                    act.wait_ge(h_turned, grp + 1)
                    act.activation(hT[0][:, :], turned[:, 0, :], ACT.Relu)
                    act.activation(hT[1][:, :], turned[:, 1, :], ACT.Relu).then_inc(h_copied, 1)
                    act.wait_ge(map1, grp + 1)
                    act.activation(mT[:, :], mid[:, 0, :], ACT.Relu, bias=g.bmsg[:, 0:1]).then_inc(relu1, 1)
                    act.wait_ge(map2, grp + 1)
                    act.activation(msg[:, :, 0:D].rearrange("p (h q) c -> p h q c", h=2), halves(tail, 0, D),
                                   ACT.Copy).then_inc(msg_ready, 1)
                    act.wait_ge(dot_ready, grp + 1)
                    act.activation(e[:, :], dot[:, :], ACT.Exp).then_inc(exp_ready, 1)
                    act.wait_ge(summed, grp + 1)
                    act.wait_ge(s.scattered[b], 16 * J * i)
                    act.activation(s.total[:, b, :, :].rearrange("p (h q) c -> p h q c", h=2), halves(tail, 0, D + 1),
                                   ACT.Copy).then_inc(s.total_ready, 1)

                for_groups(act, EDGE_GROUPS, group)


def nodes(nc, g, layer, out):
    with ExitStack() as ctx:
        sb, sem, ps = makers(nc, ctx, f"nodes{layer}")
        w = norm_space(sb, J)
        reads = {1: [g.X[0], g.T[0], g.T[1]], 2: [g.X[2], g.T[2]], 3: [g.X[3], g.T[3]]}[layer]
        to = {1: g.X[2], 2: g.X[3], 3: out}[layer]
        const = {1: g.c2, 2: g.nb2, 3: g.decb}[layer]
        slots = [sb(f"slots{k}", [P, 2, J, t.shape[1]]) for k, t in enumerate(reads)]
        eps = sb("eps", [P, J])
        half = sb("half", [P, J])
        base = sb("base", [P, 2, J, D])
        h = sb("h", [P, J, D])
        hT = sb("hT", [P, 2, GROUP])
        mid = sb("mid", [P, 2, GROUP])
        pre = sb("pre", [P, J, 2 * D if layer == 2 else D])
        done = sb("done", [P, 2, J, D])
        inv = sb("inv_weight", [P, J])
        if layer == 1:
            el = elu_space(sb)
            exp_arg = sb("exp_arg", [P, J, D])
        p_turned, p_map, p_mid, p_out = ps("p_turned", 1), ps("p_map", 2), ps("p_mid", 2), ps("p_out", 1)
        (consts, rstd_ready, base_ready, shift_ready, normed, h_ready, h_turned, h_copied, mapped, pre_ready,
         mid_turned, mid_ready, projected, out_ready, arg_ready, exp_ready, front_steps, back_steps) = (
            sem(n) for n in (
                "consts_set", "rstd_ready", "base_ready", "shift_ready", "normed", "h_ready", "h_turned", "h_copied",
                "mapped", "pre_ready", "mid_turned", "mid_ready", "projected", "out_ready",                 "exp_arg_ready", "exp_ready", "front_steps", "back_steps"))
        loaded = [sem("loaded_even"), sem("loaded_odd")]
        stored = [sem("stored_even"), sem("stored_odd")]
        h_made = h_ready if layer == 1 else normed
        used = h_ready if layer == 1 else pre_ready
        MOMENTS = (ELU_STEPS + 1 if layer == 1 else 0) + 2
        BACK = {1: 0, 2: 0, 3: 2}[layer]
        chunks = 1 if layer == 3 else 2
        last = NODE_GROUPS // 2 - 1

        with nc.Block() as block:
            @block.sync
            def _(sp):
                def rows(t, i, b, parts=P):
                    return t[bass.ds((2 * i + b) * GROUP, parts * J), :].rearrange("(p j) d -> p j d", j=J)

                def load(i, b, parts=P):
                    for t, slot in zip(reads, slots):
                        n = parts if t.shape[0] == N else P
                        sp.dma_start(slot[0:n, b, :, :], rows(t, i, b, n)).then_inc(loaded[b], 16)

                def turn(i, b, n_store=P, n_load=None):
                    sp.wait_ge(out_ready, 2 * i + b + 1)
                    sp.dma_start(rows(to, i, b, n_store), done[0:n_store, b, :, :]).then_inc(stored[b], 16)
                    if n_load:
                        sp.wait_ge(used, 2 * i + b + 1)
                        sp.wait_ge(base_ready, 2 * i + b + 1)
                        load(i + 1, b, n_load)

                load(0, 0)
                load(0, 1)
                with sp.Fori(0, last - 1) as i:
                    turn(i, 0, n_load=P)
                    turn(i, 1, n_load=P)
                turn(last - 1, 0, n_load=P)
                turn(last - 1, 1, n_load=LAST_P)
                turn(last, 0)
                turn(last, 1, n_store=LAST_P if layer == 3 else P)
                for b in range(2):
                    sp.wait_ge(stored[b], 16 * (last + 1))

            @block.gpsimd
            def _(pool):
                pool.memset(eps[:, :], LN_EPS)
                pool.memset(half[:, :], -0.5).then_inc(consts, 1)
                pool.wait_ge(consts, 1)

                def group(i, b):
                    grp = 2 * i + b
                    pool.wait_ge(normed, grp)
                    pool.wait_ge(front_steps, grp * MOMENTS + MOMENTS)
                    pool.tensor_tensor(w.var[:, :], w.mv[:, :, 1], eps[:, :], ALU.add).then_inc(consts, 1)
                    pool.wait_ge(consts, grp + 2)
                    pool.tensor_tensor(w.rstd[:, :], w.var[:, :], half[:, :], ALU.pow).then_inc(rstd_ready, 1)
                    pool.tensor_tensor(base[:, b, :, :], slots[0][:, b, :, :], const[:, :, :],
                                       ALU.add).then_inc(base_ready, 1)

                for_groups(pool, NODE_GROUPS, group)

            @block.vector
            def _(dve):
                f_chain = Chain(front_steps, MOMENTS)
                b_chain = Chain(back_steps, BACK)

                def front(i, b):
                    grp = 2 * i + b
                    f_chain.begin()
                    dve.wait_ge(loaded[b], 16 * len(reads) * (i + 1))
                    x = slots[0][:, b, :, :]
                    if layer == 1:
                        elu_back(dve, grp, f_chain, x, slots[1][:, b, :, :], el, exp_arg, exp_ready, arg_ready)
                        f_chain.done(dve.tensor_tensor(x, x, exp_arg[:, :, :], ALU.add))
                        f_chain.wait(dve, grp)
                    moments(dve, grp, f_chain, [x[:, j, :] for j in range(J)], w.stats, w.mv, w.spot)
                    f_chain.end()
                    dve.wait_ge(rstd_ready, grp + 1)
                    dve.scalar_tensor_tensor(out=w.shift[:, :], in0=w.mv[:, :, 0], scalar=-1.0, in1=w.rstd[:, :],
                                             op0=ALU.mult, op1=ALU.mult).then_inc(shift_ready, 1)
                    if layer == 1:
                        dve.wait_ge(normed, grp + 1)
                        dve.scalar_tensor_tensor(out=h[:, :, :], in0=h[:, :, :], scalar=g.eps1[:, 0:1],
                                                 in1=slots[2][:, b, :, :], op0=ALU.mult, op1=ALU.add
                                                 ).then_inc(h_ready, 1)

                def back(i, b):
                    grp = 2 * i + b
                    b_chain.begin()
                    if layer == 2:
                        dve.wait_ge(mapped, grp + 1)
                        dve.tensor_tensor(pre[:, :, :].rearrange("p (q j) c -> p q (j c)", q=2), p_map[:, :, :],
                                          slots[1][:, b, :, :].rearrange("p (q j) c -> p q (j c)", q=2),
                                          ALU.add).then_inc(pre_ready, 1)
                    if layer == 3:
                        b_chain.done(dve.tensor_scalar(inv[:, :], slots[1][:, b, :, D], 1e-30, None, ALU.max))
                        b_chain.wait(dve, grp)
                        b_chain.done(dve.reciprocal(inv[:, :], inv[:, :]))
                        b_chain.wait(dve, grp)
                        dve.wait_ge(mapped, grp + 1)
                        for j in range(J):
                            ins = dve.scalar_tensor_tensor(out=pre[:, j, :], in0=slots[1][:, b, j, 0:D],
                                                           scalar=inv[:, j:j + 1],
                                                           in1=p_map[:, 0, j * P:(j + 1) * P], op0=ALU.mult,
                                                           op1=ALU.add)
                        ins.then_inc(pre_ready, 1)
                    b_chain.end()
                    dve.wait_ge(stored[b], 16 * i)
                    dve.wait_ge(base_ready, grp + 1)
                    dve.wait_ge(projected, grp + 1)
                    dve.tensor_tensor(done[:, b, :, :], p_out[:, 0, :].rearrange("p (j c) -> p j c", j=J),
                                      base[:, b, :, :], ALU.add).then_inc(out_ready, 1)

                in_turn(dve, NODE_GROUPS, front, back)

            @block.tensor
            def _(pe):
                def front(i, b):
                    grp = 2 * i + b
                    pe.wait_ge(h_made, grp + 1)
                    pe.wait_ge(h_copied, grp)
                    for j in range(J):
                        ins = pe.transpose(p_turned[:, 0, j * P:(j + 1) * P], h[:, j, :], g.ident[:, :])
                    ins.then_inc(h_turned, 1)

                def back(i, b):
                    grp = 2 * i + b
                    pe.wait_ge(h_copied, grp + 1)
                    if layer == 1:
                        for f in range(2):
                            ins = pe.matmul(p_map[:, f, :], g.Wm1[:, f * P:(f + 1) * P], hT[:, b, :], start=True,
                                            stop=True)
                        ins.then_inc(mapped, 1)
                    else:
                        W, n = (g.nW1a, 256) if layer == 2 else (g.Wtop, 128)
                        for j in range(J):
                            at = j * n
                            ins = pe.matmul(p_map[:, at // 512, at % 512:at % 512 + n], hT[:, b, j * P:(j + 1) * P],
                                            W[:, :], start=True, stop=True)
                        ins.then_inc(mapped, 1)
                        pe.wait_ge(pre_ready, grp + 1)
                        for f in range(chunks):
                            for j in range(J):
                                ins = pe.transpose(p_mid[:, f, j * P:(j + 1) * P], pre[:, j, f * P:(f + 1) * P],
                                                   g.ident[:, :])
                        ins.then_inc(mid_turned, 1)
                    pe.wait_ge(mid_ready, chunks * (grp + 1))
                    pe.wait_ge(out_ready, grp)
                    for j in range(J):
                        for f in range(chunks):
                            W2 = {1: g.Wm2[:, f, :], 2: g.nW2[:, f, :], 3: g.dec[:, :]}[layer]
                            ins = pe.matmul(p_out[:, 0, j * P:(j + 1) * P], mid[:, f, j * P:(j + 1) * P], W2,
                                            start=(f == 0), stop=(f == chunks - 1))
                    ins.then_inc(projected, 1)

                in_turn(pe, NODE_GROUPS, front, back)

            @block.scalar
            def _(act):
                act.preload_act_table_set("silu_and_others" if layer == 2 else "exp_and_others")

                def front(i, b):
                    grp = 2 * i + b
                    if layer == 1:
                        act.wait_ge(arg_ready, grp + 1)
                        act.activation(exp_arg[:, :, :], exp_arg[:, :, :], ACT.Exp).then_inc(exp_ready, 1)
                    act.wait_ge(shift_ready, grp + 1)
                    act.wait_ge(h_turned, grp)
                    for j in range(J):
                        ins = act.activation(h[:, j, :], slots[0][:, b, j, :], ACT.Relu, bias=w.shift[:, j:j + 1],
                                             scale=w.rstd[:, j:j + 1])
                    ins.then_inc(normed, 1)
                    act.wait_ge(h_turned, grp + 1)
                    act.activation(hT[:, b, :], p_turned[:, 0, :], ACT.Copy).then_inc(h_copied, 1)

                def back(i, b):
                    grp = 2 * i + b
                    act.wait_ge(mapped if layer == 1 else mid_turned, grp + 1)
                    for f in range(chunks):
                        if layer == 1:
                            ins = act.activation(mid[:, f, :], p_map[:, f, :], ACT.Relu, bias=g.c1[:, f:f + 1],
                                                 scale=g.s1[:, f:f + 1])
                        elif layer == 2:
                            ins = act.activation(mid[:, f, :], p_mid[:, f, :], ACT.Silu, bias=g.nb1[:, f:f + 1])
                        else:
                            ins = act.activation(mid[:, f, :], p_mid[:, f, :], ACT.Relu, bias=g.btop[:, 0:1])
                        ins.then_inc(mid_ready, 1)

                in_turn(act, NODE_GROUPS, front, back)


def kernel(**inputs):
    import concourse.bacc as bacc
    import numpy as np
    from concourse.bass_utils import run_bass_kernel_spmd as run

    nc = bacc.Bacc("TRN2", target_bir_lowering=False, num_devices=1)
    arrays, args = {}, {}
    for name, value in inputs.items():
        value = np.ascontiguousarray(value)
        arrays[f"in_{name}"] = value
        args[name] = nc.dram_tensor(f"in_{name}", value.shape, mybir.dt.from_np(value.dtype),
                                    kind="ExternalInput").ap()
    out = nc.dram_tensor("out_x", (N, D), F32, kind="ExternalOutput").ap()
    build(nc, args, out)
    return run(nc, [arrays], core_ids=[0]).results[0]["out_x"]
```

```python
from contextlib import ExitStack

import concourse.bass as bass
from concourse import mybir

F32 = mybir.dt.float32
I32 = mybir.dt.int32
ALU = mybir.AluOpType
ACT = mybir.ActivationFunctionType
AXX = mybir.AxisListType.X

P = 128
D = 128
N = 50000
E = 25000
J = 4
RING = 4
GROUP = P * J
NODE_GROUPS = -(-N // GROUP)
NPAD = NODE_GROUPS * GROUP
SPARE = NPAD
ROWS = NPAD + P
LAST_P = (N - (NODE_GROUPS - 1) * GROUP) // J
EP = 125
ET = E // EP
EDGE_GROUPS = ET // J
COLS = ET + 2 * J
LN_EPS = 1e-5
MAGIC = 1597463007.0
NEWTON = 3
ZERO = 6288


class Parts:
    pass


def column(ap):
    return ap.rearrange("(k o) -> k o", o=1)


def columns(ap):
    return ap.rearrange("(c k) -> k c", k=P)


def spread(ap):
    return ap.rearrange("(o n) -> o n", o=1).partition_broadcast(P)


class Chain:

    def __init__(self, sem, steps):
        self.sem, self.steps, self.k = sem, steps, 0

    def begin(self):
        self.k = 0

    def done(self, ins):
        self.k += 1
        assert self.k <= self.steps
        ins.then_inc(self.sem, 1)

    def wait(self, eng, g):
        eng.wait_ge(self.sem, g * self.steps + self.k)

    def end(self):
        assert self.k == self.steps, (self.k, self.steps)


def pipeline(eng, groups, stages, peeled=1):
    def turn(i, c):
        for lag, function in stages:
            back, b = divmod(c - lag, RING)
            if isinstance(i, int) and not 0 <= RING * (i + back) + b < groups:
                continue
            function(i + back, b)

    for t in range(peeled * RING):
        turn(t // RING, t % RING)
    with eng.Fori(peeled, groups // RING) as i:
        for c in range(RING):
            turn(i, c)
    for t in range(groups // RING * RING, groups + max(lag for lag, _ in stages)):
        turn(t // RING, t % RING)


def beyond(i, b, count):
    return not isinstance(i, int) or RING * i + b >= count


def rsqrt(dve, g, chain, v, y, t):
    chain.done(dve.tensor_scalar(y.bitcast(I32), v.bitcast(I32), 1, None, ALU.logical_shift_right))
    chain.wait(dve, g)
    chain.done(dve.tensor_scalar(y.bitcast(I32), y.bitcast(I32), -1.0, MAGIC, ALU.mult, ALU.add))
    chain.wait(dve, g)
    for _ in range(NEWTON):
        chain.done(dve.scalar_tensor_tensor(out=t, in0=y, scalar=-0.5, in1=v, op0=ALU.mult, op1=ALU.mult))
        chain.wait(dve, g)
        chain.done(dve.tensor_tensor(t, t, y, ALU.mult))
        chain.wait(dve, g)
        chain.done(dve.scalar_tensor_tensor(out=y, in0=t, scalar=1.5, in1=y, op0=ALU.add, op1=ALU.mult))
        chain.wait(dve, g)


RSQRT_STEPS = 2 + 3 * NEWTON


def moments(dve, g, chain, tiles, stats, mv, spot):
    for k, x in enumerate(tiles):
        ins = dve.bn_stats(stats[:, k, :], x)
    chain.done(ins)
    chain.wait(dve, g)
    dve.memset(spot, 0.0)
    for k in range(len(tiles)):
        ins = dve.bn_aggr(mv[:, k, :], stats[:, k, :])
    chain.done(ins)
    chain.wait(dve, g)


NORM_STEPS = 2 + 1 + RSQRT_STEPS + 1 + 1


def normalise(dve, g, chain, tiles, w):
    n = len(tiles)
    moments(dve, g, chain, tiles, w.stats, w.mv, w.spot)
    chain.done(dve.tensor_scalar(w.var[:, 0:n], w.mv[:, 0:n, 1], LN_EPS, None, ALU.add))
    chain.wait(dve, g)
    rsqrt(dve, g, chain, w.var[:, 0:n], w.rstd[:, 0:n], w.tmp[:, 0:n])
    chain.done(dve.scalar_tensor_tensor(out=w.shift[:, 0:n], in0=w.mv[:, 0:n, 0], scalar=-1.0,
                                        in1=w.rstd[:, 0:n], op0=ALU.mult, op1=ALU.mult))
    chain.wait(dve, g)
    for k, x in enumerate(tiles):
        ins = dve.tensor_scalar(x, x, w.rstd[:, k:k + 1], w.shift[:, k:k + 1], ALU.mult, ALU.add)
    chain.done(ins)
    chain.wait(dve, g)


def norm_space(sb, n):
    q = Parts()
    q.stats = sb("stats", [P, n, 6])
    q.mv = sb("mv", [P, n, 2])
    q.var = sb("var", [P, n])
    q.rstd = sb("rstd", [P, n])
    q.tmp = sb("tmp", [P, n])
    q.shift = sb("shift", [P, n])
    q.spot = sb("spot", [P, 1])[0:1, 0:1]
    return q


def build(nc, a, out):
    with ExitStack() as whole:
        def keep(name, shape, dt=F32):
            return whole.enter_context(nc.sbuf_tensor(name, shape, dt))

        def table(name, rows, width):
            return nc.dram_tensor(name, (rows, width), F32, kind="Internal").ap()

        g = Parts()
        g.T = [table(f"sums{k}", ROWS, w) for k, w in enumerate((D + 1, D, 2 * D, D + 1))]
        g.X = [a["x"], None, table("x2", NPAD, D), table("x3", NPAD, D)]
        g.ident = keep("ident", [P, P])
        g.before = keep("before", [P, P])
        g.src = keep("src_key", [P, COLS])
        g.dst = keep("dst_key", [P, COLS])
        g.src_row = keep("src_row", [P, COLS])
        g.spare = keep("spare", [P, 1])
        g.ew = keep("ew", [P, COLS])
        g.ef = keep("ef", [P, COLS * 16])
        g.zeros = keep("zeros", [P, ZERO])
        g.Wv = keep("Wv", [P, D + 1])
        g.v1 = keep("v1", [P, D])
        g.WE = keep("WE", [17, D])
        g.Wm1 = keep("Wm1", [P, 2 * D])
        g.s1 = keep("s1", [P, 2])
        g.c1 = keep("c1", [P, 2])
        g.Wm2 = keep("Wm2", [P, 2, D])
        g.c2 = keep("c2", [P, J, D])
        g.eps1 = keep("eps1", [P, 1])
        g.eW1s = keep("eW1s", [P, 2 * D])
        g.eW1d = keep("eW1d", [P, 2 * D])
        g.eW1w = keep("eW1w", [P, 2])
        g.eb1 = keep("eb1", [P, 2])
        g.eb2 = keep("eb2", [P, 2])
        g.eW2 = keep("eW2", [P, 2, 2 * D])
        g.nW1a = keep("nW1a", [P, 2 * D])
        g.nW1b = keep("nW1b", [P, 2, 2 * D])
        g.nb1 = keep("nb1", [P, 2])
        g.nW2 = keep("nW2", [P, 2, D])
        g.nb2 = keep("nb2", [P, J, D])
        g.Wsig = keep("Wsig", [P, 16])
        g.bsig = keep("bsig", [P, 8, 16])
        g.Wmsg = keep("Wmsg", [P, D])
        g.bmsg = keep("bmsg", [P, 1])
        g.Wtop = keep("Wtop", [P, D])
        g.btop = keep("btop", [P, 1])
        g.Wbot = keep("Wbot", [P, D])
        g.dec = keep("dec", [P, D])
        g.decb = keep("decb", [P, J, D])
        g.zeroed = [whole.enter_context(nc.semaphore(f"zeroed{k}")) for k in range(4)]
        prepare(nc, a, g)
        edges0(nc, g)
        edges1(nc, g)
        nodes(nc, g, 1, None)
        edges2(nc, g)
        nodes(nc, g, 2, None)
        edges3(nc, g)
        nodes(nc, g, 3, out)


def zero_chunks(t):
    v = t.rearrange("(p r) d -> p (r d)", p=P)
    n = v.shape[1]
    return [(v[:, k:min(k + ZERO, n)], min(ZERO, n - k)) for k in range(0, n, ZERO)]


def prepare(nc, a, g):
    with ExitStack() as ctx:
        sb, sem, ps = makers(nc, ctx, "prepare")
        raw = [sb("raw_src", [P, COLS], I32), sb("raw_dst", [P, COLS], I32)]
        part = sb("part", [P, 1], I32)
        has_edge = sb("has_edge", [P, 1])
        idle_row = sb("idle_row", [P, 1])
        one_row = sb("one_row", [1, 17])
        ones = sb("ones", [P, P])
        half = sb("half", [P, 2 + P])
        W = sb("W", [P, P])
        a12 = sb("a12", [P, 2])
        a1s = sb("a1s", [P, P])
        We1 = sb("We1", [16, 2 * D])
        We1T = sb("We1T", [P, 2, 17])
        We2 = sb("We2", [P, 2, D])
        be1 = sb("be1", [P, 2])
        be2 = sb("be2", [1, D])
        bn1 = sb("bn1", [P, 5, 2])
        bn2 = sb("bn2", [P, 5, D])
        var = sb("var", [P, 2 + D])
        scale = sb("scale", [P, 2 + D])
        c2 = sb("c2row", [P, D])
        enc = sb("enc", [P, D])
        encT = sb("encT", [P, D])
        encb = sb("encb", [P, 1])
        encbs = sb("encbs", [P, P])
        sigw = sb("sigw", [P, 16])
        sigb = sb("sigb", [P, 16])
        msgw = sb("msgw", [P, D])
        msgb = sb("msgb", [P, 1])
        aggt = sb("aggt", [P, D])
        aggb = sb("aggb", [P, 1])
        pT, p1, p2 = (ps(n, 1)[:, 0, :] for n in ("p_turned", "p_first", "p_second"))

        cleared, loaded, consts, turned, copied = (sem(n) for n in (
            "cleared", "weights_loaded", "consts_ready", "turned", "turned_copied"))
        product, vec, root = sem("products_ready"), sem("vec_step"), sem("roots_ready")
        graph = sem("graph_loaded")

        loads = [
            (W[:, :], a["L0_gnn_W"]), (a12[:, :], columns(a["L0_gnn_a"].rearrange("n o -> (n o)"))),
            (We1[:, :], a["L1_gnn_We1"]), (We2[:, :, :], a["L1_gnn_We2"].rearrange("(c k) n -> k c n", k=P)),
            (be1[:, :], columns(a["L1_gnn_be1"])), (be2[:, :], a["L1_gnn_be2"].rearrange("(o n) -> o n", o=1)),
            (g.eps1[:, :], spread(a["L1_gnn_eps"])), (g.Wm1[:, :], a["L1_gnn_Wm1"]),
            (g.Wm2[:, :, :], a["L1_gnn_Wm2"].rearrange("(c k) n -> k c n", k=P)),
            (g.eW1s[:, :], a["L2_gnn_eW1"][0:P, :]), (g.eW1d[:, :], a["L2_gnn_eW1"][P:2 * P, :]),
            (g.eW1w[:, :], columns(a["L2_gnn_eW1"][2 * P:2 * P + 1, :].rearrange("o n -> (o n)"))),
            (g.eb1[:, :], columns(a["L2_gnn_eb1"])), (g.eb2[:, :], columns(a["L2_gnn_eb2"])),
            (g.eW2[:, :, :], a["L2_gnn_eW2"].rearrange("(c k) n -> k c n", k=P)),
            (g.nW1a[:, :], a["L2_gnn_nW1"][0:P, :]),
            (g.nW1b[:, :, :], a["L2_gnn_nW1"][P:3 * P, :].rearrange("(c k) n -> k c n", k=P)),
            (g.nb1[:, :], columns(a["L2_gnn_nb1"])),
            (g.nW2[:, :, :], a["L2_gnn_nW2"].rearrange("(c k) n -> k c n", k=P)),
            (enc[:, :], a["L3_gnn_enc_w"]), (encb[:, :], column(a["L3_gnn_enc_b"])),
            (sigw[:, :], a["L3_gnn_sig_w"]), (sigb[:, :], spread(a["L3_gnn_sig_b"])),
            (msgw[:, :], a["L3_gnn_msg_w"]), (msgb[:, :], column(a["L3_gnn_msg_b"])),
            (aggt[:, :], a["L3_gnn_agg_w"][0:P, :]), (g.Wbot[:, :], a["L3_gnn_agg_w"][P:2 * P, :]),
            (aggb[:, :], column(a["L3_gnn_agg_b"])), (g.dec[:, :], a["L3_gnn_dec_w"]),
        ]
        loads += [(bn1[:, k, :], columns(a["L1_gnn_" + n])) for k, n in enumerate(("g1", "b1", "m1", "v1", "bm1"))]
        loads += [(bn2[:, k, :], spread(a["L1_gnn_" + n])) for k, n in enumerate(("g2", "b2", "m2", "v2", "bm2"))]
        for j in range(J):
            loads += [(g.nb2[:, j, :], spread(a["L2_gnn_nb2"])), (g.decb[:, j, :], spread(a["L3_gnn_dec_b"]))]
        graph_loads = [
            (raw[0][0:EP, 0:ET], a["src"].rearrange("(p t) -> p t", t=ET)),
            (raw[1][0:EP, 0:ET], a["dst"].rearrange("(p t) -> p t", t=ET)),
            (g.ew[0:EP, 0:ET], a["edge_weight1"].rearrange("(p t) o -> p (t o)", t=ET)),
            (g.ef[0:EP, 0:ET * 16], a["edge_attr_16"].rearrange("(p t) d -> p (t d)", t=ET)),
        ]

        with nc.Block() as block:
            @block.sync
            def _(sp):
                sp.wait_ge(cleared, 4)
                for to, of in graph_loads:
                    sp.dma_start(to, of).then_inc(graph, 16)
                sp.wait_ge(consts, 6)
                for to, n in zero_chunks(g.T[0]):
                    sp.dma_start(to, g.zeros[:, 0:n]).then_inc(g.zeroed[0], 16)

            @block.scalar
            def _(act):
                with nc.allow_non_contiguous_dma(reason="short vectors, one element per partition"):
                    for to, of in loads:
                        act.dma_start(to, of).then_inc(loaded, 16)

            @block.gpsimd
            def _(pool):
                pool.memset(raw[0][:, :], 0).then_inc(cleared, 1)
                pool.memset(raw[1][:, :], 0).then_inc(cleared, 1)
                pool.memset(g.ew[:, :], 0.0).then_inc(cleared, 1)
                pool.memset(g.ef[:, :], 0.0).then_inc(cleared, 1)
                pool.memset(g.ident[:, :], 0.0).then_inc(consts, 1)
                pool.memset(g.before[:, :], 1.0).then_inc(consts, 1)
                pool.memset(half[:, :], -0.5)
                pool.iota(part[:, :], [[0, 1]], base=0, channel_multiplier=1)
                pool.wait_ge(consts, 2)
                pool.affine_select(out=g.ident[:, :], in_=g.ident[:, :], compare_op=ALU.not_equal, fill=1.0,
                                   base=0, pattern=[[-1, P]], channel_multiplier=1)
                pool.affine_select(out=g.before[:, :], in_=g.before[:, :], compare_op=ALU.is_gt, fill=0.0,
                                   base=0, pattern=[[-1, P]], channel_multiplier=1).then_inc(consts, 1)
                pool.memset(one_row[:, :], 0.0).then_inc(consts, 1)
                pool.wait_ge(consts, 4)
                pool.memset(one_row[:, 16:17], 1.0).then_inc(consts, 1)
                pool.memset(g.zeros[:, :], 0.0).then_inc(consts, 1)
                pool.wait_ge(vec, 1)
                pool.tensor_tensor(scale[:, :], var[:, :], half[:, :], ALU.pow).then_inc(root, 1)

            @block.tensor
            def _(pe):
                pe.wait_ge(consts, 6)
                pe.wait_ge(loaded, 16 * len(loads))
                pe.transpose(pT[:, 0:128], W[:, :], g.ident[:, :])
                pe.transpose(pT[:, 128:256], enc[:, :], g.ident[:, :])
                for c in range(2):
                    ins = pe.transpose(pT[:, 256 + 16 * c:272 + 16 * c], We1[:, c * P:(c + 1) * P],
                                       g.ident[0:16, 0:16])
                ins.then_inc(turned, 1)
                pe.wait_ge(copied, 1)
                pe.matmul(p1[:, 0:128], a1s[:, :], W[:, :], start=True, stop=True)
                pe.matmul(p1[:, 128:129], W[:, :], a12[:, 1:2], start=True, stop=True)
                pe.matmul(p1[0:17, 129:257], We1T[:, 0, :], We2[:, 0, :], start=True, stop=False)
                pe.matmul(p1[0:17, 129:257], We1T[:, 1, :], We2[:, 1, :], start=False, stop=False)
                pe.matmul(p1[0:17, 129:257], one_row[:, :], be2[:, :], start=False, stop=True)
                pe.matmul(p2[:, 0:128], encT[:, :], msgw[:, :], start=True, stop=True)
                pe.matmul(p2[:, 128:256], encT[:, :], aggt[:, :], start=True, stop=True)
                pe.matmul(p2[:, 256:272], encT[:, :], sigw[:, :], start=True, stop=True)
                pe.matmul(p2[:, 272:288], encbs[:, :], sigw[:, :], start=True, stop=True)
                pe.matmul(p2[:, 288:289], msgw[:, :], encb[:, :], start=True, stop=True)
                pe.matmul(p2[:, 289:290], aggt[:, :], encb[:, :], start=True, stop=True).then_inc(product, 1)

            @block.vector
            def _(dve):
                link = Chain(vec, 99)
                dve.wait_ge(loaded, 16 * len(loads))
                dve.tensor_scalar(var[:, 0:2], bn1[:, 3, :], 1e-3, None, ALU.add)
                link.done(dve.tensor_scalar(var[:, 2:2 + D], bn2[:, 3, :], 1e-3, None, ALU.add))
                dve.tensor_scalar(g.eps1[:, :], g.eps1[:, :], 1.0, None, ALU.add)
                link.done(dve.memset(ones[:, :], 1.0))
                link.wait(dve, 0)
                dve.tensor_scalar(a1s[:, :], ones[:, :], a12[:, 0:1], None, ALU.mult)
                dve.tensor_scalar(encbs[:, :], ones[:, :], encb[:, 0:1], None, ALU.mult)
                dve.wait_ge(turned, 1)
                dve.tensor_copy(g.Wv[:, 0:D], pT[:, 0:128])
                dve.tensor_copy(encT[:, :], pT[:, 128:256])
                for c in range(2):
                    dve.tensor_copy(We1T[:, c, 0:16], pT[:, 256 + 16 * c:272 + 16 * c])
                    ins = dve.tensor_copy(We1T[:, c, 16:17], be1[:, c:c + 1])
                ins.then_inc(copied, 1)
                dve.wait_ge(graph, 16 * len(graph_loads))
                dve.wait_ge(consts, 6)
                link.done(dve.tensor_copy(g.spare[:, :], part[:, :]))
                link.wait(dve, 0)
                dve.tensor_scalar(has_edge[:, :], g.spare[:, :], float(EP), None, ALU.is_lt)
                dve.tensor_scalar(idle_row[:, :], g.spare[:, :], float(EP), None, ALU.is_ge)
                link.done(dve.tensor_scalar(g.spare[:, :], g.spare[:, :], float(SPARE), None, ALU.add))
                link.wait(dve, 0)
                link.done(dve.tensor_tensor(idle_row[:, :], idle_row[:, :], g.spare[:, :], ALU.mult))
                link.wait(dve, 0)
                for key, ids in ((g.src, raw[0]), (g.dst, raw[1])):
                    dve.tensor_scalar(key[:, :], ids[:, :], has_edge[:, 0:1], idle_row[:, 0:1], ALU.mult, ALU.add)
                dve.wait_ge(root, 1)
                for col, bn, s, c in ((0, bn1, g.s1, g.c1), (2, bn2, bn2[:, 3, :], c2)):
                    w = 2 if col == 0 else D
                    s = s[:, 0:w]
                    link.done(dve.tensor_tensor(s, scale[:, col:col + w], bn[:, 0, :], ALU.mult))
                    link.done(dve.tensor_tensor(bn[:, 4, :], bn[:, 4, :], bn[:, 2, :], ALU.subtract))
                    link.wait(dve, 0)
                    link.done(dve.tensor_tensor(bn[:, 4, :], bn[:, 4, :], s, ALU.mult))
                    link.wait(dve, 0)
                    link.done(dve.tensor_tensor(c[:, 0:w], bn[:, 4, :], bn[:, 1, :], ALU.add))
                    link.wait(dve, 0)
                for c in range(2):
                    dve.tensor_tensor(g.Wm2[:, c, :], g.Wm2[:, c, :], bn2[:, 3, :], ALU.mult)
                for j in range(J):
                    dve.tensor_copy(g.c2[:, j, :], c2[:, :])
                dve.wait_ge(product, 1)
                dve.tensor_copy(g.v1[:, :], p1[:, 0:128])
                dve.tensor_copy(g.Wv[:, D:D + 1], p1[:, 128:129])
                dve.tensor_copy(g.WE[:, :], p1[0:17, 129:257])
                dve.tensor_copy(g.Wmsg[:, :], p2[:, 0:128])
                dve.tensor_copy(g.Wtop[:, :], p2[:, 128:256])
                dve.tensor_copy(g.Wsig[:, :], p2[:, 256:272])
                for k in range(8):
                    dve.tensor_tensor(g.bsig[:, k, :], p2[:, 272:288], sigb[:, :], ALU.add)
                dve.tensor_tensor(g.bmsg[:, :], p2[:, 288:289], msgb[:, :], ALU.add)
                dve.tensor_tensor(g.btop[:, :], p2[:, 289:290], aggb[:, :], ALU.add)


def makers(nc, ctx, phase):
    def sb(name, shape, dt=F32):
        return ctx.enter_context(nc.sbuf_tensor(f"{phase}_{name}", shape, dt))

    sems = []

    def sem(name):
        sems.append(nc.alloc_semaphore(f"{phase}_{name}"))
        return sems[-1]

    def clear():
        nc.clear_and_free_semaphores(sems)
        nc.all_engine_barrier()

    ctx.callback(clear)

    def ps(name, banks):
        return ctx.enter_context(nc.psum_tensor(f"{phase}_{name}", [P, banks, 512], F32))

    return sb, sem, ps


def edge_space(nc, ctx, phase, gathers, width):
    sb, sem, ps = makers(nc, ctx, phase)
    q = Parts()
    q.phase = phase
    q.sb = sb
    q.sem = sem
    q.ps = ps
    q.gathers = gathers
    q.rows = [sb(f"rows{k}", [P, 2, J, t.shape[1]]) for k, (t, _) in enumerate(gathers)]
    q.index = [sb(f"index{k}", [P, 2, J], I32) for k, _ in enumerate(gathers)]
    q.key = sb("key", [P, J])
    q.to = sb("scatter_to", [P, 2, J], I32)
    q.total = sb("total", [P, 2, J, width])
    q.equal = sb("equal", [P, J, P])
    q.staged = sem("indices_staged")
    q.gathered = [sem("gathered_even"), sem("gathered_odd")]
    q.scattered = [sem("scattered_even"), sem("scattered_odd")]
    q.key_ready = sem("key_ready")
    q.keys_across = sem("keys_across")
    q.total_ready = sem("total_ready")
    q.settled = sem("settled")
    q.to_ready = sem("scatter_rows_ready")
    q.steps = sem("vec_steps")
    return q


def pool_edges(pool, s, table, used):
    def gather(b, j):
        for (of, _), rows, index in zip(s.gathers, s.rows, s.index):
            pool.indirect_dma_start(rows[:, b, j, :], None, of[:, :],
                                    bass.IndirectOffsetOnAxis(ap=index[:, b, j:j + 1], axis=0)
                                    ).then_inc(s.gathered[b], 16)

    def settle():
        pool.sem_inc(s.settled, 1)

    def scatter(i, b, j):
        if j:
            pool.wait_ge(s.scattered[b], 16 * J * i + 16 * j)
        else:
            pool.wait_ge(s.scattered[1 - b], 16 * J * (i + b))
            pool.wait_ge(s.to_ready, 2 * i + b + 1)
            pool.wait_ge(s.total_ready, 2 * i + b + 1)
        settle()
        pool.indirect_dma_start(table[:, :], bass.IndirectOffsetOnAxis(ap=s.to[:, b, j:j + 1], axis=0),
                                s.total[:, b, j, :], None, compute_op=ALU.add).then_inc(s.scattered[b], 16)

    for b in range(2):
        pool.wait_ge(s.staged, b + 1)
        for j in range(J):
            gather(b, j)
    with pool.Fori(0, EDGE_GROUPS // 2 - 1) as i:
        for b in range(2):
            pool.wait_ge(s.staged, 2 * i + b + 3)
            for rows_read in used:
                pool.wait_ge(rows_read, 2 * i + b + 1)
            settle()
            for j in range(J):
                gather(b, j)
                scatter(i, b, j)
    last = EDGE_GROUPS // 2 - 1
    for b in range(2):
        for j in range(J):
            scatter(last, b, j)
    pool.wait_ge(s.scattered[1], 16 * J * (last + 1))


def stage(dve, s, i, b, ahead):
    for (_, keys), index in zip(s.gathers, s.index):
        ins = dve.tensor_scalar(index[:, b, :], keys[:, bass.ds((2 * i + b + ahead) * J, J)], float(N - 1), None,
                                ALU.min)
    ins.then_inc(s.staged, 1)


def stage_key(dve, s, keys, i, b):
    dve.tensor_scalar(s.key[:, :], keys[:, bass.ds((2 * i + b) * J, J)], 0.0, None,
                      ALU.add).then_inc(s.key_ready, 1)


def arrived(eng, s, i, b):
    eng.wait_ge(s.gathered[b], 16 * J * len(s.gathers) * (i + 1))


def key_rows(pe, s, g_, grp, across):
    pe.wait_ge(s.key_ready, grp + 1)
    for j in range(J):
        ins = pe.transpose(across[:, 0, j * P:(j + 1) * P], s.key[:, j:j + 1].to_broadcast([P, P]), g_.ident[:, :])
    ins.then_inc(s.keys_across, 1)


ROW_STEPS = 5


def scatter_rows(dve, s, g_, i, b, chain, across, w, keep=None):
    grp = 2 * i + b
    dve.wait_ge(s.keys_across, grp + 1)
    for j in range(J):
        ins = dve.scalar_tensor_tensor(out=w.junk[:, j, :], in0=across[:, 0, j * P:(j + 1) * P],
                                       scalar=s.key[:, j:j + 1], in1=g_.before[:, :], op0=ALU.is_equal,
                                       op1=ALU.mult, accum_out=w.rank[:, j:j + 1])
    chain.done(ins)
    chain.wait(dve, grp)
    chain.done(dve.tensor_scalar(w.first[:, :], w.rank[:, :], 0.5, None, ALU.is_lt))
    chain.wait(dve, grp)
    chain.done(dve.scalar_tensor_tensor(out=w.row[:, :], in0=s.key[:, :], scalar=g_.spare[:, 0:1],
                                        in1=w.first[:, :], op0=ALU.subtract, op1=ALU.mult))
    chain.wait(dve, grp)
    chain.done(dve.tensor_scalar(w.row[:, :], w.row[:, :], g_.spare[:, 0:1], None, ALU.add))
    chain.wait(dve, grp)
    dve.wait_ge(s.scattered[b], 16 * J * i)
    dve.tensor_copy(s.to[:, b, :], w.row[:, :]).then_inc(s.to_ready, 1)
    if keep is not None:
        ins = dve.tensor_scalar(keep[:, bass.ds(grp * J, J)], w.row[:, :], 0.0, None, ALU.add)
    else:
        ins = dve.tensor_scalar(w.first[:, :], w.row[:, :], 0.0, None, ALU.add)
    chain.done(ins)


def row_space(sb):
    q = Parts()
    q.junk = sb("junk", [P, J, P])
    q.rank = sb("rank", [P, J])
    q.first = sb("first", [P, J])
    q.row = sb("row", [P, J])
    return q


def known_rows(dve, s, g_, i, b):
    dve.wait_ge(s.scattered[b], 16 * J * i)
    dve.tensor_scalar(s.to[:, b, :], g_.src_row[:, bass.ds((2 * i + b) * J, J)], 0.0, None,
                      ALU.add).then_inc(s.to_ready, 1)


def width129(t, j):
    return t[:, j // 2, (j % 2) * (D + 1):(j % 2 + 1) * (D + 1)]


def halves(t, lo, hi):
    return t[:, :, 0:2 * (D + 1)].rearrange("p h (q c) -> p h q c", q=2)[:, :, :, lo:hi]


def zero_ahead(sp, g, k):
    for to, n in zero_chunks(g.T[k]):
        sp.dma_start(to, g.zeros[:, 0:n]).then_inc(g.zeroed[k], 16)


def all_zeroed(eng, g, k):
    eng.wait_ge(g.zeroed[k], 16 * len(zero_chunks(g.T[k])))


def edges0(nc, g):
    with ExitStack() as ctx:
        s = edge_space(nc, ctx, "edges0", [(g.X[0], g.src), (g.X[0], g.dst)], D + 1)
        sb, sem = s.sb, s.sem
        w = norm_space(sb, 2 * J)
        r = row_space(sb)
        hT = sb("hT", [P, GROUP])
        score = sb("score", [P, J])
        z = sb("z", [P, J])
        alpha = sb("alpha", [P, J])
        msg = sb("msg", [P, J, D + 1])
        scored_junk = sb("scored_junk", [P, J, P])
        turned, across, prod, tot = s.ps("p_turned", 1), s.ps("p_across", 1), s.ps("p_prod", 2), s.ps("p_tot", 2)
        ones_set, h_norm, h_turned, h_copied, projected, z_ready, exp_ready, msg_ready, sel_ready, summed, scored = (
            sem(n) for n in ("ones_set", "h_normed", "h_turned", "h_copied", "projected", "z_ready", "exp_ready",
                             "messages_ready", "selection_ready", "summed", "source_scored"))
        K = NORM_STEPS + ROW_STEPS + 2

        with nc.Block() as block:
            @block.sync
            def _(sp):
                for k in range(1, 4):
                    zero_ahead(sp, g, k)

            @block.gpsimd
            def _(pool):
                all_zeroed(pool, g, 0)
                pool_edges(pool, s, g.T[0], used=(scored, h_turned))

            @block.vector
            def _(dve):
                chain = Chain(s.steps, K)
                dve.memset(msg[:, :, D:D + 1], 1.0).then_inc(ones_set, 1)
                stage(dve, s, 0, 0, 0)
                stage(dve, s, 0, 1, 0)

                def group(i, b):
                    grp = 2 * i + b
                    chain.begin()
                    dve.wait_ge(sel_ready, grp)
                    arrived(dve, s, i, b)
                    stage(dve, s, i, b, 2)
                    stage_key(dve, s, g.src, i, b)
                    src, dst = ([t[:, b, j, :] for j in range(J)] for t in s.rows)
                    normalise(dve, grp, chain, dst + src, w)
                    for j in range(J):
                        ins = dve.scalar_tensor_tensor(out=scored_junk[:, j, :], in0=src[j], scalar=0.0, in1=g.v1[:, :],
                                                       op0=ALU.max, op1=ALU.mult, accum_out=score[:, j:j + 1])
                    ins.then_inc(scored, 1)
                    scatter_rows(dve, s, g, i, b, chain, across, r, keep=g.src_row)
                    dve.wait_ge(projected, grp + 1)
                    chain.done(dve.tensor_tensor(z[:, :].rearrange("p (h q) -> p h q", h=2),
                                                 halves(prod, D, D + 1).rearrange("p h q o -> p h (q o)"),
                                                 score[:, :].rearrange("p (h q) -> p h q", h=2), ALU.add))
                    chain.wait(dve, grp)
                    dve.scalar_tensor_tensor(out=z[:, :], in0=z[:, :], scalar=0.2, in1=z[:, :], op0=ALU.mult,
                                             op1=ALU.max).then_inc(z_ready, 1)
                    dve.wait_ge(exp_ready, grp + 1)
                    chain.done(dve.tensor_scalar(alpha[:, :], alpha[:, :], 5.0, -5.0, ALU.min, ALU.max))
                    chain.wait(dve, grp)
                    for j in range(J):
                        ins = dve.tensor_scalar(s.equal[:, j, :], across[:, 0, j * P:(j + 1) * P], s.key[:, j:j + 1],
                                                alpha[:, j:j + 1], ALU.is_equal, ALU.mult)
                    ins.then_inc(sel_ready, 1)
                    chain.end()

                for_groups(dve, EDGE_GROUPS, group)

            @block.tensor
            def _(pe):
                def group(i, b):
                    grp = 2 * i + b
                    key_rows(pe, s, g, grp, across)
                    pe.wait_ge(s.steps, grp * K + NORM_STEPS)
                    for j in range(J):
                        ins = pe.transpose(turned[:, 0, j * P:(j + 1) * P], s.rows[1][:, b, j, :], g.ident[:, :])
                    ins.then_inc(h_turned, 1)
                    pe.wait_ge(h_copied, grp + 1)
                    for j in range(J):
                        ins = pe.matmul(width129(prod, j), hT[:, j * P:(j + 1) * P], g.Wv[:, :], start=True, stop=True)
                    ins.then_inc(projected, 1)
                    pe.wait_ge(msg_ready, grp + 1)
                    pe.wait_ge(sel_ready, grp + 1)
                    for j in range(J):
                        ins = pe.matmul(width129(tot, j), s.equal[:, j, :], msg[:, j, :], start=True, stop=True)
                    ins.then_inc(summed, 1)

                for_groups(pe, EDGE_GROUPS, group)

            @block.scalar
            def _(act):
                act.preload_act_table_set("exp_and_others")
                act.wait_ge(ones_set, 1)

                def group(i, b):
                    grp = 2 * i + b
                    act.wait_ge(h_turned, grp + 1)
                    act.activation(hT[:, :], turned[:, 0, :], ACT.Relu).then_inc(h_copied, 1)
                    act.wait_ge(z_ready, grp + 1)
                    act.activation(alpha[:, :], z[:, :], ACT.Exp, scale=-1.0).then_inc(exp_ready, 1)
                    act.activation(msg[:, :, 0:D].rearrange("p (h q) c -> p h q c", h=2), halves(prod, 0, D),
                                   ACT.Copy).then_inc(msg_ready, 1)
                    act.wait_ge(summed, grp + 1)
                    act.wait_ge(s.scattered[b], 16 * J * i)
                    act.activation(s.total[:, b, :, :].rearrange("p (h q) c -> p h q c", h=2), halves(tot, 0, D + 1),
                                   ACT.Copy).then_inc(s.total_ready, 1)

                for_groups(act, EDGE_GROUPS, group)


def for_groups(eng, groups, group):
    with eng.Fori(0, groups // 2) as i:
        group(i, 0)
        group(i, 1)


ELU_FIRST_STEPS = 4


def elu_first(dve, grp, chain, sums, w, exp_arg, arg_ready):
    weight = sums[:, :, D]
    chain.done(dve.tensor_scalar(w.guard[:, :], weight, 0.0, 1e-8, ALU.is_le, ALU.mult))
    chain.wait(dve, grp)
    chain.done(dve.tensor_tensor(w.guard[:, :], w.guard[:, :], weight, ALU.add))
    chain.wait(dve, grp)
    chain.done(dve.reciprocal(w.inv[:, :], w.guard[:, :]))
    chain.wait(dve, grp)
    for j in range(J):
        ins = dve.tensor_scalar(exp_arg[:, j, :], sums[:, j, 0:D], w.inv[:, j:j + 1], 0.0, ALU.mult, ALU.min)
    ins.then_inc(arg_ready, 1)
    for j in range(J):
        ins = dve.tensor_scalar(w.pos[:, j, :], sums[:, j, 0:D], w.inv[:, j:j + 1], 0.0, ALU.mult, ALU.max)
    chain.done(ins)


def elu_second(dve, grp, first, chain, x, w, exp_arg):
    dve.wait_ge(first.sem, (grp + 1) * first.steps)
    chain.done(dve.scalar_tensor_tensor(out=x, in0=w.pos[:, :, :], scalar=-1.0, in1=x, op0=ALU.add, op1=ALU.add))
    chain.wait(dve, grp)
    chain.done(dve.tensor_tensor(x, x, exp_arg[:, :, :], ALU.add))
    chain.wait(dve, grp)


def elu_space(sb):
    q = Parts()
    q.guard = sb("guard", [P, J])
    q.inv = sb("inv", [P, J])
    q.pos = sb("pos", [P, J, D])
    return q


def edges1(nc, g):
    with ExitStack() as ctx:
        s = edge_space(nc, ctx, "edges1", [(g.X[0], g.src), (g.T[0], g.src)], D)
        sb, sem = s.sb, s.sem
        w = norm_space(sb, J)
        r = row_space(sb)
        el = elu_space(sb)
        exp_arg = sb("exp_arg", [P, J, D])
        feat = sb("feat", [P, J * 16])
        featT = sb("featT", [17, GROUP])
        msg = sb("msg", [P, J, D])
        across, turned, mapped, tot = (s.ps(n, 1) for n in ("p_across", "p_turned", "p_mapped", "p_tot"))
        ones_set, feat_ready, f_turned, f_copied, f_mapped, arg_ready, exp_ready, added, msg_ready, sel_ready, \
            summed = (sem(n) for n in ("ones_set", "features_staged", "features_turned", "features_copied",
                                       "features_mapped", "exp_arg_ready", "exp_ready", "message_added",
                                       "messages_ready", "selection_ready", "summed"))
        K = ELU_FIRST_STEPS + 2 + NORM_STEPS + ROW_STEPS

        with nc.Block() as block:
            @block.gpsimd
            def _(pool):
                all_zeroed(pool, g, 1)
                pool_edges(pool, s, g.T[1], used=(added,))

            @block.vector
            def _(dve):
                chain = Chain(s.steps, K)
                dve.memset(featT[:, :], 1.0).then_inc(ones_set, 1)
                stage(dve, s, 0, 0, 0)
                stage(dve, s, 0, 1, 0)

                def group(i, b):
                    grp = 2 * i + b
                    chain.begin()
                    dve.wait_ge(sel_ready, grp)
                    dve.tensor_scalar(feat[:, :], g.ef[:, bass.ds(grp * (J * 16), J * 16)], 0.0, None,
                                      ALU.add).then_inc(feat_ready, 1)
                    stage_key(dve, s, g.dst, i, b)
                    arrived(dve, s, i, b)
                    stage(dve, s, i, b, 2)
                    x, sums = s.rows[0][:, b, :, :], s.rows[1][:, b, :, :]
                    elu_first(dve, grp, chain, sums, el, exp_arg, arg_ready)
                    dve.wait_ge(exp_ready, grp + 1)
                    chain.wait(dve, grp)
                    chain.done(dve.scalar_tensor_tensor(out=x, in0=el.pos[:, :, :], scalar=-1.0, in1=x, op0=ALU.add,
                                                        op1=ALU.add))
                    chain.wait(dve, grp)
                    chain.done(dve.tensor_tensor(x, x, exp_arg[:, :, :], ALU.add))
                    chain.wait(dve, grp)
                    normalise(dve, grp, chain, [x[:, j, :] for j in range(J)], w)
                    dve.wait_ge(f_mapped, grp + 1)
                    dve.scalar_tensor_tensor(out=msg[:, :, :], in0=x, scalar=0.0,
                                             in1=mapped[:, 0, :].rearrange("p (j c) -> p j c", j=J),
                                             op0=ALU.max, op1=ALU.add).then_inc(added, 1)
                    scatter_rows(dve, s, g, i, b, chain, across, r)
                    for j in range(J):
                        ins = dve.tensor_scalar(s.equal[:, j, :], across[:, 0, j * P:(j + 1) * P], s.key[:, j:j + 1],
                                                None, ALU.is_equal)
                    ins.then_inc(sel_ready, 1)
                    chain.end()

                for_groups(dve, EDGE_GROUPS, group)

            @block.tensor
            def _(pe):
                def group(i, b):
                    grp = 2 * i + b
                    pe.wait_ge(feat_ready, grp + 1)
                    for j in range(J):
                        ins = pe.transpose(turned[0:16, 0, j * P:(j + 1) * P], feat[:, j * 16:(j + 1) * 16],
                                           g.ident[:, :])
                    ins.then_inc(f_turned, 1)
                    key_rows(pe, s, g, grp, across)
                    pe.wait_ge(f_copied, grp + 1)
                    for j in range(J):
                        ins = pe.matmul(mapped[:, 0, j * P:(j + 1) * P], featT[:, j * P:(j + 1) * P], g.WE[:, :],
                                        start=True, stop=True)
                    ins.then_inc(f_mapped, 1)
                    pe.wait_ge(msg_ready, grp + 1)
                    pe.wait_ge(sel_ready, grp + 1)
                    for j in range(J):
                        ins = pe.matmul(tot[:, 0, j * P:(j + 1) * P], s.equal[:, j, :], msg[:, j, :],
                                        start=True, stop=True)
                    ins.then_inc(summed, 1)

                for_groups(pe, EDGE_GROUPS, group)

            @block.scalar
            def _(act):
                act.preload_act_table_set("exp_and_others")
                act.wait_ge(ones_set, 1)

                def group(i, b):
                    grp = 2 * i + b
                    act.wait_ge(f_turned, grp + 1)
                    act.activation(featT[0:16, :], turned[0:16, 0, :], ACT.Copy).then_inc(f_copied, 1)
                    act.wait_ge(arg_ready, grp + 1)
                    act.activation(exp_arg[:, :, :], exp_arg[:, :, :], ACT.Exp).then_inc(exp_ready, 1)
                    act.wait_ge(added, grp + 1)
                    act.activation(msg[:, :, :], msg[:, :, :], ACT.Relu).then_inc(msg_ready, 1)
                    act.wait_ge(summed, grp + 1)
                    act.wait_ge(s.scattered[b], 16 * J * i)
                    act.activation(s.total[:, b, :, :], tot[:, 0, :].rearrange("p (j c) -> p j c", j=J),
                                   ACT.Copy).then_inc(s.total_ready, 1)

                for_groups(act, EDGE_GROUPS, group)


def edges2(nc, g):
    with ExitStack() as ctx:
        s = edge_space(nc, ctx, "edges2", [(g.X[2], g.src), (g.X[2], g.dst)], 2 * D)
        sb, sem = s.sb, s.sem
        w = norm_space(sb, 2 * J)
        hT = [sb("hT_src", [P, GROUP]), sb("hT_dst", [P, GROUP])]
        ewc = sb("ew_column", [P, J])
        ewr = sb("ew_rows", [P, GROUP])
        m1 = sb("m1", [P, 2, GROUP])
        m2 = sb("m2", [P, 2, GROUP])
        msg = sb("msg", [P, J, 2 * D])
        across, wide = s.ps("p_across", 1), s.ps("p_ew", 1)
        turned, mid, tail = s.ps("p_turned", 2), s.ps("p_mid", 2), s.ps("p_tail", 2)
        names = ("h_turned", "h_copied", "ew_across", "ew_copied", "first_map", "first_added", "first_silu",
                 "second_map", "second_silu", "third_map", "messages_ready", "selection_ready", "summed")
        (h_turned, h_copied, ew_across, ew_copied, map1, added1, silu1, map2, silu2, map3, msg_ready, sel_ready,
         summed) = (sem(n) for n in names)
        K = NORM_STEPS

        with nc.Block() as block:
            @block.gpsimd
            def _(pool):
                all_zeroed(pool, g, 2)
                pool_edges(pool, s, g.T[2], used=(h_turned,))

            @block.vector
            def _(dve):
                chain = Chain(s.steps, K)
                stage(dve, s, 0, 0, 0)
                stage(dve, s, 0, 1, 0)

                def group(i, b):
                    grp = 2 * i + b
                    chain.begin()
                    dve.wait_ge(sel_ready, grp)
                    arrived(dve, s, i, b)
                    stage(dve, s, i, b, 2)
                    dve.tensor_scalar(ewc[:, :], g.ew[:, bass.ds(grp * J, J)], 0.0, None, ALU.add)
                    stage_key(dve, s, g.src, i, b)
                    src, dst = ([t[:, b, j, :] for j in range(J)] for t in s.rows)
                    normalise(dve, grp, chain, src + dst, w)
                    dve.wait_ge(s.keys_across, grp + 1)
                    for j in range(J):
                        ins = dve.tensor_scalar(s.equal[:, j, :], across[:, 0, j * P:(j + 1) * P], s.key[:, j:j + 1],
                                                None, ALU.is_equal)
                    ins.then_inc(sel_ready, 1)
                    known_rows(dve, s, g, i, b)
                    dve.wait_ge(ew_copied, grp + 1)
                    for f in range(2):
                        dve.wait_ge(map1, 2 * grp + f + 1)
                        dve.scalar_tensor_tensor(out=m1[:, f, :], in0=ewr[:, :], scalar=g.eW1w[:, f:f + 1],
                                                 in1=mid[:, f, :], op0=ALU.mult, op1=ALU.add).then_inc(added1, 1)
                    dve.wait_ge(map3, grp + 1)
                    dve.tensor_copy(msg[:, :, :].rearrange("p (h q) c -> p h (q c)", h=2), tail[:, :, :]
                                    ).then_inc(msg_ready, 1)
                    chain.end()

                for_groups(dve, EDGE_GROUPS, group)

            @block.tensor
            def _(pe):
                def group(i, b):
                    grp = 2 * i + b
                    key_rows(pe, s, g, grp, across)
                    for j in range(J):
                        ins = pe.transpose(wide[:, 0, j * P:(j + 1) * P], ewc[:, j:j + 1].to_broadcast([P, P]),
                                           g.ident[:, :])
                    ins.then_inc(ew_across, 1)
                    pe.wait_ge(s.steps, grp * K + NORM_STEPS)
                    for k in range(2):
                        for j in range(J):
                            ins = pe.transpose(turned[:, k, j * P:(j + 1) * P], s.rows[k][:, b, j, :], g.ident[:, :])
                    ins.then_inc(h_turned, 1)
                    pe.wait_ge(h_copied, grp + 1)
                    for f in range(2):
                        pe.matmul(mid[:, f, :], g.eW1s[:, f * P:(f + 1) * P], hT[0][:, :], start=True, stop=False)
                        pe.matmul(mid[:, f, :], g.eW1d[:, f * P:(f + 1) * P], hT[1][:, :], start=False,
                                  stop=True).then_inc(map1, 1)
                    for f in range(2):
                        pe.wait_ge(silu1, 2 * grp + 2)
                        for k in range(2):
                            ins = pe.matmul(mid[:, f, :], g.eW2[:, k, f * P:(f + 1) * P], m1[:, k, :],
                                            start=(k == 0), stop=(k == 1))
                        ins.then_inc(map2, 1)
                    pe.wait_ge(silu2, 2 * grp + 2)
                    pe.wait_ge(s.total_ready, grp)
                    for j in range(J):
                        for k in range(2):
                            ins = pe.matmul(tail[:, j // 2, (j % 2) * 256:(j % 2 + 1) * 256],
                                            m2[:, k, j * P:(j + 1) * P], g.nW1b[:, k, :],
                                            start=(k == 0), stop=(k == 1))
                    ins.then_inc(map3, 1)
                    pe.wait_ge(msg_ready, grp + 1)
                    pe.wait_ge(sel_ready, grp + 1)
                    for j in range(J):
                        ins = pe.matmul(tail[:, j // 2, (j % 2) * 256:(j % 2 + 1) * 256], s.equal[:, j, :],
                                        msg[:, j, :], start=True, stop=True)
                    ins.then_inc(summed, 1)

                for_groups(pe, EDGE_GROUPS, group)

            @block.scalar
            def _(act):
                act.preload_act_table_set("silu_and_others")

                def group(i, b):
                    grp = 2 * i + b
                    act.wait_ge(ew_across, grp + 1)
                    act.activation(ewr[:, :], wide[:, 0, :], ACT.Copy).then_inc(ew_copied, 1)
                    act.wait_ge(h_turned, grp + 1)
                    act.activation(hT[0][:, :], turned[:, 0, :], ACT.Relu)
                    act.activation(hT[1][:, :], turned[:, 1, :], ACT.Relu).then_inc(h_copied, 1)
                    for f in range(2):
                        act.wait_ge(added1, 2 * grp + f + 1)
                        act.activation(m1[:, f, :], m1[:, f, :], ACT.Silu, bias=g.eb1[:, f:f + 1]).then_inc(silu1, 1)
                    for f in range(2):
                        act.wait_ge(map2, 2 * grp + f + 1)
                        act.activation(m2[:, f, :], mid[:, f, :], ACT.Silu, bias=g.eb2[:, f:f + 1]).then_inc(silu2, 1)
                    act.wait_ge(summed, grp + 1)
                    act.wait_ge(s.scattered[b], 16 * J * i)
                    act.activation(s.total[:, b, :, :].rearrange("p (h q) c -> p h (q c)", h=2), tail[:, :, :],
                                   ACT.Copy).then_inc(s.total_ready, 1)

                for_groups(act, EDGE_GROUPS, group)


def edges3(nc, g):
    with ExitStack() as ctx:
        s = edge_space(nc, ctx, "edges3", [(g.X[3], g.src), (g.X[3], g.dst)], D + 1)
        sb, sem = s.sb, s.sem
        w = norm_space(sb, 2 * J)
        hT = [sb("hT_src", [P, GROUP]), sb("hT_dst", [P, GROUP])]
        sig = sb("sig", [P, 2 * J, 16])
        square = sb("square", [P, 2 * J, 16])
        cross = sb("cross", [P, J, 16])
        norm2 = sb("norm2", [P, 2 * J])
        inv = sb("inv_norm", [P, 2 * J])
        tmp = sb("tmp_norm", [P, 2 * J])
        dot = sb("dot", [P, J])
        e = sb("e", [P, J])
        mT = sb("msgT", [P, GROUP])
        msg = sb("msg", [P, J, D + 1])
        across, sigs, mid = s.ps("p_across", 1), s.ps("p_sig", 1), s.ps("p_mid", 1)
        turned, tail = s.ps("p_turned", 2), s.ps("p_tail", 2)
        names = ("ones_set", "h_turned", "h_copied", "sig_ready", "msg_map", "msg_relu", "agg_map", "messages_ready",
                 "dot_ready", "exp_ready", "selection_ready", "summed")
        (ones_set, h_turned, h_copied, sig_ready, map1, relu1, map2, msg_ready, dot_ready, exp_ready, sel_ready,
         summed) = (sem(n) for n in names)
        K = NORM_STEPS + 4 + RSQRT_STEPS + 1

        with nc.Block() as block:
            @block.gpsimd
            def _(pool):
                all_zeroed(pool, g, 3)
                pool_edges(pool, s, g.T[3], used=(h_turned,))

            @block.vector
            def _(dve):
                chain = Chain(s.steps, K)
                dve.memset(msg[:, :, D:D + 1], 1.0).then_inc(ones_set, 1)
                stage(dve, s, 0, 0, 0)
                stage(dve, s, 0, 1, 0)

                def group(i, b):
                    grp = 2 * i + b
                    chain.begin()
                    dve.wait_ge(sel_ready, grp)
                    arrived(dve, s, i, b)
                    stage(dve, s, i, b, 2)
                    stage_key(dve, s, g.src, i, b)
                    src, dst = ([t[:, b, j, :] for j in range(J)] for t in s.rows)
                    normalise(dve, grp, chain, src + dst, w)
                    known_rows(dve, s, g, i, b)
                    dve.wait_ge(sig_ready, grp + 1)
                    chain.done(dve.tensor_tensor(sig[:, :, :], sigs[:, 0, 0:128].rearrange("p (k c) -> p k c", c=16),
                                                 g.bsig[:, :, :], ALU.add))
                    chain.wait(dve, grp)
                    dve.tensor_tensor(square[:, :, :], sig[:, :, :], sig[:, :, :], ALU.mult)
                    chain.done(dve.tensor_tensor(cross[:, :, :], sig[:, 0:J, :], sig[:, J:2 * J, :], ALU.mult))
                    chain.wait(dve, grp)
                    dve.tensor_reduce(norm2[:, :], square[:, :, :], AXX, ALU.add)
                    chain.done(dve.tensor_reduce(dot[:, :], cross[:, :, :], AXX, ALU.add))
                    chain.wait(dve, grp)
                    chain.done(dve.tensor_scalar(norm2[:, :], norm2[:, :], 1e-24, None, ALU.max))
                    chain.wait(dve, grp)
                    rsqrt(dve, grp, chain, norm2[:, :], inv[:, :], tmp[:, :])
                    chain.done(dve.tensor_tensor(dot[:, :], dot[:, :], inv[:, 0:J], ALU.mult))
                    chain.wait(dve, grp)
                    dve.tensor_tensor(dot[:, :], dot[:, :], inv[:, J:2 * J], ALU.mult).then_inc(dot_ready, 1)
                    dve.wait_ge(s.keys_across, grp + 1)
                    dve.wait_ge(exp_ready, grp + 1)
                    for j in range(J):
                        ins = dve.tensor_scalar(s.equal[:, j, :], across[:, 0, j * P:(j + 1) * P], s.key[:, j:j + 1],
                                                e[:, j:j + 1], ALU.is_equal, ALU.mult)
                    ins.then_inc(sel_ready, 1)
                    chain.end()

                for_groups(dve, EDGE_GROUPS, group)

            @block.tensor
            def _(pe):
                def group(i, b):
                    grp = 2 * i + b
                    key_rows(pe, s, g, grp, across)
                    pe.wait_ge(s.steps, grp * K + NORM_STEPS)
                    for k in range(2):
                        for j in range(J):
                            ins = pe.transpose(turned[:, k, j * P:(j + 1) * P], s.rows[k][:, b, j, :], g.ident[:, :])
                    ins.then_inc(h_turned, 1)
                    pe.wait_ge(h_copied, grp + 1)
                    for k in range(2):
                        for j in range(J):
                            at = (k * J + j) * 16
                            ins = pe.matmul(sigs[:, 0, at:at + 16], hT[k][:, j * P:(j + 1) * P], g.Wsig[:, :],
                                            start=True, stop=True)
                    ins.then_inc(sig_ready, 1)
                    pe.matmul(mid[:, 0, :], g.Wmsg[:, :], hT[1][:, :], start=True, stop=True).then_inc(map1, 1)
                    pe.wait_ge(relu1, grp + 1)
                    for j in range(J):
                        at = (j % 2) * (D + 1)
                        ins = pe.matmul(tail[:, j // 2, at:at + D], mT[:, j * P:(j + 1) * P], g.Wbot[:, :],
                                        start=True, stop=True)
                    ins.then_inc(map2, 1)
                    pe.wait_ge(msg_ready, grp + 1)
                    pe.wait_ge(sel_ready, grp + 1)
                    for j in range(J):
                        ins = pe.matmul(width129(tail, j), s.equal[:, j, :], msg[:, j, :], start=True, stop=True)
                    ins.then_inc(summed, 1)

                for_groups(pe, EDGE_GROUPS, group)

            @block.scalar
            def _(act):
                act.preload_act_table_set("exp_and_others")
                act.wait_ge(ones_set, 1)

                def group(i, b):
                    grp = 2 * i + b
                    act.wait_ge(h_turned, grp + 1)
                    act.activation(hT[0][:, :], turned[:, 0, :], ACT.Relu)
                    act.activation(hT[1][:, :], turned[:, 1, :], ACT.Relu).then_inc(h_copied, 1)
                    act.wait_ge(map1, grp + 1)
                    act.activation(mT[:, :], mid[:, 0, :], ACT.Relu, bias=g.bmsg[:, 0:1]).then_inc(relu1, 1)
                    act.wait_ge(map2, grp + 1)
                    act.activation(msg[:, :, 0:D].rearrange("p (h q) c -> p h q c", h=2), halves(tail, 0, D),
                                   ACT.Copy).then_inc(msg_ready, 1)
                    act.wait_ge(dot_ready, grp + 1)
                    act.activation(e[:, :], dot[:, :], ACT.Exp).then_inc(exp_ready, 1)
                    act.wait_ge(summed, grp + 1)
                    act.wait_ge(s.scattered[b], 16 * J * i)
                    act.activation(s.total[:, b, :, :].rearrange("p (h q) c -> p h q c", h=2), halves(tail, 0, D + 1),
                                   ACT.Copy).then_inc(s.total_ready, 1)

                for_groups(act, EDGE_GROUPS, group)


def nodes(nc, g, layer, out):
    with ExitStack() as ctx:
        sb, sem, ps = makers(nc, ctx, f"nodes{layer}")
        reads = {1: [g.X[0], g.T[0], g.T[1]], 2: [g.X[2], g.T[2]], 3: [g.X[3], g.T[3]]}[layer]
        to = {1: g.X[2], 2: g.X[3], 3: out}[layer]
        const = {1: g.c2, 2: g.nb2, 3: g.decb}[layer]
        slots = [sb(f"slots{k}", [P, RING, J, t.shape[1]]) for k, t in enumerate(reads)]
        stats = sb("stats", [P, J, 6])
        mv = sb("mv", [P, J, 2])
        spot = sb("spot", [P, 1])[0:1, 0:1]
        var = sb("var", [P, J])
        rstd = sb("rstd", [P, 2, J])
        shift = sb("shift", [P, 2, J])
        eps = sb("eps", [P, J])
        half = sb("half", [P, J])
        base = sb("base", [P, RING, J, D])
        h = sb("h", [P, 2, J, D])
        hT = sb("hT", [P, 2, GROUP])
        mid = sb("mid", [P, 2, 2, GROUP])
        pre = sb("pre", [P, 2, J, 2 * D if layer == 2 else D])
        done = sb("done", [P, RING, J, D])
        inv = sb("inv_weight", [P, J])
        if layer == 1:
            el = elu_space(sb)
            exp_arg = sb("exp_arg", [P, J, D])
        p_turned, p_map, p_mid, p_out = ps("p_turned", 1), ps("p_map", 2), ps("p_mid", 2), ps("p_out", 2)
        (consts, var_ready, rstd_ready, base_ready, shift_ready, normed, mixed, h_turned, h_copied, mapped,
         pre_ready, mid_turned, mid_ready, projected, out_ready, arg_ready, exp_ready, elu_steps, stat_steps,
         pre_steps) = (
            sem(n) for n in (
                "consts_set", "var_ready", "rstd_ready", "base_ready", "shift_ready", "normed", "mixed", "h_turned",
                "h_copied", "mapped", "pre_ready", "mid_turned", "mid_ready", "projected", "out_ready",
                "exp_arg_ready", "exp_ready", "elu_steps", "stat_steps", "pre_steps"))
        loaded = [sem(f"loaded{b}") for b in range(RING)]
        stored = [sem(f"stored{b}") for b in range(RING)]
        h_made = mixed if layer == 1 else normed
        STATS = 4 if layer == 1 else 2
        FIRST = 1 if layer == 1 else 0
        chunks = 1 if layer == 3 else 2

        with nc.Block() as block:
            @block.sync
            def _(sp):
                def rows(t, i, b, parts=P):
                    return t[bass.ds((RING * i + b) * GROUP, parts * J), :].rearrange("(p j) d -> p j d", j=J)

                def load(i, b):
                    last = isinstance(i, int) and RING * i + b == NODE_GROUPS - 1
                    for t, slot in zip(reads, slots):
                        n = LAST_P if last and t.shape[0] == N else P
                        sp.dma_start(slot[0:n, b, :, :], rows(t, i, b, n)).then_inc(loaded[b], 16)

                def reload(i, b):
                    grp = RING * i + b
                    if isinstance(i, int) and grp + RING >= NODE_GROUPS:
                        return
                    sp.wait_ge(normed, grp + 1)
                    sp.wait_ge(base_ready, grp + 1)
                    sp.wait_ge(mixed if layer == 1 else pre_ready, grp + 1)
                    load(i + 1, b)

                def store(i, b):
                    last = isinstance(i, int) and RING * i + b == NODE_GROUPS - 1
                    n = LAST_P if last and layer == 3 else P
                    sp.wait_ge(out_ready, RING * i + b + 1)
                    sp.dma_start(rows(to, i, b, n), done[0:n, b, :, :]).then_inc(stored[b], 16)

                for b in range(RING):
                    load(0, b)
                pipeline(sp, NODE_GROUPS, [(3, reload), (4, store)])
                for b in range(RING):
                    sp.wait_ge(stored[b], 16 * len(range(b, NODE_GROUPS, RING)))

            @block.gpsimd
            def _(pool):
                pool.memset(eps[:, :], LN_EPS)
                pool.memset(half[:, :], -0.5).then_inc(consts, 1)
                pool.wait_ge(consts, 1)

                def roots(i, b):
                    grp = RING * i + b
                    pool.wait_ge(stat_steps, grp * STATS + STATS)
                    pool.tensor_tensor(var[:, :], mv[:, :, 1], eps[:, :], ALU.add).then_inc(var_ready, 1)
                    pool.wait_ge(var_ready, grp + 1)
                    if beyond(i, b, 2):
                        pool.wait_ge(normed, grp - 1)
                    pool.tensor_tensor(rstd[:, b % 2, :], var[:, :], half[:, :], ALU.pow).then_inc(rstd_ready, 1)

                def add_bias(i, b):
                    grp = RING * i + b
                    if beyond(i, b, RING):
                        pool.wait_ge(out_ready, RING * (i - 1) + b + 1)
                    pool.tensor_tensor(base[:, b, :, :], slots[0][:, b, :, :], const[:, :, :],
                                       ALU.add).then_inc(base_ready, 1)

                pipeline(pool, NODE_GROUPS, [(FIRST, roots), (FIRST, add_bias)])

            @block.vector
            def _(dve):
                elu_chain = Chain(elu_steps, ELU_FIRST_STEPS)
                stat_chain = Chain(stat_steps, STATS)
                pre_chain = Chain(pre_steps, 2)

                def elu(i, b):
                    grp = RING * i + b
                    elu_chain.begin()
                    dve.wait_ge(loaded[b], 16 * len(reads) * (i + 1))
                    dve.wait_ge(stat_steps, grp * STATS)
                    elu_first(dve, grp, elu_chain, slots[1][:, b, :, :], el, exp_arg, arg_ready)
                    elu_chain.end()

                def moment(i, b):
                    grp = RING * i + b
                    x = slots[0][:, b, :, :]
                    stat_chain.begin()
                    if layer == 1:
                        dve.wait_ge(exp_ready, grp + 1)
                        elu_second(dve, grp, elu_chain, stat_chain, x, el, exp_arg)
                    else:
                        dve.wait_ge(loaded[b], 16 * len(reads) * (i + 1))
                    dve.wait_ge(var_ready, grp)
                    dve.wait_ge(shift_ready, grp)
                    moments(dve, grp, stat_chain, [x[:, j, :] for j in range(J)], stats, mv, spot)
                    stat_chain.end()

                def make_shift(i, b):
                    grp = RING * i + b
                    dve.wait_ge(rstd_ready, grp + 1)
                    dve.scalar_tensor_tensor(out=shift[:, b % 2, :], in0=mv[:, :, 0], scalar=-1.0,
                                             in1=rstd[:, b % 2, :], op0=ALU.mult, op1=ALU.mult
                                             ).then_inc(shift_ready, 1)

                def mix(i, b):
                    dve.wait_ge(normed, RING * i + b + 1)
                    dve.scalar_tensor_tensor(out=h[:, b % 2, :, :], in0=h[:, b % 2, :, :], scalar=g.eps1[:, 0:1],
                                             in1=slots[2][:, b, :, :], op0=ALU.mult, op1=ALU.add
                                             ).then_inc(mixed, 1)

                def add_sums(i, b):
                    grp = RING * i + b
                    if layer == 2:
                        dve.wait_ge(mapped, grp + 1)
                        dve.tensor_tensor(pre[:, b % 2, :, :].rearrange("p (q j) c -> p q (j c)", q=2),
                                          p_map[:, :, :], slots[1][:, b, :, :].rearrange("p (q j) c -> p q (j c)", q=2),
                                          ALU.add).then_inc(pre_ready, 1)
                    else:
                        pre_chain.begin()
                        dve.wait_ge(pre_ready, grp)
                        pre_chain.done(dve.tensor_scalar(inv[:, :], slots[1][:, b, :, D], 1e-30, None, ALU.max))
                        pre_chain.wait(dve, grp)
                        pre_chain.done(dve.reciprocal(inv[:, :], inv[:, :]))
                        pre_chain.wait(dve, grp)
                        pre_chain.end()
                        dve.wait_ge(mapped, grp + 1)
                        for j in range(J):
                            ins = dve.scalar_tensor_tensor(out=pre[:, b % 2, j, :], in0=slots[1][:, b, j, 0:D],
                                                           scalar=inv[:, j:j + 1],
                                                           in1=p_map[:, b % 2, j * P:(j + 1) * P], op0=ALU.mult,
                                                           op1=ALU.add)
                        ins.then_inc(pre_ready, 1)

                def finish(i, b):
                    grp = RING * i + b
                    dve.wait_ge(stored[b], 16 * i)
                    dve.wait_ge(base_ready, grp + 1)
                    dve.wait_ge(projected, grp + 1)
                    dve.tensor_tensor(done[:, b, :, :], p_out[:, b % 2, :].rearrange("p (j c) -> p j c", j=J),
                                      base[:, b, :, :], ALU.add).then_inc(out_ready, 1)

                if layer == 1:
                    stages = [(2, mix), (1, moment), (0, elu), (1, make_shift), (4, finish)]
                else:
                    stages = [(0, moment), (4, finish), (2, add_sums), (0, make_shift)]
                pipeline(dve, NODE_GROUPS, stages)

            @block.tensor
            def _(pe):
                def turn(i, b):
                    grp = RING * i + b
                    pe.wait_ge(h_made, grp + 1)
                    pe.wait_ge(h_copied, grp)
                    for j in range(J):
                        ins = pe.transpose(p_turned[:, 0, j * P:(j + 1) * P], h[:, b % 2, j, :], g.ident[:, :])
                    ins.then_inc(h_turned, 1)

                def first_map(i, b):
                    grp = RING * i + b
                    pe.wait_ge(h_copied, grp + 1)
                    if layer == 1:
                        pe.wait_ge(mid_ready, chunks * grp)
                        for f in range(2):
                            ins = pe.matmul(p_map[:, f, :], g.Wm1[:, f * P:(f + 1) * P], hT[:, b % 2, :], start=True,
                                            stop=True)
                    else:
                        pe.wait_ge(pre_ready, grp)
                        for j in range(J):
                            if layer == 2:
                                bank, at, W = j // 2, (j % 2) * 2 * D, g.nW1a
                            else:
                                bank, at, W = b % 2, j * D, g.Wtop
                            n = W.shape[1]
                            ins = pe.matmul(p_map[:, bank, at:at + n], hT[:, b % 2, j * P:(j + 1) * P], W[:, :],
                                            start=True, stop=True)
                    ins.then_inc(mapped, 1)

                def turn_hidden(i, b):
                    grp = RING * i + b
                    pe.wait_ge(pre_ready, grp + 1)
                    pe.wait_ge(mid_ready, chunks * grp)
                    for f in range(chunks):
                        for j in range(J):
                            ins = pe.transpose(p_mid[:, f, j * P:(j + 1) * P], pre[:, b % 2, j, f * P:(f + 1) * P],
                                               g.ident[:, :])
                    ins.then_inc(mid_turned, 1)

                def project(i, b):
                    grp = RING * i + b
                    pe.wait_ge(mid_ready, chunks * (grp + 1))
                    if beyond(i, b, 2):
                        pe.wait_ge(out_ready, grp - 1)
                    for j in range(J):
                        for f in range(chunks):
                            W2 = {1: g.Wm2[:, f, :], 2: g.nW2[:, f, :], 3: g.dec[:, :]}[layer]
                            ins = pe.matmul(p_out[:, b % 2, j * P:(j + 1) * P],
                                            mid[:, b % 2, f, j * P:(j + 1) * P], W2, start=(f == 0),
                                            stop=(f == chunks - 1))
                    ins.then_inc(projected, 1)

                if layer == 1:
                    stages = [(4, project), (3, first_map), (2, turn)]
                else:
                    stages = [(4, project), (2, first_map), (3, turn_hidden), (1, turn)]
                pipeline(pe, NODE_GROUPS, stages, peeled=2)

            @block.scalar
            def _(act):
                act.preload_act_table_set("silu_and_others" if layer == 2 else "exp_and_others")

                def exps(i, b):
                    act.wait_ge(arg_ready, RING * i + b + 1)
                    act.activation(exp_arg[:, :, :], exp_arg[:, :, :], ACT.Exp).then_inc(exp_ready, 1)

                def norm(i, b):
                    grp = RING * i + b
                    act.wait_ge(shift_ready, grp + 1)
                    if beyond(i, b, 2):
                        act.wait_ge(h_turned, grp - 1)
                    for j in range(J):
                        ins = act.activation(h[:, b % 2, j, :], slots[0][:, b, j, :], ACT.Relu,
                                             bias=shift[:, b % 2, j:j + 1], scale=rstd[:, b % 2, j:j + 1])
                    ins.then_inc(normed, 1)

                def copy(i, b):
                    grp = RING * i + b
                    act.wait_ge(h_turned, grp + 1)
                    if beyond(i, b, 2):
                        act.wait_ge(mapped, grp - 1)
                    act.activation(hT[:, b % 2, :], p_turned[:, 0, :], ACT.Copy).then_inc(h_copied, 1)

                def hidden(i, b):
                    grp = RING * i + b
                    act.wait_ge(mapped if layer == 1 else mid_turned, grp + 1)
                    if beyond(i, b, 2):
                        act.wait_ge(projected, grp - 1)
                    for f in range(chunks):
                        if layer == 1:
                            ins = act.activation(mid[:, b % 2, f, :], p_map[:, f, :], ACT.Relu, bias=g.c1[:, f:f + 1],
                                                 scale=g.s1[:, f:f + 1])
                        elif layer == 2:
                            ins = act.activation(mid[:, b % 2, f, :], p_mid[:, f, :], ACT.Silu,
                                                 bias=g.nb1[:, f:f + 1])
                        else:
                            ins = act.activation(mid[:, b % 2, f, :], p_mid[:, f, :], ACT.Relu, bias=g.btop[:, 0:1])
                        ins.then_inc(mid_ready, 1)

                if layer == 1:
                    stages = [(3, hidden), (2, copy), (0, exps), (1, norm)]
                else:
                    stages = [(3, hidden), (1, copy), (0, norm)]
                pipeline(act, NODE_GROUPS, stages)


def kernel(**inputs):
    import concourse.bacc as bacc
    import numpy as np
    from concourse.bass_utils import run_bass_kernel_spmd as run

    nc = bacc.Bacc("TRN2", target_bir_lowering=False, num_devices=1)
    arrays, args = {}, {}
    for name, value in inputs.items():
        value = np.ascontiguousarray(value)
        arrays[f"in_{name}"] = value
        args[name] = nc.dram_tensor(f"in_{name}", value.shape, mybir.dt.from_np(value.dtype),
                                    kind="ExternalInput").ap()
    out = nc.dram_tensor("out_x", (N, D), F32, kind="ExternalOutput").ap()
    build(nc, args, out)
    return run(nc, [arrays], core_ids=[0]).results[0]["out_x"]
```

```python
from contextlib import ExitStack

import concourse.bass as bass
from concourse import mybir

F32 = mybir.dt.float32
I32 = mybir.dt.int32
ALU = mybir.AluOpType
ACT = mybir.ActivationFunctionType
AXX = mybir.AxisListType.X

P = 128
D = 128
N = 50000
E = 25000
J = 4
RING = 4
GROUP = P * J
NODE_GROUPS = -(-N // GROUP)
NPAD = NODE_GROUPS * GROUP
SPARE = NPAD
ROWS = NPAD + P
LAST_P = (N - (NODE_GROUPS - 1) * GROUP) // J
ET = -(-E // GROUP) * J
EDGE_GROUPS = ET // J
FULL_P = E // ET
REST = E - FULL_P * ET
LN_EPS = 1e-5
MAGIC = 1597463007.0
NEWTON = 3
FIRST_CHUNKS = 9
CHUNKS = (EDGE_GROUPS - 1) * J


class Parts:
    pass


def column(ap):
    return ap.rearrange("(k o) -> k o", o=1)


def columns(ap):
    return ap.rearrange("(c k) -> k c", k=P)


def spread(ap):
    return ap.rearrange("(o n) -> o n", o=1).partition_broadcast(P)


class Chain:

    def __init__(self, sem, steps):
        self.sem, self.steps, self.k = sem, steps, 0

    def begin(self):
        self.k = 0

    def done(self, ins):
        self.k += 1
        assert self.k <= self.steps
        ins.then_inc(self.sem, 1)

    def wait(self, eng, g):
        eng.wait_ge(self.sem, g * self.steps + self.k)

    def before(self, eng, i, b):
        if beyond(i, b, 1):
            eng.wait_ge(self.sem, (RING * i + b) * self.steps)

    def end(self):
        assert self.k == self.steps, (self.k, self.steps)


def pipeline(eng, groups, stages):
    def turn(i, c):
        for lag, function in stages:
            back, b = divmod(c - lag, RING)
            if isinstance(i, int) and not 0 <= RING * (i + back) + b < groups:
                continue
            function(i + back, b)

    for t in range(2 * RING):
        turn(t // RING, t % RING)
    with eng.Fori(2, groups // RING) as i:
        for c in range(RING):
            turn(i, c)
    for t in range(groups // RING * RING, groups + max(lag for lag, _ in stages)):
        turn(t // RING, t % RING)


def two_before(i, b):
    return (i, b - 2) if b >= 2 else (i - 1, b - 2 + RING)


def one_behind(i, b):
    return (i, b + 1) if b < RING - 1 else (i + 1, 0)


def beyond(i, b, count):
    return not isinstance(i, int) or RING * i + b >= count


def rsqrt_in_steps(dve, g, chain, v, y, t):
    chain.done(dve.tensor_scalar(y.bitcast(I32), v.bitcast(I32), 1, None, ALU.logical_shift_right))
    yield
    chain.wait(dve, g)
    chain.done(dve.tensor_scalar(y.bitcast(I32), y.bitcast(I32), -1.0, MAGIC, ALU.mult, ALU.add))
    yield
    for _ in range(NEWTON):
        chain.wait(dve, g)
        chain.done(dve.scalar_tensor_tensor(out=t, in0=y, scalar=-0.5, in1=v, op0=ALU.mult, op1=ALU.mult))
        yield
        chain.wait(dve, g)
        chain.done(dve.tensor_tensor(t, t, y, ALU.mult))
        yield
        chain.wait(dve, g)
        chain.done(dve.scalar_tensor_tensor(out=y, in0=t, scalar=1.5, in1=y, op0=ALU.add, op1=ALU.mult))
        yield


RSQRT_STEPS = 2 + 3 * NEWTON


def moments(dve, g, chain, tiles, stats, mv, spot, between=iter(())):
    for k, x in enumerate(tiles):
        ins = dve.bn_stats(stats[:, k, :], x)
        if k == len(tiles) - 1:
            chain.done(ins)
        next(between, None)
    chain.wait(dve, g)
    dve.memset(spot, 0.0)
    for k in range(len(tiles)):
        ins = dve.bn_aggr(mv[:, k, :], stats[:, k, :])
        if k < len(tiles) - 1:
            next(between, None)
    chain.done(ins)
    chain.wait(dve, g)


NORM_STEPS = 2 + 1 + RSQRT_STEPS


def norm_factors(dve, i, b, chain, tiles, w, normed, shift_ready, between=iter(())):
    grp = RING * i + b
    n = len(tiles)
    moments(dve, grp, chain, tiles, w.stats, w.mv, w.spot)
    roots_of_variances(dve, i, b, chain, n, w, normed, shift_ready, between)


def roots_of_variances(dve, i, b, chain, n, w, normed, shift_ready, between=iter(())):
    grp = RING * i + b
    chain.done(dve.tensor_scalar(w.var[:, 0:n], w.mv[:, 0:n, 1], LN_EPS, None, ALU.add))
    chain.wait(dve, grp)
    if beyond(i, b, 1):
        dve.wait_ge(normed, grp)
    for _ in rsqrt_in_steps(dve, grp, chain, w.var[:, 0:n], w.rstd[:, 0:n], w.tmp[:, 0:n]):
        next(between, None)
    chain.wait(dve, grp)
    dve.scalar_tensor_tensor(out=w.shift[:, 0:n], in0=w.mv[:, 0:n, 0], scalar=-1.0, in1=w.rstd[:, 0:n],
                             op0=ALU.mult, op1=ALU.mult).then_inc(shift_ready, 1)
    for _ in between:
        pass


def chained(*works):
    for work in works:
        yield from work


def norm_relu(act, tiles, w):
    for k, x in enumerate(tiles):
        ins = act.activation(x, x, ACT.Relu, bias=w.shift[:, k:k + 1], scale=w.rstd[:, k:k + 1])
    return ins


def norm_space(sb, n):
    q = Parts()
    q.stats = sb("stats", [P, n, 6])
    q.mv = sb("mv", [P, n, 2])
    q.var = sb("var", [P, n])
    q.rstd = sb("rstd", [P, n])
    q.tmp = sb("tmp", [P, n])
    q.shift = sb("shift", [P, n])
    q.spot = sb("spot", [P, 1])[0:1, 0:1]
    return q


def build(nc, a, out):
    with ExitStack() as whole:
        def keep(name, shape, dt=F32):
            return whole.enter_context(nc.sbuf_tensor(name, shape, dt))

        def table(name, rows, width):
            return nc.dram_tensor(name, (rows, width), F32, kind="Internal").ap()

        g = Parts()
        g.T = [table(f"sums{k}", ROWS, w) for k, w in enumerate((D + 1, D, 2 * D, D + 1))]
        g.key_rows = table("key_rows", ET, P)
        g.ew_rows = table("ew_rows", ET, P)
        g.xs = table("x_src", EDGE_GROUPS * P, J * D)
        g.X = [a["x"], None, table("x2", NPAD, D), table("x3", NPAD, D)]
        g.ident = keep("ident", [P, P])
        g.before = keep("before", [P, P])
        g.src = keep("src_key", [P, ET])
        g.dst = keep("dst_key", [P, ET])
        g.src_row = keep("src_row", [P, ET])
        g.spare = keep("spare", [P, 1])
        g.ew = keep("ew", [P, ET])
        g.ef = keep("ef", [P, ET * 16])
        g.zeros = keep("zeros", [P, zero_chunks(g.T[0], FIRST_CHUNKS)[1]])
        g.Wv = keep("Wv", [P, D + 1])
        g.v1 = keep("v1", [P, D])
        g.WE = keep("WE", [17, D])
        g.Wm1 = keep("Wm1", [P, 2 * D])
        g.s1 = keep("s1", [P, 2])
        g.c1 = keep("c1", [P, 2])
        g.Wm2 = keep("Wm2", [P, 2, D])
        g.c2 = keep("c2", [P, J, D])
        g.eps1 = keep("eps1", [P, 1])
        g.eW1s = keep("eW1s", [P, 2 * D])
        g.eW1d = keep("eW1d", [P, 2 * D])
        g.eW1w = keep("eW1w", [P, 2])
        g.eb1 = keep("eb1", [P, 2])
        g.eb2 = keep("eb2", [P, 2])
        g.eW2 = keep("eW2", [P, 2, 2 * D])
        g.nW1a = keep("nW1a", [P, 2 * D])
        g.nW1b = keep("nW1b", [P, 2, 2 * D])
        g.nb1 = keep("nb1", [P, 2])
        g.nW2 = keep("nW2", [P, 2, D])
        g.nb2 = keep("nb2", [P, J, D])
        g.Wsig = keep("Wsig", [P, 16])
        g.bsig = keep("bsig", [P, 8, 16])
        g.Wmsg = keep("Wmsg", [P, D])
        g.bmsg = keep("bmsg", [P, 1])
        g.Wtop = keep("Wtop", [P, D])
        g.btop = keep("btop", [P, 1])
        g.Wbot = keep("Wbot", [P, D])
        g.dec = keep("dec", [P, D])
        g.decb = keep("decb", [P, J, D])
        g.by_tile = keep("by_tile", [P, 2, 2, P])
        g.tiles_stored = whole.enter_context(nc.semaphore("tiles_stored"))
        g.zeroed = [whole.enter_context(nc.semaphore(f"zeroed{k}")) for k in range(4)]
        prepare(nc, a, g)
        edges0(nc, g)
        edges1(nc, g)
        nodes(nc, g, 1, None)
        edges2(nc, g)
        nodes(nc, g, 2, None)
        edges3(nc, g)
        nodes(nc, g, 3, out)


def zero_chunks(t, count):
    v = t.rearrange("(p r) d -> p (r d)", p=P)
    n = v.shape[1] // count
    return v, n, v.shape[1] - n * count


def zero_first(sp, g):
    v, n, rest = zero_chunks(g.T[0], FIRST_CHUNKS)
    assert rest == 0
    with sp.Fori(0, FIRST_CHUNKS) as i:
        sp.dma_start(v[:, bass.ds(i * n, n)], g.zeros[:, 0:n]).then_inc(g.zeroed[0], 16)


def zero_along(sp, s, g, k):
    v, n, rest = zero_chunks(g.T[k], CHUNKS)
    if rest:
        sp.dma_start(v[:, CHUNKS * n:CHUNKS * n + rest], g.zeros[:, 0:rest]).then_inc(g.zeroed[k], 16)

    def of_group(i, b):
        grp = RING * i + b
        if isinstance(i, int) and grp >= CHUNKS // J:
            return
        for j in range(J):
            sp.wait_ge(s.scattered, grp * (16 * J) + 16 * (j + 1))
            sp.dma_start(v[:, bass.ds((grp * J + j) * n, n)], g.zeros[:, 0:n]).then_inc(g.zeroed[k], 16)
    return of_group


def all_zeroed(eng, g, k):
    eng.wait_ge(g.zeroed[k], 16 * (FIRST_CHUNKS if k == 0 else CHUNKS + (zero_chunks(g.T[k], CHUNKS)[2] > 0)))


def prepare(nc, a, g):
    with ExitStack() as ctx:
        sb, sem, ps = makers(nc, ctx, "prepare")
        raw = [sb("raw_src", [P, ET], I32), sb("raw_dst", [P, ET], I32)]
        part = sb("part", [P, 1], I32)
        one_row = sb("one_row", [1, 17])
        ones = sb("ones", [P, P])
        W = sb("W", [P, P])
        a12 = sb("a12", [P, 2])
        a1s = sb("a1s", [P, P])
        We1 = sb("We1", [16, 2 * D])
        We1T = sb("We1T", [P, 2, 17])
        We2 = sb("We2", [P, 2, D])
        be1 = sb("be1", [P, 2])
        be2 = sb("be2", [1, D])
        bn1 = sb("bn1", [P, 5, 2])
        bn2 = sb("bn2", [P, 5, D])
        var = sb("var", [P, 2 + D])
        scale = sb("scale", [P, 2 + D])
        tmp = sb("root_tmp", [P, 2 + D])
        c2 = sb("c2row", [P, D])
        enc = sb("enc", [P, D])
        encT = sb("encT", [P, D])
        encb = sb("encb", [P, 1])
        encbs = sb("encbs", [P, P])
        sigw = sb("sigw", [P, 16])
        sigb = sb("sigb", [P, 16])
        msgw = sb("msgw", [P, D])
        msgb = sb("msgb", [P, 1])
        aggt = sb("aggt", [P, D])
        aggb = sb("aggb", [P, 1])
        by_tile = g.by_tile
        pT, p1, p2, p3 = (ps(n, 1)[:, 0, :] for n in ("p_turned", "p_first", "p_second", "p_by_tile"))

        cleared, loaded, consts, turned, copied = (sem(n) for n in (
            "cleared", "weights_loaded", "consts_ready", "turned", "turned_copied"))
        product, vec = sem("products_ready"), sem("vec_step")
        graph, zeros_set = sem("graph_loaded"), sem("zeros_set")
        keys_ready, tiles_turned, tiles_copied = (sem(n) for n in ("keys_ready", "tiles_turned", "tiles_copied"))

        loads = [
            (W[:, :], a["L0_gnn_W"]), (a12[:, :], columns(a["L0_gnn_a"].rearrange("n o -> (n o)"))),
            (We1[:, :], a["L1_gnn_We1"]), (We2[:, :, :], a["L1_gnn_We2"].rearrange("(c k) n -> k c n", k=P)),
            (be1[:, :], columns(a["L1_gnn_be1"])), (be2[:, :], a["L1_gnn_be2"].rearrange("(o n) -> o n", o=1)),
            (g.eps1[:, :], spread(a["L1_gnn_eps"])), (g.Wm1[:, :], a["L1_gnn_Wm1"]),
            (g.Wm2[:, :, :], a["L1_gnn_Wm2"].rearrange("(c k) n -> k c n", k=P)),
            (g.eW1s[:, :], a["L2_gnn_eW1"][0:P, :]), (g.eW1d[:, :], a["L2_gnn_eW1"][P:2 * P, :]),
            (g.eW1w[:, :], columns(a["L2_gnn_eW1"][2 * P:2 * P + 1, :].rearrange("o n -> (o n)"))),
            (g.eb1[:, :], columns(a["L2_gnn_eb1"])), (g.eb2[:, :], columns(a["L2_gnn_eb2"])),
            (g.eW2[:, :, :], a["L2_gnn_eW2"].rearrange("(c k) n -> k c n", k=P)),
            (g.nW1a[:, :], a["L2_gnn_nW1"][0:P, :]),
            (g.nW1b[:, :, :], a["L2_gnn_nW1"][P:3 * P, :].rearrange("(c k) n -> k c n", k=P)),
            (g.nb1[:, :], columns(a["L2_gnn_nb1"])),
            (g.nW2[:, :, :], a["L2_gnn_nW2"].rearrange("(c k) n -> k c n", k=P)),
            (enc[:, :], a["L3_gnn_enc_w"]), (encb[:, :], column(a["L3_gnn_enc_b"])),
            (sigw[:, :], a["L3_gnn_sig_w"]), (sigb[:, :], spread(a["L3_gnn_sig_b"])),
            (msgw[:, :], a["L3_gnn_msg_w"]), (msgb[:, :], column(a["L3_gnn_msg_b"])),
            (aggt[:, :], a["L3_gnn_agg_w"][0:P, :]), (g.Wbot[:, :], a["L3_gnn_agg_w"][P:2 * P, :]),
            (aggb[:, :], column(a["L3_gnn_agg_b"])), (g.dec[:, :], a["L3_gnn_dec_w"]),
        ]
        loads += [(bn1[:, k, :], columns(a["L1_gnn_" + n])) for k, n in enumerate(("g1", "b1", "m1", "v1", "bm1"))]
        loads += [(bn2[:, k, :], spread(a["L1_gnn_" + n])) for k, n in enumerate(("g2", "b2", "m2", "v2", "bm2"))]
        for j in range(J):
            loads += [(g.nb2[:, j, :], spread(a["L2_gnn_nb2"])), (g.decb[:, j, :], spread(a["L3_gnn_dec_b"]))]
        graph_loads = []
        for to, of in ((raw[0], a["src"]), (raw[1], a["dst"]), (g.ew, a["edge_weight1"].rearrange("e o -> (e o)"))):
            graph_loads += [(to[0:FULL_P, :], of[0:FULL_P * ET].rearrange("(p t) -> p t", t=ET)),
                            (to[FULL_P:FULL_P + 1, 0:REST], of[FULL_P * ET:E].rearrange("(p t) -> p t", p=1))]
        ef = a["edge_attr_16"]
        graph_loads += [(g.ef[0:FULL_P, :], ef[0:FULL_P * ET, :].rearrange("(p t) d -> p (t d)", t=ET)),
                        (g.ef[FULL_P:FULL_P + 1, 0:REST * 16],
                         ef[FULL_P * ET:E, :].rearrange("(p t) d -> p (t d)", p=1))]

        with nc.Block() as block:
            @block.sync
            def _(sp):
                sp.wait_ge(cleared, 4)
                for to, of in graph_loads:
                    sp.dma_start(to, of).then_inc(graph, 16)
                sp.wait_ge(loaded, 16 * len(loads))
                sp.wait_ge(zeros_set, 1)
                zero_first(sp, g)
                sp.wait_ge(tiles_copied, 1)
                for k, to in enumerate((g.key_rows, g.ew_rows)):
                    sp.dma_start(to[0:P, :], by_tile[:, k, 0, :]).then_inc(g.tiles_stored, 16)
                    sp.dma_start(to[P:ET, :], by_tile[0:ET - P, k, 1, :]).then_inc(g.tiles_stored, 16)

            @block.scalar
            def _(act):
                with nc.allow_non_contiguous_dma(reason="short vectors, one element per partition"):
                    for to, of in loads:
                        act.dma_start(to, of).then_inc(loaded, 16)

            @block.gpsimd
            def _(pool):
                pool.memset(g.zeros[:, :], 0.0).then_inc(zeros_set, 1)
                pool.memset(raw[0][:, :], SPARE + FULL_P).then_inc(cleared, 1)
                pool.memset(raw[1][:, :], SPARE + FULL_P).then_inc(cleared, 1)
                pool.memset(g.ew[:, :], 0.0).then_inc(cleared, 1)
                pool.memset(g.ef[:, :], 0.0).then_inc(cleared, 1)
                pool.memset(g.ident[:, :], 0.0).then_inc(consts, 1)
                pool.memset(g.before[:, :], 1.0).then_inc(consts, 1)
                pool.iota(part[:, :], [[0, 1]], base=0, channel_multiplier=1)
                pool.wait_ge(consts, 2)
                pool.affine_select(out=g.ident[:, :], in_=g.ident[:, :], compare_op=ALU.not_equal, fill=1.0,
                                   base=0, pattern=[[-1, P]], channel_multiplier=1)
                pool.affine_select(out=g.before[:, :], in_=g.before[:, :], compare_op=ALU.is_gt, fill=0.0,
                                   base=0, pattern=[[-1, P]], channel_multiplier=1).then_inc(consts, 1)
                pool.memset(one_row[:, :], 0.0).then_inc(consts, 1)
                pool.wait_ge(consts, 4)
                pool.memset(one_row[:, 16:17], 1.0).then_inc(consts, 1)

            @block.tensor
            def _(pe):
                pe.wait_ge(consts, 5)
                pe.wait_ge(loaded, 16 * len(loads))
                pe.transpose(pT[:, 0:128], W[:, :], g.ident[:, :])
                pe.transpose(pT[:, 128:256], enc[:, :], g.ident[:, :])
                for c in range(2):
                    ins = pe.transpose(pT[:, 256 + 16 * c:272 + 16 * c], We1[:, c * P:(c + 1) * P],
                                       g.ident[0:16, 0:16])
                ins.then_inc(turned, 1)
                pe.wait_ge(copied, 1)
                pe.matmul(p1[:, 0:128], a1s[:, :], W[:, :], start=True, stop=True)
                pe.matmul(p1[:, 128:129], W[:, :], a12[:, 1:2], start=True, stop=True)
                pe.matmul(p1[0:17, 129:257], We1T[:, 0, :], We2[:, 0, :], start=True, stop=False)
                pe.matmul(p1[0:17, 129:257], We1T[:, 1, :], We2[:, 1, :], start=False, stop=False)
                pe.matmul(p1[0:17, 129:257], one_row[:, :], be2[:, :], start=False, stop=True)
                pe.matmul(p2[:, 0:128], encT[:, :], msgw[:, :], start=True, stop=True)
                pe.matmul(p2[:, 128:256], encT[:, :], aggt[:, :], start=True, stop=True)
                pe.matmul(p2[:, 256:272], encT[:, :], sigw[:, :], start=True, stop=True)
                pe.matmul(p2[:, 272:288], encbs[:, :], sigw[:, :], start=True, stop=True)
                pe.matmul(p2[:, 288:289], msgw[:, :], encb[:, :], start=True, stop=True)
                pe.matmul(p2[:, 289:290], aggt[:, :], encb[:, :], start=True, stop=True).then_inc(product, 1)
                pe.wait_ge(keys_ready, 2)
                pe.wait_ge(graph, 16 * len(graph_loads))
                for k, of in enumerate((g.src, g.ew)):
                    pe.transpose(p3[:, k * P:(k + 1) * P], of[:, 0:P], g.ident[:, :])
                    ins = pe.transpose(p3[0:ET - P, (2 + k) * P:(3 + k) * P], of[:, P:ET], g.ident[:, :])
                ins.then_inc(tiles_turned, 1)

            @block.vector
            def _(dve):
                link = Chain(vec, 99)
                dve.wait_ge(loaded, 16 * len(loads))
                dve.tensor_scalar(var[:, 0:2], bn1[:, 3, :], 1e-3, None, ALU.add)
                link.done(dve.tensor_scalar(var[:, 2:2 + D], bn2[:, 3, :], 1e-3, None, ALU.add))
                dve.tensor_scalar(g.eps1[:, :], g.eps1[:, :], 1.0, None, ALU.add)
                link.done(dve.memset(ones[:, :], 1.0))
                link.wait(dve, 0)
                dve.tensor_scalar(a1s[:, :], ones[:, :], a12[:, 0:1], None, ALU.mult)
                dve.tensor_scalar(encbs[:, :], ones[:, :], encb[:, 0:1], None, ALU.mult)
                dve.wait_ge(turned, 1)
                dve.tensor_copy(g.Wv[:, 0:D], pT[:, 0:128])
                dve.tensor_copy(encT[:, :], pT[:, 128:256])
                for c in range(2):
                    dve.tensor_copy(We1T[:, c, 0:16], pT[:, 256 + 16 * c:272 + 16 * c])
                    ins = dve.tensor_copy(We1T[:, c, 16:17], be1[:, c:c + 1])
                ins.then_inc(copied, 1)
                dve.wait_ge(graph, 16 * len(graph_loads))
                dve.wait_ge(consts, 5)
                link.done(dve.tensor_copy(g.spare[:, :], part[:, :]))
                link.wait(dve, 0)
                link.done(dve.tensor_scalar(g.spare[:, :], g.spare[:, :], float(SPARE), None, ALU.add))
                for key, ids in ((g.src, raw[0]), (g.dst, raw[1])):
                    dve.tensor_copy(key[:, :], ids[:, :]).then_inc(keys_ready, 1)
                for _ in rsqrt_in_steps(dve, 0, link, var[:, :], scale[:, :], tmp[:, :]):
                    pass
                link.wait(dve, 0)
                for col, bn, s, c in ((0, bn1, g.s1, g.c1), (2, bn2, bn2[:, 3, :], c2)):
                    w = 2 if col == 0 else D
                    s = s[:, 0:w]
                    link.done(dve.tensor_tensor(s, scale[:, col:col + w], bn[:, 0, :], ALU.mult))
                    link.done(dve.tensor_tensor(bn[:, 4, :], bn[:, 4, :], bn[:, 2, :], ALU.subtract))
                    link.wait(dve, 0)
                    link.done(dve.tensor_tensor(bn[:, 4, :], bn[:, 4, :], s, ALU.mult))
                    link.wait(dve, 0)
                    link.done(dve.tensor_tensor(c[:, 0:w], bn[:, 4, :], bn[:, 1, :], ALU.add))
                    link.wait(dve, 0)
                for c in range(2):
                    dve.tensor_tensor(g.Wm2[:, c, :], g.Wm2[:, c, :], bn2[:, 3, :], ALU.mult)
                for j in range(J):
                    dve.tensor_copy(g.c2[:, j, :], c2[:, :])
                dve.wait_ge(product, 1)
                dve.tensor_copy(g.v1[:, :], p1[:, 0:128])
                dve.tensor_copy(g.Wv[:, D:D + 1], p1[:, 128:129])
                dve.tensor_copy(g.WE[:, :], p1[0:17, 129:257])
                dve.tensor_copy(g.Wmsg[:, :], p2[:, 0:128])
                dve.tensor_copy(g.Wtop[:, :], p2[:, 128:256])
                dve.tensor_copy(g.Wsig[:, :], p2[:, 256:272])
                for k in range(8):
                    dve.tensor_tensor(g.bsig[:, k, :], p2[:, 272:288], sigb[:, :], ALU.add)
                dve.tensor_tensor(g.bmsg[:, :], p2[:, 288:289], msgb[:, :], ALU.add)
                dve.tensor_tensor(g.btop[:, :], p2[:, 289:290], aggb[:, :], ALU.add)
                dve.wait_ge(tiles_turned, 1)
                dve.tensor_copy(by_tile[:, :, 0, :], p3[:, 0:2 * P].rearrange("p (k c) -> p k c", k=2))
                dve.tensor_copy(by_tile[0:ET - P, :, 1, :], p3[0:ET - P, 2 * P:4 * P].rearrange(
                    "p (k c) -> p k c", k=2)).then_inc(tiles_copied, 1)


def makers(nc, ctx, phase):
    def sb(name, shape, dt=F32):
        return ctx.enter_context(nc.sbuf_tensor(f"{phase}_{name}", shape, dt))

    sems = []

    def sem(name):
        sems.append(nc.alloc_semaphore(f"{phase}_{name}"))
        return sems[-1]

    def clear():
        nc.clear_and_free_semaphores(sems)
        nc.all_engine_barrier()

    ctx.callback(clear)

    def ps(name, banks):
        return ctx.enter_context(nc.psum_tensor(f"{phase}_{name}", [P, banks, 512], F32))

    return sb, sem, ps


def edge_space(nc, ctx, phase, gathers, width):
    sb, sem, ps = makers(nc, ctx, phase)
    q = Parts()
    q.phase = phase
    q.sb = sb
    q.sem = sem
    q.ps = ps
    q.gathers = gathers
    q.rows = [sb(f"rows{k}", [P, RING, J, t.shape[1]]) for k, (t, _) in enumerate(gathers)]
    q.index = [sb(f"index{k}", [P, RING, J], I32) for k, _ in enumerate(gathers)]
    q.key = sb("key", [P, 2, J])
    q.to = sb("scatter_to", [P, RING, J], I32)
    q.total = sb("total", [P, RING, J, width])
    q.equal = sb("equal", [P, 2, J, P])
    q.staged = sem("indices_staged")
    q.gathered = [sem(f"gathered{b}") for b in range(RING)]
    q.scattered = sem("scattered")
    q.key_ready = sem("key_ready")
    q.keys_across = sem("keys_across")
    q.equal_ready = sem("equal_ready")
    q.summed = sem("summed")
    q.total_ready = sem("total_ready")
    q.settled = sem("settled")
    q.to_ready = sem("scatter_rows_ready")
    return q


def pool_edges(pool, s, g_, layer, used):
    table = g_.T[layer]

    def settle():
        pool.sem_inc(s.settled, 1)

    def gather(j):
        def of_group(i, b):
            if j == 0:
                pool.wait_ge(s.staged, RING * i + b + 1)
                if beyond(i, b, RING):
                    for rows_read in used:
                        pool.wait_ge(rows_read, RING * (i - 1) + b + 1)
                settle()
            for (of, _), rows, index in zip(s.gathers, s.rows, s.index):
                pool.indirect_dma_start(rows[:, b, j, :], None, of[:, :],
                                        bass.IndirectOffsetOnAxis(ap=index[:, b, j:j + 1], axis=0)
                                        ).then_inc(s.gathered[b], 16)
        return of_group

    def scatter(j):
        def of_group(i, b):
            grp = RING * i + b
            if j or beyond(i, b, 1):
                pool.wait_ge(s.scattered, grp * (16 * J) + 16 * j)
            else:
                all_zeroed(pool, g_, layer)
            if j == 0:
                pool.wait_ge(s.to_ready, grp + 1)
                pool.wait_ge(s.total_ready, grp + 1)
            settle()
            pool.indirect_dma_start(table[:, :], bass.IndirectOffsetOnAxis(ap=s.to[:, b, j:j + 1], axis=0),
                                    s.total[:, b, j, :], None, compute_op=ALU.add).then_inc(s.scattered, 16)
        return of_group

    stages = []
    for j in range(J):
        stages += [(0, gather(j)), (4, scatter(j))]
    pipeline(pool, EDGE_GROUPS, stages)
    pool.wait_ge(s.scattered, 16 * J * EDGE_GROUPS)


def stage_index(dve, s):
    def of_group(i, b):
        if beyond(i, b, RING):
            dve.wait_ge(s.gathered[b], (16 * J * len(s.gathers)) * i)
        for (_, keys), index in zip(s.gathers, s.index):
            ins = dve.tensor_scalar(index[:, b, :], keys[:, bass.ds((RING * i + b) * J, J)], float(N - 1), None,
                                    ALU.min)
        ins.then_inc(s.staged, 1)
    return of_group


def arrived(eng, s, i, b):
    eng.wait_ge(s.gathered[b], (16 * J * len(s.gathers)) * (i + 1))


def stage_key(dve, s, keys, turned=True):
    def of_group(i, b):
        if beyond(i, b, 2):
            dve.wait_ge(s.equal_ready, RING * i + b - 1)
            if turned:
                dve.wait_ge(s.keys_across, RING * i + b - 1)
            dve.wait_ge(s.to_ready, RING * i + b - 1)
        dve.tensor_scalar(s.key[:, b % 2, :], keys[:, bass.ds((RING * i + b) * J, J)], 0.0, None,
                          ALU.add).then_inc(s.key_ready, 1)
    return of_group


def key_rows(pe, s, g_, across):
    def of_group(i, b):
        grp = RING * i + b
        pe.wait_ge(s.key_ready, grp + 1)
        if beyond(i, b, 1):
            pe.wait_ge(s.equal_ready, grp)
            pe.wait_ge(s.to_ready, grp)
        for j in range(J):
            ins = pe.transpose(across[:, 0, j * P:(j + 1) * P], s.key[:, b % 2, j:j + 1].to_broadcast([P, P]),
                               g_.ident[:, :])
        ins.then_inc(s.keys_across, 1)
    return of_group


def first_rows_in_steps(dve, s, g_, across, w, chain, keep=None):
    def of_group(i, b):
        grp = RING * i + b
        chain.before(dve, i, b)
        chain.begin()
        dve.wait_ge(s.key_ready, grp + 1)
        dve.wait_ge(s.keys_across, grp + 1)
        for j in range(J):
            ins = dve.scalar_tensor_tensor(out=w.junk[:, j, :], in0=across[:, 0, j * P:(j + 1) * P],
                                           scalar=s.key[:, b % 2, j:j + 1], in1=g_.before[:, :], op0=ALU.is_equal,
                                           op1=ALU.mult, accum_out=w.rank[:, j:j + 1])
            if j == J - 1:
                chain.done(ins)
            yield
        chain.wait(dve, grp)
        chain.done(dve.tensor_scalar(w.first[:, :], w.rank[:, :], 0.5, None, ALU.is_lt))
        yield
        chain.wait(dve, grp)
        chain.done(dve.scalar_tensor_tensor(out=w.row[:, :], in0=s.key[:, b % 2, :], scalar=g_.spare[:, 0:1],
                                            in1=w.first[:, :], op0=ALU.subtract, op1=ALU.mult))
        yield
        chain.wait(dve, grp)
        chain.done(dve.tensor_scalar(w.row[:, :], w.row[:, :], g_.spare[:, 0:1], None, ALU.add))
        yield
        chain.wait(dve, grp)
        if keep is not None:
            dve.tensor_scalar(keep[:, bass.ds(grp * J, J)], w.row[:, :], 0.0, None, ALU.add)
        if beyond(i, b, RING):
            dve.wait_ge(s.scattered, (16 * J) * (RING * (i - 1) + b + 1))
        dve.tensor_copy(s.to[:, b, :], w.row[:, :]).then_inc(s.to_ready, 1)
        chain.done(dve.tensor_scalar(w.first[:, :], w.row[:, :], 0.0, None, ALU.add))
        chain.end()
    return of_group


def first_rows(dve, s, g_, across, w, chain, keep=None):
    return whole(first_rows_in_steps(dve, s, g_, across, w, chain, keep))


def whole(work):
    def of_group(i, b):
        for _ in work(i, b):
            pass
    return of_group


ROW_STEPS = 5


def row_space(sb):
    q = Parts()
    q.junk = sb("junk", [P, J, P])
    q.rank = sb("rank", [P, J])
    q.first = sb("first", [P, J])
    q.row = sb("row", [P, J])
    return q


def known_rows(dve, s, g_):
    def of_group(i, b):
        if beyond(i, b, RING):
            dve.wait_ge(s.scattered, (16 * J) * (RING * (i - 1) + b + 1))
        dve.tensor_scalar(s.to[:, b, :], g_.src_row[:, bass.ds((RING * i + b) * J, J)], 0.0, None,
                          ALU.add).then_inc(s.to_ready, 1)
    return of_group


def select_in_steps(dve, s, across, weight=None, weight_ready=None):
    def of_group(i, b):
        grp = RING * i + b
        dve.wait_ge(s.key_ready, grp + 1)
        dve.wait_ge(s.keys_across, grp + 1)
        if beyond(i, b, 2):
            dve.wait_ge(s.summed, grp - 1)
        if weight is not None:
            dve.wait_ge(weight_ready, grp + 1)
        for j in range(J):
            across_j, key_j = across[:, 0, j * P:(j + 1) * P], s.key[:, b % 2, j:j + 1]
            if weight is None:
                ins = dve.tensor_scalar(s.equal[:, b % 2, j, :], across_j, key_j, None, ALU.is_equal)
            else:
                ins = dve.tensor_scalar(s.equal[:, b % 2, j, :], across_j, key_j, weight[:, j:j + 1], ALU.is_equal,
                                        ALU.mult)
            if j == J - 1:
                ins.then_inc(s.equal_ready, 1)
            yield
    return of_group


def select(dve, s, across, weight=None, weight_ready=None):
    return whole(select_in_steps(dve, s, across, weight, weight_ready))


def width129(t, j):
    return t[:, j // 2, (j % 2) * (D + 1):(j % 2 + 1) * (D + 1)]


def halves(t, lo, hi):
    return t[:, :, 0:2 * (D + 1)].rearrange("p h (q c) -> p h q c", q=2)[:, :, :, lo:hi]


def save_total(act, s, view):
    def of_group(i, b):
        act.wait_ge(s.summed, RING * i + b + 1)
        if beyond(i, b, RING):
            act.wait_ge(s.scattered, (16 * J) * (RING * (i - 1) + b + 1))
        to, of = view(s.total[:, b, :, :])
        act.activation(to, of, ACT.Copy).then_inc(s.total_ready, 1)
    return of_group


def edges0(nc, g):
    with ExitStack() as ctx:
        s = edge_space(nc, ctx, "edges0", [(g.X[0], g.src), (g.X[0], g.dst)], D + 1)
        sb, sem = s.sb, s.sem
        w = norm_space(sb, 2 * J)
        r = row_space(sb)
        hT = sb("hT", [P, GROUP])
        score = sb("score", [P, J])
        z = sb("z", [P, J])
        ez = sb("ez", [P, J])
        alpha = sb("alpha", [P, J])
        msg = sb("msg", [P, 2, J, D + 1])
        scored_junk = sb("scored_junk", [P, J, P])
        turned, across, prod, tot = s.ps("p_turned", 1), s.ps("p_across", 1), s.ps("p_prod", 2), s.ps("p_tot", 2)
        ones_set, shift_ready, normed, h_turned, h_copied, projected, z_ready, exp_ready, alpha_ready, msg_ready, \
            scored, norm_steps, score_steps, row_steps = (
                sem(n) for n in ("ones_set", "shift_ready", "h_normed", "h_turned", "h_copied", "projected",
                                 "z_ready", "exp_ready", "alpha_ready", "messages_ready", "source_scored",
                                 "norm_steps", "score_steps", "row_steps"))

        saved = [sem(f"saved{b}") for b in range(RING)]

        with nc.Block() as block:
            @block.sync
            def _(sp):
                def save(i, b):
                    arrived(sp, s, i, b)
                    sp.dma_start(g.xs[bass.ds((RING * i + b) * P, P), :].rearrange("p (j d) -> p j d", j=J),
                                 s.rows[0][:, b, :, :]).then_inc(saved[b], 16)

                pipeline(sp, EDGE_GROUPS, [(0, save), (4, zero_along(sp, s, g, 1))])
                for b in range(RING):
                    sp.wait_ge(saved[b], 16 * len(range(b, EDGE_GROUPS, RING)))

            @block.gpsimd
            def _(pool):
                pool_edges(pool, s, g, 0, used=(scored, h_turned))

            @block.vector
            def _(dve):
                norm_chain, row_chain = Chain(norm_steps, NORM_STEPS), Chain(row_steps, ROW_STEPS)
                score_chain = Chain(score_steps, 1)
                dve.memset(msg[:, :, :, D:D + 1], 1.0).then_inc(ones_set, 1)

                def moment(i, b):
                    arrived(dve, s, i, b)
                    norm_chain.before(dve, i, b)
                    norm_chain.begin()
                    norm_factors(dve, i, b, norm_chain, [s.rows[k][:, b, j, :] for k in range(2) for j in range(J)],
                                 w, normed, shift_ready)
                    norm_chain.end()

                def add_scores(i, b):
                    grp = RING * i + b
                    dve.wait_ge(normed, grp + 1)
                    if beyond(i, b, 1):
                        dve.wait_ge(exp_ready, grp)
                        dve.wait_ge(scored, grp)
                    for j in range(J):
                        ins = dve.scalar_tensor_tensor(out=scored_junk[:, j, :], in0=s.rows[0][:, b, j, :], scalar=1.0,
                                                       in1=g.v1[:, :], op0=ALU.mult, op1=ALU.mult,
                                                       accum_out=score[:, j:j + 1])
                    ins.then_inc(scored, 1)
                    dve.wait_ge(scored, grp + 1)
                    dve.wait_ge(msg_ready, grp + 1)
                    score_chain.begin()
                    score_chain.done(dve.tensor_tensor(z[:, :].rearrange("p (h q) -> p h q", h=2),
                                                       halves(prod, D, D + 1).rearrange("p h q o -> p h (q o)"),
                                                       score[:, :].rearrange("p (h q) -> p h q", h=2), ALU.add))
                    score_chain.wait(dve, grp)
                    score_chain.end()
                    dve.scalar_tensor_tensor(out=z[:, :], in0=z[:, :], scalar=0.2, in1=z[:, :], op0=ALU.mult,
                                             op1=ALU.max).then_inc(z_ready, 1)

                def clip(i, b):
                    grp = RING * i + b
                    dve.wait_ge(exp_ready, grp + 1)
                    if beyond(i, b, 1):
                        dve.wait_ge(s.equal_ready, grp)
                    dve.tensor_scalar(alpha[:, :], ez[:, :], 5.0, -5.0, ALU.min, ALU.max).then_inc(alpha_ready, 1)

                pipeline(dve, EDGE_GROUPS, [
                    (0, stage_index(dve, s)), (3, stage_key(dve, s, g.src)), (2, moment), (3, add_scores),
                    (3, first_rows(dve, s, g, across, r, row_chain, keep=g.src_row)), (3, clip),
                    (3, select(dve, s, across, alpha, alpha_ready))])

            @block.tensor
            def _(pe):
                def turn(i, b):
                    grp = RING * i + b
                    pe.wait_ge(normed, grp + 1)
                    if beyond(i, b, 1):
                        pe.wait_ge(h_copied, grp)
                    for j in range(J):
                        ins = pe.transpose(turned[:, 0, j * P:(j + 1) * P], s.rows[1][:, b, j, :], g.ident[:, :])
                    ins.then_inc(h_turned, 1)

                def project(i, b):
                    grp = RING * i + b
                    pe.wait_ge(h_copied, grp + 1)
                    if beyond(i, b, 1):
                        pe.wait_ge(msg_ready, grp)
                        pe.wait_ge(z_ready, grp)
                    for j in range(J):
                        ins = pe.matmul(width129(prod, j), hT[:, j * P:(j + 1) * P], g.Wv[:, :], start=True, stop=True)
                    ins.then_inc(projected, 1)

                def sum_up(i, b):
                    grp = RING * i + b
                    pe.wait_ge(msg_ready, grp + 1)
                    pe.wait_ge(s.equal_ready, grp + 1)
                    if beyond(i, b, 1):
                        pe.wait_ge(s.total_ready, grp)
                    for j in range(J):
                        ins = pe.matmul(width129(tot, j), s.equal[:, b % 2, j, :], msg[:, b % 2, j, :], start=True,
                                        stop=True)
                    ins.then_inc(s.summed, 1)

                pipeline(pe, EDGE_GROUPS, [(3, turn), (3, key_rows(pe, s, g, across)), (4, sum_up), (3, project)])

            @block.scalar
            def _(act):
                act.preload_act_table_set("exp_and_others")
                act.wait_ge(ones_set, 1)

                def copy(i, b):
                    grp = RING * i + b
                    act.wait_ge(h_turned, grp + 1)
                    if beyond(i, b, 1):
                        act.wait_ge(projected, grp)
                    act.activation(hT[:, :], turned[:, 0, :], ACT.Copy).then_inc(h_copied, 1)

                def message(i, b):
                    grp = RING * i + b
                    act.wait_ge(projected, grp + 1)
                    if beyond(i, b, 2):
                        act.wait_ge(s.summed, grp - 1)
                    act.activation(msg[:, b % 2, :, 0:D].rearrange("p (h q) c -> p h q c", h=2), halves(prod, 0, D),
                                   ACT.Copy).then_inc(msg_ready, 1)

                def exps(i, b):
                    grp = RING * i + b
                    act.wait_ge(z_ready, grp + 1)
                    if beyond(i, b, 1):
                        act.wait_ge(alpha_ready, grp)
                    act.activation(ez[:, :], z[:, :], ACT.Exp, scale=-1.0).then_inc(exp_ready, 1)

                def norm(i, b):
                    act.wait_ge(shift_ready, RING * i + b + 1)
                    act.wait_ge(saved[b], 16 * (i + 1))
                    norm_relu(act, [s.rows[k][:, b, j, :] for k in range(2) for j in range(J)], w
                              ).then_inc(normed, 1)

                def view(total):
                    return total.rearrange("p (h q) c -> p h q c", h=2), halves(tot, 0, D + 1)

                pipeline(act, EDGE_GROUPS, [(3, copy), (4, save_total(act, s, view)), (3, message), (3, exps),
                                            (2, norm)])


def elu_space(sb):
    q = Parts()
    q.guard = sb("guard", [P, J])
    q.inv = sb("inv", [P, J])
    q.pos = sb("pos", [P, J, D])
    q.exp_arg = sb("exp_arg", [P, J, D])
    return q


def elu_argument(dve, grp, chain, sums, w, arg_ready):
    chain.done(dve.tensor_scalar(w.guard[:, :], sums[:, :, D], 1e-37, None, ALU.max))
    chain.wait(dve, grp)
    chain.done(dve.reciprocal(w.inv[:, :], w.guard[:, :]))
    chain.wait(dve, grp)
    for j in range(J):
        ins = dve.tensor_scalar(w.exp_arg[:, j, :], sums[:, j, 0:D], w.inv[:, j:j + 1], 0.0, ALU.mult, ALU.min)
    ins.then_inc(arg_ready, 1)


def edges1(nc, g):
    with ExitStack() as ctx:
        s = edge_space(nc, ctx, "edges1", [(g.T[0], g.src)], D)
        sb, sem = s.sb, s.sem
        x_rows = sb("x_rows", [P, RING, J, D])
        loaded = [sem(f"x_loaded{b}") for b in range(RING)]
        w = norm_space(sb, J)
        r = row_space(sb)
        el = elu_space(sb)
        exp_arg = el.exp_arg
        feat = sb("feat", [P, J * 16])
        featT = sb("featT", [17, GROUP])
        added = sb("added", [P, J, D])
        msg = sb("msg", [P, 2, J, D])
        across, turned, tot, mapped = s.ps("p_across", 1), s.ps("p_turned", 1), s.ps("p_tot", 1), s.ps("p_mapped", 2)
        ones_set, feat_ready, f_turned, f_copied, f_mapped, arg_ready, exp_ready, shift_ready, normed, add_ready, \
            msg_ready, elu_steps, norm_steps, row_steps = (
                sem(n) for n in ("ones_set", "features_staged", "features_turned", "features_copied",
                                 "features_mapped", "exp_arg_ready", "exp_ready", "shift_ready", "h_normed",
                                 "message_added", "messages_ready", "elu_steps", "norm_steps", "row_steps"))

        with nc.Block() as block:
            @block.sync
            def _(sp):
                def load(i, b):
                    if beyond(i, b, RING):
                        sp.wait_ge(add_ready, RING * (i - 1) + b + 1)
                    sp.dma_start(x_rows[:, b, :, :], g.xs[bass.ds((RING * i + b) * P, P), :].rearrange(
                        "p (j d) -> p j d", j=J)).then_inc(loaded[b], 16)

                pipeline(sp, EDGE_GROUPS, [(0, load), (4, zero_along(sp, s, g, 2))])

            @block.gpsimd
            def _(pool):
                pool_edges(pool, s, g, 1, used=(add_ready,))

            @block.vector
            def _(dve):
                elu_chain = Chain(elu_steps, 2)
                norm_chain, row_chain = Chain(norm_steps, 2 + NORM_STEPS), Chain(row_steps, ROW_STEPS)
                dve.memset(featT[:, :], 1.0).then_inc(ones_set, 1)

                def stage_features(i, b):
                    grp = RING * i + b
                    if beyond(i, b, 1):
                        dve.wait_ge(f_turned, grp)
                    dve.tensor_scalar(feat[:, :], g.ef[:, bass.ds(grp * (J * 16), J * 16)], 0.0, None,
                                      ALU.add).then_inc(feat_ready, 1)

                def elu(i, b):
                    grp = RING * i + b
                    arrived(dve, s, i, b)
                    elu_chain.begin()
                    if beyond(i, b, 1):
                        dve.wait_ge(exp_ready, grp)
                        dve.wait_ge(norm_steps, norm_chain.steps * grp)
                    elu_argument(dve, grp, elu_chain, s.rows[0][:, b, :, :], el, arg_ready)
                    elu_chain.end()

                find_rows = first_rows_in_steps(dve, s, g, across, r, row_chain)
                compare = select_in_steps(dve, s, across)

                def moment(i, b):
                    grp = RING * i + b
                    x = x_rows[:, b, :, :]
                    dve.wait_ge(exp_ready, grp + 1)
                    dve.wait_ge(loaded[b], 16 * (i + 1))
                    norm_chain.before(dve, i, b)
                    norm_chain.begin()
                    norm_chain.done(dve.scalar_tensor_tensor(out=x, in0=el.pos[:, :, :], scalar=-1.0, in1=x,
                                                             op0=ALU.add, op1=ALU.add))
                    norm_chain.wait(dve, grp)
                    norm_chain.done(dve.tensor_tensor(x, x, exp_arg[:, :, :], ALU.add))
                    norm_chain.wait(dve, grp)
                    norm_factors(dve, i, b, norm_chain, [x[:, j, :] for j in range(J)], w, normed, shift_ready,
                                 chained(find_rows(i, b), compare(i, b)))
                    norm_chain.end()

                def add(i, b):
                    grp = RING * i + b
                    dve.wait_ge(normed, grp + 1)
                    dve.wait_ge(f_mapped, grp + 1)
                    if beyond(i, b, 1):
                        dve.wait_ge(msg_ready, grp)
                    dve.tensor_tensor(added[:, :, :], x_rows[:, b, :, :],
                                      mapped[:, b % 2, :].rearrange("p (j c) -> p j c", j=J),
                                      ALU.add).then_inc(add_ready, 1)

                pipeline(dve, EDGE_GROUPS, [
                    (0, stage_index(dve, s)), (3, stage_features), (3, stage_key(dve, s, g.dst)), (4, add),
                    (3, moment), (2, elu)])

            @block.tensor
            def _(pe):
                def turn_features(i, b):
                    grp = RING * i + b
                    pe.wait_ge(feat_ready, grp + 1)
                    if beyond(i, b, 1):
                        pe.wait_ge(f_copied, grp)
                    for j in range(J):
                        ins = pe.transpose(turned[0:16, 0, j * P:(j + 1) * P], feat[:, j * 16:(j + 1) * 16],
                                           g.ident[:, :])
                    ins.then_inc(f_turned, 1)

                def map_features(i, b):
                    grp = RING * i + b
                    pe.wait_ge(f_copied, grp + 1)
                    if beyond(i, b, 2):
                        pe.wait_ge(add_ready, grp - 1)
                    for j in range(J):
                        ins = pe.matmul(mapped[:, b % 2, j * P:(j + 1) * P], featT[:, j * P:(j + 1) * P], g.WE[:, :],
                                        start=True, stop=True)
                    ins.then_inc(f_mapped, 1)

                def sum_up(i, b):
                    grp = RING * i + b
                    pe.wait_ge(msg_ready, grp + 1)
                    pe.wait_ge(s.equal_ready, grp + 1)
                    if beyond(i, b, 1):
                        pe.wait_ge(s.total_ready, grp)
                    for j in range(J):
                        ins = pe.matmul(tot[:, 0, j * P:(j + 1) * P], s.equal[:, b % 2, j, :], msg[:, b % 2, j, :],
                                        start=True, stop=True)
                    ins.then_inc(s.summed, 1)

                pipeline(pe, EDGE_GROUPS, [(3, turn_features), (3, key_rows(pe, s, g, across)), (3, map_features),
                                           (4, sum_up)])

            @block.scalar
            def _(act):
                act.preload_act_table_set("exp_and_others")
                act.wait_ge(ones_set, 1)

                def copy_features(i, b):
                    grp = RING * i + b
                    act.wait_ge(f_turned, grp + 1)
                    if beyond(i, b, 1):
                        act.wait_ge(f_mapped, grp)
                    act.activation(featT[0:16, :], turned[0:16, 0, :], ACT.Copy).then_inc(f_copied, 1)

                def exps(i, b):
                    act.wait_ge(arg_ready, RING * i + b + 1)
                    for j in range(J):
                        act.activation(el.pos[:, j, :], s.rows[0][:, b, j, 0:D], ACT.Relu, scale=el.inv[:, j:j + 1])
                    act.activation(exp_arg[:, :, :], exp_arg[:, :, :], ACT.Exp).then_inc(exp_ready, 1)

                def norm(i, b):
                    act.wait_ge(shift_ready, RING * i + b + 1)
                    norm_relu(act, [x_rows[:, b, j, :] for j in range(J)], w).then_inc(normed, 1)

                def relu(i, b):
                    grp = RING * i + b
                    act.wait_ge(add_ready, grp + 1)
                    if beyond(i, b, 2):
                        act.wait_ge(s.summed, grp - 1)
                    act.activation(msg[:, b % 2, :, :], added[:, :, :], ACT.Relu).then_inc(msg_ready, 1)

                def view(total):
                    return total, tot[:, 0, :].rearrange("p (j c) -> p j c", j=J)

                pipeline(act, EDGE_GROUPS, [(3, copy_features), (4, relu), (4, save_total(act, s, view)), (3, norm),
                                            (2, exps)])


def edges2(nc, g):
    with ExitStack() as ctx:
        s = edge_space(nc, ctx, "edges2", [(g.X[2], g.src), (g.X[2], g.dst)], 2 * D)
        sb, sem = s.sb, s.sem
        w = norm_space(sb, 2 * J)
        hT = [sb("hT_src", [P, GROUP]), sb("hT_dst", [P, GROUP])]
        across = sb("keys_across", [P, RING, GROUP])
        ewr = sb("weights_across", [P, RING, GROUP])
        spread_out = [sem(f"spread{b}") for b in range(RING)]
        m1 = sb("m1", [P, 2, GROUP])
        s1 = sb("s1", [P, 2, GROUP])
        m2 = sb("m2", [P, 2, GROUP])
        msg = sb("msg", [P, J, 2 * D])
        turned, first, second, tail = s.ps("p_turned", 2), s.ps("p_first", 2), s.ps("p_second", 2), s.ps("p_tail", 2)
        names = ("shift_ready", "h_normed", "h_turned", "h_copied", 
                 "first_map", "first_added", "first_silu", "second_map", "second_silu", "third_map", "messages_even",
                 "messages_odd", "norm_steps")
        (shift_ready, normed, h_turned, h_copied, map1, added1, silu1, map2, silu2,
         map3, msg_even, msg_odd, norm_steps) = (sem(n) for n in names)

        with nc.Block() as block:
            @block.sync
            def _(sp):
                def load(i, b):
                    grp = RING * i + b
                    if beyond(i, b, RING):
                        sp.wait_ge(s.total_ready, RING * (i - 1) + b + 1)
                    for to, of in ((across, g.key_rows), (ewr, g.ew_rows)):
                        sp.dma_start(to[:, b, :], of[bass.ds(grp * J, J), :].rearrange("(o j) e -> o (j e)", o=1)
                                     .partition_broadcast(P)).then_inc(spread_out[b], 16)

                sp.wait_ge(g.tiles_stored, 64)
                pipeline(sp, EDGE_GROUPS, [(0, load), (4, zero_along(sp, s, g, 3))])

            @block.gpsimd
            def _(pool):
                pool_edges(pool, s, g, 2, used=(h_turned,))

            @block.vector
            def _(dve):
                norm_chain = Chain(norm_steps, NORM_STEPS)

                def compare(i, b):
                    grp = RING * i + b
                    dve.wait_ge(s.key_ready, grp + 1)
                    dve.wait_ge(spread_out[b], 32 * (i + 1))
                    if beyond(i, b, 2):
                        dve.wait_ge(s.summed, grp - 1)
                    for j in range(J):
                        ins = dve.tensor_scalar(s.equal[:, b % 2, j, :], across[:, b, j * P:(j + 1) * P],
                                                s.key[:, b % 2, j:j + 1], None, ALU.is_equal)
                    ins.then_inc(s.equal_ready, 1)

                def moment(i, b):
                    arrived(dve, s, i, b)
                    norm_chain.before(dve, i, b)
                    norm_chain.begin()
                    norm_factors(dve, i, b, norm_chain, [s.rows[k][:, b, j, :] for k in range(2) for j in range(J)],
                                 w, normed, shift_ready)
                    norm_chain.end()

                def add_weight(i, b):
                    grp = RING * i + b
                    dve.wait_ge(spread_out[b], 32 * (i + 1))
                    if beyond(i, b, 1):
                        dve.wait_ge(silu1, 2 * grp)
                    for f in range(2):
                        dve.wait_ge(map1, 2 * grp + f + 1)
                        dve.scalar_tensor_tensor(out=m1[:, f, :], in0=ewr[:, b, :], scalar=g.eW1w[:, f:f + 1],
                                                 in1=first[:, f, :], op0=ALU.mult, op1=ALU.add).then_inc(added1, 1)

                def message(i, b):
                    grp = RING * i + b
                    dve.wait_ge(map3, 2 * grp + 1)
                    if beyond(i, b, 1):
                        dve.wait_ge(s.summed, grp)
                    dve.tensor_copy(msg[:, 0:2, :].rearrange("p q c -> p (q c)"), tail[:, 0, :]).then_inc(msg_even, 1)

                pipeline(dve, EDGE_GROUPS, [
                    (0, stage_index(dve, s)), (3, stage_key(dve, s, g.src, turned=False)), (2, moment),
                    (3, known_rows(dve, s, g)), (3, compare), (3, add_weight), (4, message)])

            @block.tensor
            def _(pe):
                def turn(i, b):
                    grp = RING * i + b
                    pe.wait_ge(normed, grp + 1)
                    if beyond(i, b, 1):
                        pe.wait_ge(h_copied, grp)
                    for k in range(2):
                        for j in range(J):
                            ins = pe.transpose(turned[:, k, j * P:(j + 1) * P], s.rows[k][:, b, j, :], g.ident[:, :])
                    ins.then_inc(h_turned, 1)

                def first_map(i, b):
                    grp = RING * i + b
                    pe.wait_ge(h_copied, grp + 1)
                    if beyond(i, b, 1):
                        pe.wait_ge(added1, 2 * grp)
                    for f in range(2):
                        pe.matmul(first[:, f, :], g.eW1s[:, f * P:(f + 1) * P], hT[0][:, :], start=True, stop=False)
                        pe.matmul(first[:, f, :], g.eW1d[:, f * P:(f + 1) * P], hT[1][:, :], start=False,
                                  stop=True).then_inc(map1, 1)

                def second_map(i, b):
                    grp = RING * i + b
                    pe.wait_ge(silu1, 2 * grp + 2)
                    if beyond(i, b, 1):
                        pe.wait_ge(silu2, 2 * grp)
                    for f in range(2):
                        for k in range(2):
                            ins = pe.matmul(second[:, f, :], g.eW2[:, k, f * P:(f + 1) * P], s1[:, k, :],
                                            start=(k == 0), stop=(k == 1))
                        ins.then_inc(map2, 1)

                def third_map(i, b):
                    grp = RING * i + b
                    pe.wait_ge(silu2, 2 * grp + 2)
                    if beyond(i, b, 1):
                        pe.wait_ge(s.total_ready, grp)
                    for j in range(J):
                        for k in range(2):
                            ins = pe.matmul(tail[:, j // 2, (j % 2) * 256:(j % 2 + 1) * 256],
                                            m2[:, k, j * P:(j + 1) * P], g.nW1b[:, k, :],
                                            start=(k == 0), stop=(k == 1))
                        if j % 2:
                            ins.then_inc(map3, 1)

                def sum_up(i, b):
                    grp = RING * i + b
                    pe.wait_ge(s.equal_ready, grp + 1)
                    for j in range(J):
                        if j % 2 == 0:
                            pe.wait_ge(msg_odd if j else msg_even, grp + 1)
                        ins = pe.matmul(tail[:, j // 2, (j % 2) * 256:(j % 2 + 1) * 256], s.equal[:, b % 2, j, :],
                                        msg[:, j, :], start=True, stop=True)
                    ins.then_inc(s.summed, 1)

                pipeline(pe, EDGE_GROUPS, [
                    (3, turn), (4, second_map), (3, first_map), (4, third_map), (4, sum_up)])

            @block.scalar
            def _(act):
                act.preload_act_table_set("silu_and_others")

                def copy(i, b):
                    grp = RING * i + b
                    act.wait_ge(h_turned, grp + 1)
                    if beyond(i, b, 1):
                        act.wait_ge(map1, 2 * grp)
                    act.activation(hT[0][:, :], turned[:, 0, :], ACT.Copy)
                    act.activation(hT[1][:, :], turned[:, 1, :], ACT.Copy).then_inc(h_copied, 1)

                def norm(i, b):
                    act.wait_ge(shift_ready, RING * i + b + 1)
                    norm_relu(act, [s.rows[k][:, b, j, :] for k in range(2) for j in range(J)], w
                              ).then_inc(normed, 1)

                def first_silu(i, b):
                    grp = RING * i + b
                    if beyond(i, b, 1):
                        act.wait_ge(map2, 2 * grp)
                    for f in range(2):
                        act.wait_ge(added1, 2 * grp + f + 1)
                        act.activation(s1[:, f, :], m1[:, f, :], ACT.Silu, bias=g.eb1[:, f:f + 1]).then_inc(silu1, 1)

                def second_silu(i, b):
                    grp = RING * i + b
                    if beyond(i, b, 1):
                        act.wait_ge(map3, 2 * grp)
                    for f in range(2):
                        act.wait_ge(map2, 2 * grp + f + 1)
                        act.activation(m2[:, f, :], second[:, f, :], ACT.Silu, bias=g.eb2[:, f:f + 1]
                                       ).then_inc(silu2, 1)

                def message(i, b):
                    grp = RING * i + b
                    act.wait_ge(map3, 2 * grp + 2)
                    if beyond(i, b, 1):
                        act.wait_ge(s.summed, grp)
                    act.activation(msg[:, 2:4, :].rearrange("p q c -> p (q c)"), tail[:, 1, :], ACT.Copy
                                   ).then_inc(msg_odd, 1)

                def view(total):
                    return total.rearrange("p (h q) c -> p h (q c)", h=2), tail[:, :, :]

                pipeline(act, EDGE_GROUPS, [
                    (3, copy), (4, second_silu), (2, norm), (3, first_silu), (4, message),
                    (4, save_total(act, s, view))])


def edges3(nc, g):
    with ExitStack() as ctx:
        s = edge_space(nc, ctx, "edges3", [(g.X[3], g.src), (g.X[3], g.dst)], D + 1)
        sb, sem = s.sb, s.sem
        S = 2 * J
        w = norm_space(sb, S)
        hT = [sb("hT_src", [P, GROUP]), sb("hT_dst", [P, GROUP])]
        sig = sb("sig", [P, S, 16])
        square = sb("square", [P, S, 16])
        cross = sb("cross", [P, J, 16])
        norm2 = sb("norm2", [P, S])
        inv = sb("inv_norm", [P, S])
        tmp = sb("tmp_norm", [P, S])
        dot = sb("dot", [P, J])
        cosine = sb("cosine", [P, J])
        e = sb("e", [P, J])
        mT = sb("msgT", [P, GROUP])
        msg = sb("msg", [P, 2, J, D + 1])
        across, sigs, mid = s.ps("p_across", 1), s.ps("p_sig", 1), s.ps("p_mid", 1)
        turned, tail = s.ps("p_turned", 2), s.ps("p_tail", 2)
        names = ("ones_set", "shift_ready", "h_normed", "h_turned", "h_copied", "sig_ready", "msg_map", "msg_relu",
                 "agg_map", "messages_ready", "dot_ready", "exp_ready", "norm_steps", "sig_steps", "dot_steps",
                 "root_steps", "factor_steps")
        (ones_set, shift_ready, normed, h_turned, h_copied, sig_ready, map1, relu1, map2, msg_ready, dot_ready,
         exp_ready, norm_steps, sig_steps, dot_steps, root_steps, factor_steps) = (sem(n) for n in names)

        with nc.Block() as block:
            @block.gpsimd
            def _(pool):
                pool_edges(pool, s, g, 3, used=(h_turned,))

            @block.vector
            def _(dve):
                norm_chain, factor_chain = Chain(norm_steps, 2), Chain(factor_steps, NORM_STEPS - 2)
                sig_chain, root_chain, dot_chain = Chain(sig_steps, 4), Chain(root_steps, RSQRT_STEPS), \
                    Chain(dot_steps, 1)
                dve.memset(msg[:, :, :, D:D + 1], 1.0).then_inc(ones_set, 1)

                def roots(i, b):
                    grp = RING * i + b
                    root_chain.before(dve, i, b)
                    root_chain.begin()
                    dve.wait_ge(sig_steps, (grp + 1) * sig_chain.steps)
                    if beyond(i, b, 1):
                        dve.wait_ge(dot_ready, grp)
                    yield from rsqrt_in_steps(dve, grp, root_chain, norm2[:, :], inv[:, :], tmp[:, :])
                    root_chain.end()

                def moment(i, b):
                    arrived(dve, s, i, b)
                    norm_chain.before(dve, i, b)
                    norm_chain.begin()
                    between = roots(*two_before(i, b)) if beyond(i, b, 2) else iter(())
                    moments(dve, RING * i + b, norm_chain, [s.rows[k][:, b, j, :] for k in range(2)
                                                            for j in range(J)], w.stats, w.mv, w.spot, between)
                    for _ in between:
                        pass
                    norm_chain.end()

                def roots_alone(i, b):
                    if isinstance(i, int) and RING * i + b >= EDGE_GROUPS - 2:
                        for _ in roots(i, b):
                            pass

                def factors(i, b):
                    factor_chain.before(dve, i, b)
                    factor_chain.begin()
                    roots_of_variances(dve, i, b, factor_chain, S, w, normed, shift_ready)
                    factor_chain.end()

                def signatures(i, b):
                    grp = RING * i + b
                    dve.wait_ge(sig_ready, grp + 1)
                    sig_chain.before(dve, i, b)
                    if beyond(i, b, 1):
                        dve.wait_ge(dot_ready, grp)
                    sig_chain.begin()
                    sig_chain.done(dve.tensor_tensor(sig[:, :, :], sigs[:, 0, 0:S * 16].rearrange(
                        "p (k c) -> p k c", c=16), g.bsig[:, :, :], ALU.add))
                    sig_chain.wait(dve, grp)
                    dve.tensor_tensor(square[:, :, :], sig[:, :, :], sig[:, :, :], ALU.mult)
                    sig_chain.done(dve.tensor_tensor(cross[:, :, :], sig[:, 0:J, :], sig[:, J:S, :], ALU.mult))
                    sig_chain.wait(dve, grp)
                    dve.tensor_reduce(norm2[:, :], square[:, :, :], AXX, ALU.add)
                    sig_chain.done(dve.tensor_reduce(dot[:, :], cross[:, :, :], AXX, ALU.add))
                    sig_chain.wait(dve, grp)
                    sig_chain.done(dve.tensor_scalar(norm2[:, :], norm2[:, :], 1e-24, None, ALU.max))
                    sig_chain.end()

                def cosines(i, b):
                    grp = RING * i + b
                    dot_chain.before(dve, i, b)
                    dve.wait_ge(root_steps, (grp + 1) * root_chain.steps)
                    if beyond(i, b, 1):
                        dve.wait_ge(exp_ready, grp)
                    dot_chain.begin()
                    dot_chain.done(dve.tensor_tensor(cosine[:, :], dot[:, :], inv[:, 0:J], ALU.mult))
                    dot_chain.wait(dve, grp)
                    dot_chain.end()
                    dve.tensor_tensor(cosine[:, :], cosine[:, :], inv[:, J:S], ALU.mult).then_inc(dot_ready, 1)

                pipeline(dve, EDGE_GROUPS, [
                    (0, stage_index(dve, s)), (4, stage_key(dve, s, g.src)), (2, moment),
                    (4, roots_alone), (4, cosines), (4, known_rows(dve, s, g)), (2, factors),
                    (4, select(dve, s, across, e, exp_ready)), (3, signatures)])

            @block.tensor
            def _(pe):
                def turn(i, b):
                    grp = RING * i + b
                    pe.wait_ge(normed, grp + 1)
                    if beyond(i, b, 1):
                        pe.wait_ge(h_copied, grp)
                    for k in range(2):
                        for j in range(J):
                            ins = pe.transpose(turned[:, k, j * P:(j + 1) * P], s.rows[k][:, b, j, :], g.ident[:, :])
                    ins.then_inc(h_turned, 1)

                def first_maps(i, b):
                    grp = RING * i + b
                    pe.wait_ge(h_copied, grp + 1)
                    if beyond(i, b, 1):
                        pe.wait_ge(sig_steps, 4 * grp)
                        pe.wait_ge(relu1, grp)
                    for k in range(2):
                        for j in range(J):
                            at = (k * J + j) * 16
                            ins = pe.matmul(sigs[:, 0, at:at + 16], hT[k][:, j * P:(j + 1) * P], g.Wsig[:, :],
                                            start=True, stop=True)
                    ins.then_inc(sig_ready, 1)
                    pe.matmul(mid[:, 0, :], g.Wmsg[:, :], hT[1][:, :], start=True, stop=True).then_inc(map1, 1)

                def second_map(i, b):
                    grp = RING * i + b
                    pe.wait_ge(relu1, grp + 1)
                    if beyond(i, b, 1):
                        pe.wait_ge(s.total_ready, grp)
                    for j in range(J):
                        at = (j % 2) * (D + 1)
                        ins = pe.matmul(tail[:, j // 2, at:at + D], mT[:, j * P:(j + 1) * P], g.Wbot[:, :],
                                        start=True, stop=True)
                    ins.then_inc(map2, 1)

                def sum_up(i, b):
                    grp = RING * i + b
                    pe.wait_ge(s.equal_ready, grp + 1)
                    pe.wait_ge(msg_ready, grp + 1)
                    for j in range(J):
                        ins = pe.matmul(width129(tail, j), s.equal[:, b % 2, j, :], msg[:, b % 2, j, :], start=True,
                                        stop=True)
                    ins.then_inc(s.summed, 1)

                pipeline(pe, EDGE_GROUPS, [(3, turn), (4, key_rows(pe, s, g, across)), (3, first_maps), (4, sum_up),
                                           (3, second_map)])

            @block.scalar
            def _(act):
                act.preload_act_table_set("exp_and_others")
                act.wait_ge(ones_set, 1)

                def copy(i, b):
                    grp = RING * i + b
                    act.wait_ge(h_turned, grp + 1)
                    if beyond(i, b, 1):
                        act.wait_ge(map1, grp)
                    act.activation(hT[0][:, :], turned[:, 0, :], ACT.Copy)
                    act.activation(hT[1][:, :], turned[:, 1, :], ACT.Copy).then_inc(h_copied, 1)

                def relu(i, b):
                    grp = RING * i + b
                    act.wait_ge(map1, grp + 1)
                    if beyond(i, b, 1):
                        act.wait_ge(map2, grp)
                    act.activation(mT[:, :], mid[:, 0, :], ACT.Relu, bias=g.bmsg[:, 0:1]).then_inc(relu1, 1)

                def message(i, b):
                    grp = RING * i + b
                    act.wait_ge(map2, grp + 1)
                    if beyond(i, b, 2):
                        act.wait_ge(s.summed, grp - 1)
                    act.activation(msg[:, b % 2, :, 0:D].rearrange("p (h q) c -> p h q c", h=2), halves(tail, 0, D),
                                   ACT.Copy).then_inc(msg_ready, 1)

                def exps(i, b):
                    grp = RING * i + b
                    act.wait_ge(dot_ready, grp + 1)
                    if beyond(i, b, 1):
                        act.wait_ge(s.equal_ready, grp)
                    act.activation(e[:, :], cosine[:, :], ACT.Exp).then_inc(exp_ready, 1)

                def norm(i, b):
                    act.wait_ge(shift_ready, RING * i + b + 1)
                    norm_relu(act, [s.rows[k][:, b, j, :] for k in range(2) for j in range(J)], w
                              ).then_inc(normed, 1)

                def view(total):
                    return total.rearrange("p (h q) c -> p h q c", h=2), halves(tail, 0, D + 1)

                pipeline(act, EDGE_GROUPS, [(3, copy), (4, exps), (3, relu), (2, norm), (4, save_total(act, s, view)),
                                            (3, message)])


def nodes(nc, g, layer, out):
    with ExitStack() as ctx:
        sb, sem, ps = makers(nc, ctx, f"nodes{layer}")
        reads = {1: [g.X[0], g.T[0], g.T[1]], 2: [g.X[2], g.T[2]], 3: [g.X[3], g.T[3]]}[layer]
        to = {1: g.X[2], 2: g.X[3], 3: out}[layer]
        const = {1: g.c2, 2: g.nb2, 3: g.decb}[layer]
        slots = [sb(f"slots{k}", [P, RING, J, t.shape[1]]) for k, t in enumerate(reads)]
        stats = sb("stats", [P, J, 6])
        mv = sb("mv", [P, J, 2])
        spot = sb("spot", [P, 1])[0:1, 0:1]
        var = sb("var", [P, J])
        rstd = sb("rstd", [P, 2, J])
        shift = sb("shift", [P, 2, J])
        eps = sb("eps", [P, J])
        half = sb("half", [P, J])
        base = sb("base", [P, RING, J, D])
        h = sb("h", [P, 2, J, D])
        hT = sb("hT", [P, 2, GROUP])
        mid = sb("mid", [P, 2, 2, GROUP])
        pre = sb("pre", [P, 2, J, 2 * D if layer == 2 else D])
        done = sb("done", [P, RING, J, D])
        inv = sb("inv_weight", [P, J])
        if layer == 1:
            el = elu_space(sb)
            exp_arg = el.exp_arg
        p_turned, p_map, p_mid, p_out = ps("p_turned", 1), ps("p_map", 2), ps("p_mid", 2), ps("p_out", 2)
        (consts, var_ready, rstd_ready, base_ready, shift_ready, normed, mixed, h_turned, h_copied, mapped,
         pre_ready, mid_turned, mid_ready, projected, out_ready, arg_ready, exp_ready, pos_ready, pos_added,
         elu_steps, stat_steps, pre_steps) = (
            sem(n) for n in (
                "consts_set", "var_ready", "rstd_ready", "base_ready", "shift_ready", "normed", "mixed", "h_turned",
                "h_copied", "mapped", "pre_ready", "mid_turned", "mid_ready", "projected", "out_ready",
                "exp_arg_ready", "exp_ready", "pos_ready", "pos_added", "elu_steps", "stat_steps", "pre_steps"))
        loaded = [sem(f"loaded{b}") for b in range(RING)]
        stored = [sem(f"stored{b}") for b in range(RING)]
        h_made = mixed if layer == 1 else normed
        STATS = 3 if layer == 1 else 2
        chunks = 1 if layer == 3 else 2

        with nc.Block() as block:
            @block.sync
            def _(sp):
                def rows(t, i, b, parts=P):
                    return t[bass.ds((RING * i + b) * GROUP, parts * J), :].rearrange("(p j) d -> p j d", j=J)

                def load(i, b):
                    last = isinstance(i, int) and RING * i + b == NODE_GROUPS - 1
                    for t, slot in zip(reads, slots):
                        n = LAST_P if last and t.shape[0] == N else P
                        sp.dma_start(slot[0:n, b, :, :], rows(t, i, b, n)).then_inc(loaded[b], 16)

                def reload(i, b):
                    grp = RING * i + b
                    if isinstance(i, int) and grp + RING >= NODE_GROUPS:
                        return
                    sp.wait_ge(normed, grp + 1)
                    sp.wait_ge(base_ready, grp + 1)
                    sp.wait_ge(mixed if layer == 1 else pre_ready, grp + 1)
                    load(i + 1, b)

                def store(i, b):
                    last = isinstance(i, int) and RING * i + b == NODE_GROUPS - 1
                    n = LAST_P if last and layer == 3 else P
                    sp.wait_ge(out_ready, RING * i + b + 1)
                    sp.dma_start(rows(to, i, b, n), done[0:n, b, :, :]).then_inc(stored[b], 16)

                for b in range(RING):
                    load(0, b)
                pipeline(sp, NODE_GROUPS, [(3, reload), (4, store)])
                for b in range(RING):
                    sp.wait_ge(stored[b], 16 * len(range(b, NODE_GROUPS, RING)))

            @block.gpsimd
            def _(pool):
                pool.memset(eps[:, :], LN_EPS)
                pool.memset(half[:, :], -0.5).then_inc(consts, 1)
                pool.wait_ge(consts, 1)

                def roots(i, b):
                    grp = RING * i + b
                    pool.wait_ge(stat_steps, grp * STATS + STATS)
                    pool.tensor_tensor(var[:, :], mv[:, :, 1], eps[:, :], ALU.add).then_inc(var_ready, 1)
                    pool.wait_ge(var_ready, grp + 1)
                    if beyond(i, b, 2):
                        pool.wait_ge(normed, grp - 1)
                    pool.tensor_tensor(rstd[:, b % 2, :], var[:, :], half[:, :], ALU.pow).then_inc(rstd_ready, 1)

                def add_bias(i, b):
                    grp = RING * i + b
                    if beyond(i, b, RING):
                        pool.wait_ge(out_ready, RING * (i - 1) + b + 1)
                    pool.tensor_tensor(base[:, b, :, :], slots[0][:, b, :, :], const[:, :, :],
                                       ALU.add).then_inc(base_ready, 1)

                def add_pos(i, b):
                    pool.wait_ge(pos_ready, RING * i + b + 1)
                    x = slots[0][:, b, :, :]
                    pool.tensor_tensor(x, x, el.pos[:, :, :], ALU.add).then_inc(pos_added, 1)

                if layer == 1:
                    stages = [(1, roots), (0, add_pos), (1, add_bias)]
                else:
                    stages = [(0, roots), (0, add_bias)]
                pipeline(pool, NODE_GROUPS, stages)

            @block.vector
            def _(dve):
                elu_chain = Chain(elu_steps, 2)
                stat_chain = Chain(stat_steps, STATS)
                pre_chain = Chain(pre_steps, 2)

                def inverse(i, b):
                    grp = RING * i + b
                    chain = elu_chain if layer == 1 else pre_chain
                    chain.begin()
                    dve.wait_ge(loaded[b], 16 * len(reads) * (i + 1))
                    guard, at = (el.guard, el.inv) if layer == 1 else (inv, inv)
                    dve.wait_ge(pos_ready if layer == 1 else pre_ready, grp)
                    chain.done(dve.tensor_scalar(guard[:, :], slots[1][:, b, :, D], 1e-37, None, ALU.max))
                    yield
                    chain.wait(dve, grp)
                    chain.done(dve.reciprocal(at[:, :], guard[:, :]))
                    yield
                    chain.end()

                def inverse_alone(i, b):
                    if isinstance(i, int) and (RING * i + b == 0 if layer == 1 else
                                               RING * i + b >= NODE_GROUPS - 2):
                        for _ in inverse(i, b):
                            pass

                def elu(i, b):
                    grp = RING * i + b
                    dve.wait_ge(elu_steps, (grp + 1) * 2)
                    dve.wait_ge(stat_steps, grp * STATS)
                    dve.wait_ge(pos_added, grp)
                    sums = slots[1][:, b, :, :]
                    for j in range(J):
                        ins = dve.tensor_scalar(el.pos[:, j, :], sums[:, j, 0:D], el.inv[:, j:j + 1], 0.0, ALU.mult,
                                                ALU.max)
                    ins.then_inc(pos_ready, 1)
                    for j in range(J):
                        ins = dve.tensor_scalar(exp_arg[:, j, :], sums[:, j, 0:D], el.inv[:, j:j + 1], 0.0,
                                                ALU.mult, ALU.min)
                    ins.then_inc(arg_ready, 1)

                def moment(i, b):
                    grp = RING * i + b
                    x = slots[0][:, b, :, :]
                    stat_chain.begin()
                    if layer == 1:
                        dve.wait_ge(exp_ready, grp + 1)
                        dve.wait_ge(pos_added, grp + 1)
                        stat_chain.done(dve.scalar_tensor_tensor(out=x, in0=exp_arg[:, :, :], scalar=-1.0, in1=x,
                                                                 op0=ALU.add, op1=ALU.add))
                        stat_chain.wait(dve, grp)
                    else:
                        dve.wait_ge(loaded[b], 16 * len(reads) * (i + 1))
                    dve.wait_ge(var_ready, grp)
                    dve.wait_ge(shift_ready, grp)
                    between = iter(())
                    if layer == 1 and not (isinstance(i, int) and grp == NODE_GROUPS - 1):
                        between = inverse(*one_behind(i, b))
                    if layer == 3 and beyond(i, b, 2):
                        between = inverse(*two_before(i, b))
                    moments(dve, grp, stat_chain, [x[:, j, :] for j in range(J)], stats, mv, spot, between)
                    stat_chain.end()

                def make_shift(i, b):
                    grp = RING * i + b
                    dve.wait_ge(rstd_ready, grp + 1)
                    dve.scalar_tensor_tensor(out=shift[:, b % 2, :], in0=mv[:, :, 0], scalar=-1.0,
                                             in1=rstd[:, b % 2, :], op0=ALU.mult, op1=ALU.mult
                                             ).then_inc(shift_ready, 1)

                def mix(i, b):
                    dve.wait_ge(normed, RING * i + b + 1)
                    dve.scalar_tensor_tensor(out=h[:, b % 2, :, :], in0=h[:, b % 2, :, :], scalar=g.eps1[:, 0:1],
                                             in1=slots[2][:, b, :, :], op0=ALU.mult, op1=ALU.add
                                             ).then_inc(mixed, 1)

                def add_sums(i, b):
                    grp = RING * i + b
                    if layer == 2:
                        dve.wait_ge(mapped, grp + 1)
                        dve.tensor_tensor(pre[:, b % 2, :, :].rearrange("p (q j) c -> p q (j c)", q=2),
                                          p_map[:, :, :], slots[1][:, b, :, :].rearrange("p (q j) c -> p q (j c)", q=2),
                                          ALU.add).then_inc(pre_ready, 1)
                    else:
                        dve.wait_ge(pre_steps, (grp + 1) * 2)
                        dve.wait_ge(mapped, grp + 1)
                        for j in range(J):
                            ins = dve.scalar_tensor_tensor(out=pre[:, b % 2, j, :], in0=slots[1][:, b, j, 0:D],
                                                           scalar=inv[:, j:j + 1],
                                                           in1=p_map[:, b % 2, j * P:(j + 1) * P], op0=ALU.mult,
                                                           op1=ALU.add)
                        ins.then_inc(pre_ready, 1)

                def finish(i, b):
                    grp = RING * i + b
                    dve.wait_ge(stored[b], 16 * i)
                    dve.wait_ge(base_ready, grp + 1)
                    dve.wait_ge(projected, grp + 1)
                    dve.tensor_tensor(done[:, b, :, :], p_out[:, b % 2, :].rearrange("p (j c) -> p j c", j=J),
                                      base[:, b, :, :], ALU.add).then_inc(out_ready, 1)

                if layer == 1:
                    stages = [(1, moment), (2, mix), (0, inverse_alone), (0, elu), (1, make_shift), (4, finish)]
                else:
                    stages = [(0, moment), (4, finish), (0, make_shift), (2, add_sums)]
                if layer == 3:
                    stages = [(0, moment), (4, finish), (2, inverse_alone), (2, add_sums), (0, make_shift)]
                pipeline(dve, NODE_GROUPS, stages)

            @block.tensor
            def _(pe):
                def turn(i, b):
                    grp = RING * i + b
                    pe.wait_ge(h_made, grp + 1)
                    pe.wait_ge(h_copied, grp)
                    for j in range(J):
                        ins = pe.transpose(p_turned[:, 0, j * P:(j + 1) * P], h[:, b % 2, j, :], g.ident[:, :])
                    ins.then_inc(h_turned, 1)

                def first_map(i, b):
                    grp = RING * i + b
                    pe.wait_ge(h_copied, grp + 1)
                    if layer == 1:
                        pe.wait_ge(mid_ready, chunks * grp)
                        for f in range(2):
                            ins = pe.matmul(p_map[:, f, :], g.Wm1[:, f * P:(f + 1) * P], hT[:, b % 2, :], start=True,
                                            stop=True)
                    else:
                        pe.wait_ge(pre_ready, grp)
                        for j in range(J):
                            if layer == 2:
                                bank, at, W = j // 2, (j % 2) * 2 * D, g.nW1a
                            else:
                                bank, at, W = b % 2, j * D, g.Wtop
                            n = W.shape[1]
                            ins = pe.matmul(p_map[:, bank, at:at + n], hT[:, b % 2, j * P:(j + 1) * P], W[:, :],
                                            start=True, stop=True)
                    ins.then_inc(mapped, 1)

                def turn_hidden(i, b):
                    grp = RING * i + b
                    pe.wait_ge(pre_ready, grp + 1)
                    pe.wait_ge(mid_ready, chunks * grp)
                    for f in range(chunks):
                        for j in range(J):
                            ins = pe.transpose(p_mid[:, f, j * P:(j + 1) * P], pre[:, b % 2, j, f * P:(f + 1) * P],
                                               g.ident[:, :])
                    ins.then_inc(mid_turned, 1)

                def project(i, b):
                    grp = RING * i + b
                    pe.wait_ge(mid_ready, chunks * (grp + 1))
                    if beyond(i, b, 2):
                        pe.wait_ge(out_ready, grp - 1)
                    for j in range(J):
                        for f in range(chunks):
                            W2 = {1: g.Wm2[:, f, :], 2: g.nW2[:, f, :], 3: g.dec[:, :]}[layer]
                            ins = pe.matmul(p_out[:, b % 2, j * P:(j + 1) * P],
                                            mid[:, b % 2, f, j * P:(j + 1) * P], W2, start=(f == 0),
                                            stop=(f == chunks - 1))
                    ins.then_inc(projected, 1)

                if layer == 1:
                    stages = [(4, project), (3, first_map), (2, turn)]
                else:
                    stages = [(4, project), (3, turn_hidden), (1, turn), (2, first_map)]
                if layer == 3:
                    stages = [(4, project), (2, first_map), (3, turn_hidden), (1, turn)]
                pipeline(pe, NODE_GROUPS, stages)

            @block.scalar
            def _(act):
                act.preload_act_table_set("silu_and_others" if layer == 2 else "exp_and_others")

                def exps(i, b):
                    act.wait_ge(arg_ready, RING * i + b + 1)
                    act.activation(exp_arg[:, :, :], exp_arg[:, :, :], ACT.Exp).then_inc(exp_ready, 1)

                def norm(i, b):
                    grp = RING * i + b
                    act.wait_ge(shift_ready, grp + 1)
                    if beyond(i, b, 2):
                        act.wait_ge(h_turned, grp - 1)
                    for j in range(J):
                        ins = act.activation(h[:, b % 2, j, :], slots[0][:, b, j, :], ACT.Relu,
                                             bias=shift[:, b % 2, j:j + 1], scale=rstd[:, b % 2, j:j + 1])
                    ins.then_inc(normed, 1)

                def copy(i, b):
                    grp = RING * i + b
                    act.wait_ge(h_turned, grp + 1)
                    if beyond(i, b, 2):
                        act.wait_ge(mapped, grp - 1)
                    act.activation(hT[:, b % 2, :], p_turned[:, 0, :], ACT.Copy).then_inc(h_copied, 1)

                def hidden(i, b):
                    grp = RING * i + b
                    act.wait_ge(mapped if layer == 1 else mid_turned, grp + 1)
                    if beyond(i, b, 2):
                        act.wait_ge(projected, grp - 1)
                    for f in range(chunks):
                        if layer == 1:
                            ins = act.activation(mid[:, b % 2, f, :], p_map[:, f, :], ACT.Relu, bias=g.c1[:, f:f + 1],
                                                 scale=g.s1[:, f:f + 1])
                        elif layer == 2:
                            ins = act.activation(mid[:, b % 2, f, :], p_mid[:, f, :], ACT.Silu,
                                                 bias=g.nb1[:, f:f + 1])
                        else:
                            ins = act.activation(mid[:, b % 2, f, :], p_mid[:, f, :], ACT.Relu, bias=g.btop[:, 0:1])
                        ins.then_inc(mid_ready, 1)

                if layer == 1:
                    stages = [(3, hidden), (2, copy), (0, exps), (1, norm)]
                else:
                    stages = [(3, hidden), (1, copy), (0, norm)]
                pipeline(act, NODE_GROUPS, stages)


def kernel(**inputs):
    import concourse.bacc as bacc
    import numpy as np
    from concourse.bass_utils import run_bass_kernel_spmd as run

    nc = bacc.Bacc("TRN2", target_bir_lowering=False, num_devices=1)
    arrays, args = {}, {}
    for name, value in inputs.items():
        value = np.ascontiguousarray(value)
        arrays[f"in_{name}"] = value
        args[name] = nc.dram_tensor(f"in_{name}", value.shape, mybir.dt.from_np(value.dtype),
                                    kind="ExternalInput").ap()
    out = nc.dram_tensor("out_x", (N, D), F32, kind="ExternalOutput").ap()
    build(nc, args, out)
    return run(nc, [arrays], core_ids=[0]).results[0]["out_x"]
```
